# Optimizing a Trainium2 kernel written in Bass

```python
import numpy as np
import jax
import jax.numpy as jnp

def _softmax(x, axis=-1):
    return jax.nn.softmax(x, axis=axis)

def _gelu(x):
    return jax.nn.gelu(x, approximate=True)

def _silu(x):
    return jax.nn.silu(x)

def _sigmoid(x):
    return jax.nn.sigmoid(x)

def _layernorm(x, axis=-1, eps=1e-05):
    m = jnp.mean(x, axis=axis, keepdims=True)
    v = jnp.var(x, axis=axis, keepdims=True)
    return (x - m) / jnp.sqrt(v + eps)

def _scatter_add(tgt, idx, src, axis=0):
    return tgt.at[idx].add(src)

def _segment_sum(src, seg, n):
    return jax.ops.segment_sum(src, seg, n)
kernel_name = 'mk_hybrid_d1_jaxref_r8_485be2'

def setup_inputs(seed: int=0):
    np.random.seed(seed)
    _w = jnp.asarray

    def _L0_attn_a_setup():
        import jax, jax.numpy as jnp
        import numpy as np
        import math
        N_HEADS = 8

        def _head_dirs():
            t = np.array([[(i >> 2 & 1) * 2 - 1, (i >> 1 & 1) * 2 - 1, (i & 1) * 2 - 1] for i in range(8)], dtype=np.float32)
            return jnp.asarray(t / np.sqrt(3.0, dtype=np.float32))
        key = jax.random.key(seed)
        k1, k2, k3, k4 = jax.random.split(key, 4)
        B, T, C = (2, 256, 128)
        x = jax.random.normal(k1, (B, T, C), dtype=jnp.float32)
        w_qkv = jax.random.normal(k2, (C, 3 * C), dtype=jnp.float32) * (1.0 / math.sqrt(C))
        w_out = jax.random.normal(k3, (C, C), dtype=jnp.float32) * (1.0 / math.sqrt(C))
        head_scales = jax.random.normal(k4, (N_HEADS,), dtype=jnp.float32) * 0.1
        return {'x': x, 'w_qkv': w_qkv, 'w_out': w_out, 'head_scales': head_scales}
    _L0_attn_a_in = _L0_attn_a_setup()

    def _L0_attn_b_setup():
        import jax, jax.numpy as jnp
        import numpy as np
        NUM_HEADS = 16
        key = jax.random.key(seed)
        kx, kq, kk, kv = jax.random.split(key, 4)
        N, S, D = (2, 512, 128)
        scale = 1.0 / np.sqrt(D)
        x = jax.random.normal(kx, (N, S, D), dtype=jnp.float32)
        Wq = jax.random.normal(kq, (D, D), dtype=jnp.float32) * scale
        Wk = jax.random.normal(kk, (D, D), dtype=jnp.float32) * scale
        Wv = jax.random.normal(kv, (D, D), dtype=jnp.float32) * scale
        return {'x': x, 'Wq': Wq, 'Wk': Wk, 'Wv': Wv}
    _L0_attn_b_in = _L0_attn_b_setup()

    def _L0_ffn_setup():
        import jax, jax.numpy as jnp
        import numpy as np
        B, S, D, F, E = (2, 256, 128, 512, 8)
        LN_EPS = 1e-05

        def _layer_norm(x, gamma, beta):
            mu = jnp.mean(x, axis=-1, keepdims=True)
            var = jnp.mean(jnp.square(x - mu), axis=-1, keepdims=True)
            return (x - mu) * jax.lax.rsqrt(var + LN_EPS) * gamma + beta
        key = jax.random.key(seed)
        ks = jax.random.split(key, 8)

        def xavier(k, shape):
            fan_in, fan_out = (shape[-1], shape[-2])
            a = jnp.sqrt(6.0 / (fan_in + fan_out))
            return jax.random.uniform(k, shape, jnp.float32, -a, a)
        return {'tgt': jax.random.normal(ks[0], (B, S, D), jnp.float32), 'Wr': xavier(ks[1], (E, D)), 'br': jnp.zeros((E,), jnp.float32), 'W1': xavier(ks[2], (E, F, D)), 'b1': jnp.zeros((E, F), jnp.float32), 'W2': xavier(ks[3], (E, D, F)), 'b2': jnp.zeros((E, D), jnp.float32), 'gamma': jnp.ones((D,), jnp.float32), 'beta': jnp.zeros((D,), jnp.float32)}
    _L0_ffn_in = _L0_ffn_setup()
    _d = {'L0_attn_a_x': _L0_attn_a_in['x'], 'L0_attn_a_w_qkv': _L0_attn_a_in['w_qkv'], 'L0_attn_a_w_out': _L0_attn_a_in['w_out'], 'L0_attn_a_head_scales': _L0_attn_a_in['head_scales'], 'L0_attn_b_Wq': _L0_attn_b_in['Wq'], 'L0_attn_b_Wk': _L0_attn_b_in['Wk'], 'L0_attn_b_Wv': _L0_attn_b_in['Wv'], 'L0_ffn_Wr': _L0_ffn_in['Wr'], 'L0_ffn_br': _L0_ffn_in['br'], 'L0_ffn_W1': _L0_ffn_in['W1'], 'L0_ffn_b1': _L0_ffn_in['b1'], 'L0_ffn_W2': _L0_ffn_in['W2'], 'L0_ffn_b2': _L0_ffn_in['b2'], 'L0_ffn_gamma': _L0_ffn_in['gamma'], 'L0_ffn_beta': _L0_ffn_in['beta']}
    _x0 = _d['L0_attn_a_x']
    _d['L0_attn_a_x'] = jax.random.normal(jax.random.fold_in(jax.random.key(seed), 1), (16, 256, 128), dtype=_x0.dtype)
    del _x0
    return _d

def reference(L0_attn_a_x, L0_attn_a_w_qkv, L0_attn_a_w_out, L0_attn_a_head_scales, L0_attn_b_Wq, L0_attn_b_Wk, L0_attn_b_Wv, L0_ffn_Wr, L0_ffn_br, L0_ffn_W1, L0_ffn_b1, L0_ffn_W2, L0_ffn_b2, L0_ffn_gamma, L0_ffn_beta):

    def _L0_attn_a_ref(x, w_qkv, w_out, head_scales):
        import jax, jax.numpy as jnp
        import numpy as np
        import math
        N_HEADS = 8

        def _head_dirs():
            t = np.array([[(i >> 2 & 1) * 2 - 1, (i >> 1 & 1) * 2 - 1, (i & 1) * 2 - 1] for i in range(8)], dtype=np.float32)
            return jnp.asarray(t / np.sqrt(3.0, dtype=np.float32))
        B, T, C = x.shape
        H = N_HEADS
        hd = C // H
        scale = 1.0 / math.sqrt(hd)
        dirs = _head_dirs()
        qkv = (x @ w_qkv).reshape(B, T, 3, H, hd)
        q = jnp.transpose(qkv[:, :, 0], (0, 2, 1, 3))
        k = jnp.transpose(qkv[:, :, 1], (0, 2, 1, 3))
        v = jnp.transpose(qkv[:, :, 2], (0, 2, 1, 3))
        scores = jnp.einsum('bhqd,bhkd->bhqk', q, k) * scale
        causal = jnp.tril(jnp.ones((T, T), dtype=bool))
        scores = jnp.where(causal[None, None], scores, -jnp.inf)
        q_proj = jnp.einsum('bhtd,hd->bht', q[..., :3], dirs)
        k_proj = jnp.einsum('bhtd,hd->bht', k[..., :3], dirs)
        geo = q_proj[..., :, None] * k_proj[..., None, :]
        scores = scores + head_scales[None, :, None, None] * geo
        attn = jax.nn.softmax(scores, axis=-1)
        out = jnp.einsum('bhqk,bhkd->bqhd', attn, v).reshape(B, T, C)
        return out @ w_out

    def _L0_attn_b_ref(x, Wq, Wk, Wv):
        import jax, jax.numpy as jnp
        import numpy as np
        NUM_HEADS = 16
        N, S, D = x.shape
        H = NUM_HEADS
        hd = D // H
        q = (x @ Wq.T).reshape(N, S, H, hd).transpose(0, 2, 1, 3)
        k = (x @ Wk.T).reshape(N, S, H, hd).transpose(0, 2, 1, 3)
        v = (x @ Wv.T).reshape(N, S, H, hd).transpose(0, 2, 1, 3)
        energy = jnp.einsum('nhqd,nhkd->nhqk', q, k)
        attn = jax.nn.softmax(energy / jnp.sqrt(jnp.float32(hd)), axis=3)
        out = jnp.einsum('nhql,nhld->nhqd', attn, v)
        return out.transpose(0, 2, 1, 3).reshape(N, S, D)

    def _L0_ffn_ref(tgt, Wr, br, W1, b1, W2, b2, gamma, beta):
        import jax, jax.numpy as jnp
        import numpy as np
        B, S, D, F, E = (2, 256, 128, 512, 8)
        LN_EPS = 1e-05

        def _layer_norm(x, gamma, beta):
            mu = jnp.mean(x, axis=-1, keepdims=True)
            var = jnp.mean(jnp.square(x - mu), axis=-1, keepdims=True)
            return (x - mu) * jax.lax.rsqrt(var + LN_EPS) * gamma + beta
        logits = jnp.einsum('bsd,ed->bse', tgt, Wr) + br
        top_v, top_i = jax.lax.top_k(logits, 2)
        top_w = jax.nn.softmax(top_v, axis=-1)
        n_exp = logits.shape[-1]
        router_w = jnp.sum(jax.nn.one_hot(top_i, n_exp, dtype=top_w.dtype) * top_w[..., None], axis=-2)
        h = jnp.einsum('bsd,efd->bsef', tgt, W1) + b1
        h = jax.nn.relu(h)
        o = jnp.einsum('bsef,edf->bsed', h, W2) + b2
        tgt2 = jnp.einsum('bsed,bse->bsd', o, router_w)
        return _layer_norm(tgt + tgt2, gamma, beta)
    x = L0_attn_a_x
    x = x + _L0_attn_a_ref(_layernorm(x, axis=-1), L0_attn_a_w_qkv, L0_attn_a_w_out, L0_attn_a_head_scales)
    x = x + _L0_ffn_ref(_layernorm(x, axis=-1), L0_ffn_Wr, L0_ffn_br, L0_ffn_W1, L0_ffn_b1, L0_ffn_W2, L0_ffn_b2, L0_ffn_gamma, L0_ffn_beta)
    x = x + _L0_attn_b_ref(_layernorm(x, axis=-1), L0_attn_b_Wq, L0_attn_b_Wk, L0_attn_b_Wv)
    x = x + _L0_ffn_ref(_layernorm(x, axis=-1), L0_ffn_Wr, L0_ffn_br, L0_ffn_W1, L0_ffn_b1, L0_ffn_W2, L0_ffn_b2, L0_ffn_gamma, L0_ffn_beta)
    return x

_drawn_inputs = setup_inputs


def setup_inputs(seed=0):
    import zlib

    import numpy as np

    out = dict(_drawn_inputs(seed))
    spreads = {'L0_ffn_br': (0.0, 0.1),
     'L0_ffn_b1': (0.0, 0.1),
     'L0_ffn_b2': (0.0, 0.1),
     'L0_ffn_gamma': (1.0, 0.2),
     'L0_ffn_beta': (0.0, 0.1)}
    factors = {}
    for name, (base, spread) in spreads.items():
        noise = np.random.default_rng([zlib.crc32(name.encode()), seed]).standard_normal(out[name].shape)
        drawn = base * np.exp(spread * noise) if base else spread * noise
        out[name] = jnp.asarray(drawn.astype(out[name].dtype))
    for name, factor in factors.items():
        out[name] = (out[name] * factor).astype(out[name].dtype)
    return out
```

```python
from contextlib import ExitStack

import numpy as np

import concourse.bass as bass
from concourse import mybir

F32 = mybir.dt.float32
BF16 = mybir.dt.bfloat16
I32 = mybir.dt.int32
U32 = mybir.dt.uint32
ACT = mybir.ActivationFunctionType
ALU = mybir.AluOpType
AX = mybir.AxisListType

P = 128
B = 16
T = 256
QC = T // P
NT = B * QC
F = 512
FC = F // P
E = 8
TILE = 256
NJ = (2 * B * T + E * (TILE - 1)) // TILE
SLOTS = 3
WCOLS = F + FC * P + FC + 1
EPS = 1e-5
MASKED = -1.0e30
PIPE = 7
RING = 3
REGION = B * T + TILE
SPARE = NJ - 2 * B * T // TILE
ROW = P + 2
PAIRS = 2 * B * T
COMBINE, NORM, PROJECT, MAXIMA, EXPS, OUTPUT, ROUTE = range(PIPE)
assert NJ % SLOTS == 0 and (B - PIPE) % RING == 0
BANK = [dict(lnT=0, oT=1, tT=0, qk=1, v=0, lg=1, onT=0, mxT=1, rank=0, pr=1),
        dict(lnT=1, oT=0, oT2=1, tT=0, qk=1, v=0, lg=1, rank=0, mxT=1)]

LAYERS = [
    dict(H=8, hd=16, causal=True, width=2, q_parts=[2, 0, 1, 0], k_parts=[1, 0, 2],
         q_runs=[2, 1, 0], k_runs=[0, 0, 1], ones=96, groups=2),
    dict(H=16, hd=8, causal=False, width=3, q_parts=[0, 1, 2, 0, 1], k_parts=[0, 1, 2],
         q_runs=[0, 1, 2], k_runs=[0, 0, 0], ones=64, groups=4),
]
for _l in LAYERS:
    _l["rows"] = 3 * _l["width"] * _l["hd"]
    _l["banks"] = 3 if _l["causal"] else 4


class At:

    def __init__(self, i, a, c):
        self.i, self.a, self.c = i, a, c

    def __add__(self, n):
        return At(self.i, self.a, self.c + n)

    def __sub__(self, n):
        return At(self.i, self.a, self.c - n)

    def __mul__(self, n):
        return At(self.i, self.a * n, self.c * n)

    def __floordiv__(self, n):
        assert self.a % n == 0
        return At(self.i, self.a // n, self.c // n)

    __radd__, __rmul__ = __add__, __mul__


def val(n):
    if not isinstance(n, At):
        return n
    return n.i * n.a + n.c if n.c else n.i * n.a


def ds(n, size):
    return bass.ds(val(n), size)


def score_banks(layer, g):
    heads = [4 * g + j for j in range(4)]
    if layer["causal"]:
        return [("wide", heads[0:2]), ("wide", heads[2:4]), ("narrow", heads)]
    return [(c, heads[2 * i:2 * i + 2]) for c in range(QC) for i in range(2)]


def build(nc, x_in, w_a, w_o, wq_t, w_b, hs_in, wr, br, wall, gamma, beta, consts, counts, id_in, pads, out):
    with ExitStack() as ctx:
        def sb(name, shape, dt=F32):
            return ctx.enter_context(nc.sbuf_tensor(name, shape, dt))

        def pb(name):
            return ctx.enter_context(nc.psum_tensor(name, [P, 512], F32))

        q_scr = [nc.dram_tensor(f"q_scr{i}", (5, P, T), BF16).ap() for i in range(RING)]
        k_scr = [nc.dram_tensor(f"k_scr{i}", (3, P, T), BF16).ap() for i in range(RING)]
        xs = nc.dram_tensor("xs", (E * REGION + SPARE * TILE, ROW), F32).ap()
        ys = nc.dram_tensor("ys", (PAIRS + (E + SPARE) * TILE, P), F32).ap()

        x = sb("x", [P, NT, P])
        t = sb("t", [P, NT, P])
        cst = sb("cst", [P, 5, P])
        cnt = sb("cnt", [P, 2 * E + NJ])
        identb = sb("identb", [P, P], BF16)
        maskm_w = sb("maskm_w", [P, 2, 2, P], BF16)
        maskm_n = sb("maskm_n", [P, 4, P], BF16)
        maske_w = sb("maske_w", [P, 2, 2, P], BF16)
        maske_n = sb("maske_n", [P, 4, P], BF16)
        earlier = sb("earlier", [P, P], BF16)
        onesb = sb("onesb", [P, P], BF16)
        halfm = sb("halfm", [P, QC])
        ids = sb("ids", [P, NT, 2], I32)
        wqkv = [sb(f"wqkv{i}", [P, 3, P]) for i in range(2)]
        wo = sb("wo", [P, P])
        wqt = sb("wqt", [P, P])
        hs = sb("hs_sb", [P, 1])
        geo = sb("geo", [P, P])
        wrs = sb("wrs", [P, E])
        brs = sb("brs", [P, QC, E])
        gam = sb("gam", [P, QC, P])
        bet = sb("bet", [P, QC, P])
        ident, iota8, iotaj = cst[:, 0, :], cnt[:, 0:E], cnt[:, 2 * E:2 * E + NJ]
        first_row = cnt[:, E:2 * E]

        ln = sb("ln", [P, RING, QC, P])
        stats = sb("stats", [P, 3, QC, 6])
        mv = sb("mv", [P, 3, RING, QC, 2])
        rstd = sb("rstd", [P, 3, RING, QC, 2])
        lnT = sb("lnT", [P, RING, T])
        parts = sb("parts", [P, RING, 3, 2, T], BF16)
        rest = sb("rest", [P, RING, 2, T])
        vaug = sb("vaug", [P, RING, QC, 16, 32])
        qst = sb("qst", [P, RING, 16, T], BF16)
        kst = sb("kst", [P, RING, 16, T], BF16)
        mx = sb("mx", [P, RING, 32])
        mparts = sb("mparts", [32, RING, 2, P], BF16)
        prob = sb("prob", [P, 2, 4, 512])
        oT = sb("oT", [P, RING, 4, T])
        rden = sb("rden", [P, QC, 16])
        on = sb("on", [P, RING, QC, P])
        onT = sb("onT", [P, RING, T])
        row = sb("row", [P, RING, QC, 2, ROW])
        tT = sb("tT", [P, RING, T])
        lg = sb("lg", [P, RING, QC, E])
        mx8 = sb("mx8", [P, RING, QC, 8])
        ix8 = sb("ix8", [P, RING, QC, 8], U32)
        ixf = sb("ixf", [P, QC, 2])
        oh = sb("oh", [P, QC, 2, E])
        ohb = sb("ohb", [P, RING, QC, E], BF16)
        place = sb("place", [P, QC, E])
        pick = sb("pick", [P, QC, 2, E])
        placed = sb("placed", [P, QC, 2])
        index = sb("index", [P, RING, QC, 2], U32)
        run = sb("run", [P, E])
        dv = sb("dv", [P, RING, 3, QC])
        ct = sb("ct", [P, E])
        ct_i = sb("ct_i", [P, E], I32)
        ct_s = sb("ct_s", [P, E], I32)
        tiles = sb("tiles", [P, E])
        upto = [sb(f"upto{i}", [P, E]) for i in range(2)]
        skip = sb("skip", [P, E])
        past = sb("past", [P, NJ, E])
        skipped = sb("skipped", [P, NJ, E])
        t_exp = sb("t_exp", [P, NJ])
        t_row = sb("t_row", [P, NJ])
        t_exp_i = sb("t_exp_i", [P, NJ], I32)
        t_row_i = sb("t_row_i", [P, NJ], I32)
        pad_row = sb("pad_row", [P, E], I32)
        wsl = sb("wsl", [P, SLOTS, WCOLS])
        xt = sb("xt", [P, SLOTS, QC, ROW])
        idw = sb("idw", [P, SLOTS, QC, 2])
        xT = prob[:, 1, :, :].rearrange("p k (a t) -> p (k a) t", a=2)[:, 0:SLOTS, :]
        hT = prob[:, 0, 0:FC // 2, :].rearrange("p k (a t) -> p (k a) t", a=2)
        yT = sb("yT", [P, SLOTS, TILE])
        yt = sb("yt", [P, SLOTS, QC, P])
        yg = sb("yg", [P, RING, 2, QC, P])
        r = sb("r", [P, RING, QC, P])

        pS = [pb("score0"), pb("score1")]
        pM = [pb("max0"), pb("max1")]
        pO = [pb("attn0"), pb("attn1")]
        pX = [pb("misc0"), pb("misc1")]
        pH = [pS[0], pS[1], pM[0], pM[1]]
        pXT, pY, pYT = pO[0], pO[1], pX[0]

        sems = {}

        def s_(name):
            if name not in sems:
                sems[name] = ctx.enter_context(nc.semaphore(name))
            return sems[name]

        for name in """consts_in x_in weights_in bf_made consts_made filled wq_ps wq_made ones_set spare_in
            c_sum c_add c_stats1 c_stats c_eps c_rstd c_norm c_gam c_bet c_x
            ln_stats1 ln_stats ln_eps ln_rstd ln_ready lnT_ps lnT_sb qk_ps part1 rest1 part2 part3 v_ps v_sb
            max_ps max_read mxT_ps m_hi m_lo exp_ps exp_done av_done o_sb oT_ps rden_done on_done onT_ps onT_sb
            pr_ps x_ready t_stats1 t_stats t_eps t_rstd t_ready tT_ps tT_sb lg_ps lg_done mx8_done ix8_done
            ixf_done diff e_done oh_done ohb_done den_done w0_done w1_done rank_ps place_done rank_read pick_done
            placed_done index_done id_done chain tiles_known pads_in xT_ps xT_sb idw_done h_ps h_act h_dve y_ps
            yT_sb yt_ps yt_sb out_w""".split():
            s_(name)
        for name in "y_in scr_w st_in m_in t_cp scat w_in xt_in y_out".split():
            for i in range(RING):
                s_(f"{name}{i}")
        block = ctx.enter_context(nc.Block())

        def wait(eng, name, n):
            if isinstance(n, At):
                assert n.c >= 1, (name, n.a, n.c)
                eng.wait_ge(s_(name), val(n))
            elif n > 0:
                eng.wait_ge(s_(name), n)

        def wait_apart(eng, name, n):
            if isinstance(n, At):
                assert n.c >= 1, (name, n.a, n.c)
                n = eng.to_reg(val(n))
                eng.wait_ge(s_("consts_made"), 1)
                eng.wait_ge(s_(name), n)
            else:
                wait(eng, name, n)

        def steps(eng, stages, step):
            for s in range(stages):
                step(s, s, [k for k in range(stages) if 0 <= s - k < B])
            with eng.Fori(0, (B - stages) // RING) as i:
                for u in range(RING):
                    step(At(i, RING, stages + u), stages + u, list(range(stages)))
            for s in range(B, B + stages - 1):
                step(s, s, [k for k in range(stages) if 0 <= s - k < B])

        def nth(b, slot, li):
            return (b - slot) // RING + 1 + li * len(range(slot, B, RING))

        def sent(b, slot, li):
            return nth(b, slot, li) * 64

        def tok(b):
            return ds(b * QC, QC)

        def tile_of(a, b, c):
            return a[:, ds(b * QC + c, 1), :].rearrange("p a d -> p (a d)")

        LN, TN, CN = 0, 1, 2

        def dve_stats(dve, src, which, pre, v, slot):
            for c in range(QC):
                ins = nc.vector.bn_stats(stats[:, which, c, :], src(c))
            ins.then_inc(s_(pre + "_stats1"), 1)
            wait_apart(dve, pre + "_stats1", v)
            for c in range(QC):
                ins = nc.vector.bn_aggr(mv[:, which, slot, c, :], stats[:, which, c, :])
            ins.then_inc(s_(pre + "_stats"), 1)

        def pool_rstd(pool, which, pre, v, slot):
            wait_apart(pool, pre + "_stats", v)
            nc.gpsimd.tensor_scalar(rstd[:, which, slot, :, 0], mv[:, which, slot, :, 1], EPS, None, ALU.add)\
                .then_inc(s_(pre + "_eps"), 1)
            wait(pool, pre + "_eps", v)
            nc.gpsimd.tensor_tensor(rstd[:, which, slot, :, 1], rstd[:, which, slot, :, 0], halfm[:, :], ALU.pow)\
                .then_inc(s_(pre + "_rstd"), 1)

        def dve_normalise(dve, src, dst, which, pre, v, slot):
            wait(dve, pre + "_rstd", v)
            for c in range(QC):
                ins = nc.vector.tensor_scalar(dst(c), src(c), mv[:, which, slot, c, 0:1],
                                              rstd[:, which, slot, c, 1:2], ALU.subtract, ALU.mult)
            return ins

        def sp_results(sp, b, slot, li):
            wait_apart(sp, "c_sum", B * li + b + 1 - RING)
            for k in range(2):
                src = ys[ds(b * T + k * B * T, T), :].rearrange("(c p) d -> p c d", p=P)
                sp.dma_start(yg[:, slot, k, :, :], src).then_inc(s_(f"y_in{slot}"), 16)

        def pool_sum(pool, b, slot, li):
            v = B * li + b + 1
            wait(pool, f"y_in{slot}", nth(b, slot, li) * 32)
            wait(pool, "c_x", v - RING)
            nc.gpsimd.tensor_tensor(r[:, slot, :, :], yg[:, slot, 0, :, :], yg[:, slot, 1, :, :], ALU.add)\
                .then_inc(s_("c_sum"), 1)

        def dve_sum(dve, b, slot, li):
            v = B * li + b + 1
            wait(dve, "c_sum", v)
            nc.vector.tensor_tensor(r[:, slot, :, :], r[:, slot, :, :], t[:, tok(b), :], ALU.add)\
                .then_inc(s_("c_add"), 1)
            wait_apart(dve, "c_add", v)
            dve_stats(dve, lambda c: r[:, slot, c, :], CN, "c", v, slot)

        def dve_norm(dve, b, slot, li):
            dve_normalise(dve, lambda c: r[:, slot, c, :], lambda c: r[:, slot, c, :], CN, "c",
                          B * li + b + 1, slot).then_inc(s_("c_norm"), 1)

        def pool_scale(pool, b, slot, li):
            v = B * li + b + 1
            wait(pool, "c_norm", v)
            nc.gpsimd.tensor_tensor(r[:, slot, :, :], r[:, slot, :, :], gam[:, :, :], ALU.mult)\
                .then_inc(s_("c_gam"), 1)
            wait(pool, "c_gam", v)
            nc.gpsimd.tensor_tensor(r[:, slot, :, :], r[:, slot, :, :], bet[:, :, :], ALU.add)\
                .then_inc(s_("c_bet"), 1)

        def dve_residual(dve, b, slot, li):
            wait(dve, "c_bet", B * li + b + 1)
            nc.vector.tensor_tensor(x[:, tok(b), :], x[:, tok(b), :], r[:, slot, :, :], ALU.add)\
                .then_inc(s_("c_x"), 1)

        def counts_of(li):
            L0 = LAYERS[0]
            return (B * L0["groups"] * L0["banks"] * li, B * L0["groups"] * li, B * li, 1 + li)

        def names(s, m):
            b = [s - k for k in range(PIPE)]
            return b, [(m - k) % RING for k in range(PIPE)]

        def act_attention(act, li):
            L = LAYERS[li]
            H, hd, G, NB = L["H"], L["hd"], L["groups"], L["banks"]
            e0, g0, _, _ = counts_of(li)

            def exps(b, g, on_):
                if EXPS not in on_:
                    return
                wait(act, "av_done", g0 + b * G + g - 1)
                for k in range(NB):
                    wait(act, "exp_ps", e0 + (b * G + g) * NB + k + 1)
                    nc.scalar.activation(prob[:, g % 2, k, :], pS[(g * NB + k) % 2][:, :], ACT.Exp)\
                        .then_inc(s_("exp_done"), 1)

            def step(s, m, on_):
                b, sl = names(s, m)
                V = [n + (B * li + 1) for n in b]
                bank = BANK[li]
                if PROJECT in on_:
                    wait(act, "lnT_ps", V[2])
                    wait(act, "v_ps", V[2] - RING)
                    nc.scalar.copy(lnT[:, sl[2], :], pX[bank["lnT"]][:, 0:T]).then_inc(s_("lnT_sb"), 1)
                if ROUTE in on_:
                    wait(act, "tT_ps", V[6])
                    nc.scalar.copy(tT[:, sl[6], :], pX[bank["tT"]][:, 0:T]).then_inc(s_("tT_sb"), 1)
                exps(b[4], 0, on_)
                if PROJECT in on_:
                    wait(act, "qk_ps", V[2])
                    wait(act, f"scr_w{sl[2]}", scr_total(b[2], sl[2], li) - scr_per(li))
                    nc.scalar.copy(parts[:, sl[2], 0, :, :],
                                   pX[bank["qk"]][:, :].rearrange("p (a t) -> p a t", a=2)).then_inc(s_("part1"), 1)
                    wait(act, "v_ps", V[2])
                    nc.scalar.copy(vaug[:, sl[2], :, 0:H, 0:hd],
                                   pX[bank["v"]][:, 0:T].rearrange("p (c h d) -> p c h d", c=QC, d=hd))\
                        .then_inc(s_("v_sb"), 1)
                    wait(act, "rest1", V[2])
                    nc.scalar.copy(parts[:, sl[2], 1, :, :], rest[:, sl[2], :, :]).then_inc(s_("part2"), 1)
                if OUTPUT in on_ and L["causal"]:
                    wait(act, "onT_ps", b[5] + 1)
                    nc.scalar.copy(onT[:, sl[5], :], pX[bank["onT"]][:, 0:T]).then_inc(s_("onT_sb"), 1)
                exps(b[4], 1, on_)
                if ROUTE in on_:
                    wait(act, "diff", V[6])
                    nc.scalar.activation(dv[:, sl[6], 1, :], dv[:, sl[6], 0, :], ACT.Exp).then_inc(s_("e_done"), 1)
                for g in range(2, G):
                    exps(b[4], g, on_)
                if EXPS in on_:
                    wait(act, "av_done", g0 + (b[4] + 1) * G)
                    for h in range(G // 2):
                        nc.scalar.copy(oT[:, sl[4], 2 * h:2 * h + 2, :],
                                       pO[h][:, :].rearrange("p (a t) -> p a t", a=2)).then_inc(s_("o_sb"), 1)
            steps(act, PIPE, step)

        def scr_per(li):
            return 16 * (len(LAYERS[li]["q_parts"]) + len(LAYERS[li]["k_parts"]))

        def scr_total(b, slot, li):
            before = len(range(slot, B, RING))
            return (nth(b, slot, 0)) * scr_per(li) + before * li * scr_per(0)

        def sp_attention(sp, li):
            L = LAYERS[li]
            H, hd = L["H"], L["hd"]
            rows = L["width"] * hd
            _, g0, _, _ = counts_of(li)

            def step(s, m, on_):
                b, sl = names(s, m)
                V = [n + (B * li + 1) for n in b]
                if COMBINE in on_ and li:
                    sp_results(sp, b[0], sl[0], 0)
                if PROJECT in on_:
                    i2 = sl[2]
                    wait_apart(sp, "part3", V[2])
                    wait_apart(sp, "part2", V[2])
                    wait_apart(sp, f"st_in{i2}", nth(b[2], i2, li) * 96 - 96)
                    for i, part in enumerate(L["q_parts"]):
                        sp.dma_start(q_scr[i2][i], parts[:, i2, part, 0, :]).then_inc(s_(f"scr_w{i2}"), 16)
                    for i, part in enumerate(L["k_parts"]):
                        sp.dma_start(k_scr[i2][i], parts[:, i2, part, 1, :]).then_inc(s_(f"scr_w{i2}"), 16)
                    wait_apart(sp, f"scr_w{i2}", scr_total(b[2], i2, li))
                    wait_apart(sp, "av_done", g0 + (b[2] - RING + 1) * L["groups"])
                    if isinstance(s, int) and s < 2 + RING:
                        sp.wait_ge(s_("ones_set"), 1 + li)
                    for i in range(3):
                        for st, scr, runs in ((qst, q_scr, L["q_runs"]), (kst, k_scr, L["k_runs"])):
                            src = scr[i2].rearrange("s (r h) t -> (s r) (h t)", h=H)
                            sp.dma_start(st[i * rows:(i + 1) * rows, i2, 0:H, :].rearrange("p h t -> p (h t)"),
                                         src[runs[i] * hd:runs[i] * hd + rows]).then_inc(s_(f"st_in{i2}"), 16)
                if MAXIMA in on_:
                    wait_apart(sp, "m_lo", V[3])
                    for i in range(2):
                        sp.dma_start(qst[L["rows"] + i:L["rows"] + i + 1, sl[3], 0:H, :],
                                     mparts[0:2 * H, sl[3], i, :]).then_inc(s_(f"m_in{sl[3]}"), 16)
                if OUTPUT in on_:
                    wait_apart(sp, "t_ready", V[5])
                    sp.dma_start(t[:, tok(b[5]), :], row[:, sl[5], :, 0, 0:P]).then_inc(s_(f"t_cp{sl[5]}"), 16)
                    sp.dma_start(row[:, sl[5], :, 1, 0:P], row[:, sl[5], :, 0, 0:P])\
                        .then_inc(s_(f"t_cp{sl[5]}"), 16)
            steps(sp, PIPE, step)

        def pe_attention(pe, li):
            L = LAYERS[li]
            H, hd, G, NB, R = L["H"], L["hd"], L["groups"], L["banks"], L["rows"]
            e0, g0, o0, o_per = counts_of(li)
            bank = BANK[li]
            read = {0: None, 1: None}

            def take(name):
                last = read[bank[name]]
                if last:
                    wait(pe, *last)
                read[bank[name]] = None
                return pX[bank[name]]

            def given(name, sem, n):
                read[bank[name]] = (sem, n)

            def mask(dst, m):
                nc.tensor.matmul(dst, identb[:, :], m, start=True, stop=False, skip_group_check=True)

            def exp_banks(b, slot, g, on_, k):
                if EXPS not in on_:
                    return
                c, heads = score_banks(L, g)[k]
                wait(pe, "exp_done", e0 + (b * G + g) * NB + k - 1)
                if k == 0 and g == 0:
                    wait(pe, f"m_in{slot}", nth(b, slot, li) * 32)
                dst = pS[(g * NB + k) % 2]
                if c == "wide":
                    mask(dst[:, :], maske_w[:, :, :, :].rearrange("p a b q -> p (a b q)"))
                    kc, q0, w = 0, 0, T
                elif c == "narrow":
                    mask(dst[:, :], maske_n[:, :, :].rearrange("p a q -> p (a q)"))
                    kc, q0, w = 1, P, P
                else:
                    kc, q0, w = c, 0, T
                for i, h in enumerate(heads):
                    mm = nc.tensor.matmul(dst[:, i * w:(i + 1) * w], kst[0:R + 2, slot, h, kc * P:(kc + 1) * P],
                                          qst[0:R + 2, slot, h, q0:q0 + w],
                                          start=not L["causal"], stop=True, skip_group_check=True)
                mm.then_inc(s_("exp_ps"), 1)

            def max_banks(b, slot, g, on_, k):
                if MAXIMA not in on_:
                    return
                c, heads = score_banks(L, g)[k]
                wait(pe, "max_read", e0 + (b * G + g) * NB + k - 1)
                if k == 0 and g == 0:
                    wait(pe, f"st_in{slot}", nth(b, slot, li) * 96)
                dst = pM[(g * NB + k) % 2]
                if c == "wide":
                    mask(dst[:, :], maskm_w[:, :, :, :].rearrange("p a b q -> p (a b q)"))
                    qc, w = 1, T
                elif c == "narrow":
                    mask(dst[:, :], maskm_n[:, :, :].rearrange("p a q -> p (a q)"))
                    qc, w = 0, P
                else:
                    qc, w = c, T
                for i, h in enumerate(heads):
                    mm = nc.tensor.matmul(dst[:, i * w:(i + 1) * w], qst[0:R, slot, h, qc * P:(qc + 1) * P],
                                          kst[0:R, slot, h, 0:w],
                                          start=not L["causal"], stop=True, skip_group_check=True)
                mm.then_inc(s_("max_ps"), 1)

            def weigh(b, slot, g, on_):
                if EXPS not in on_:
                    return
                wait(pe, "exp_done", e0 + (b * G + g + 1) * NB)
                if g == 0:
                    wait(pe, "v_sb", b + (B * li + 1))
                if g % 2 == 0:
                    wait(pe, "o_sb", o0 + (b - 1) * o_per + g // 2 + 1)
                for kc in range(QC):
                    for j in range(4):
                        lo, src = (g % 2) * T, prob[:, g % 2]
                        if not L["causal"]:
                            rhs = prob[:, g % 2, 2 * kc + j // 2, (j % 2) * T:(j % 2 + 1) * T]
                        elif kc == 0:
                            rhs = prob[:, g % 2, j // 2, (j % 2) * T:(j % 2 + 1) * T]
                        else:
                            rhs, lo = prob[:, g % 2, 2, j * P:(j + 1) * P], lo + P
                        mm = nc.tensor.matmul(pO[g // 2][32 * j:32 * j + 32, lo:(g % 2 + 1) * T],
                                              vaug[:, slot, kc, 4 * g + j, :], rhs,
                                              start=(kc == 0), stop=(kc == QC - 1), skip_group_check=True)
                mm.then_inc(s_("av_done"), 1)

            def step(s, m, on_):
                b, sl = names(s, m)
                V = [n + (B * li + 1) for n in b]
                if not isinstance(s, int) or s == B:
                    read[0] = ("rank_read", V[6] - 1)
                    read[1] = ("m_lo", V[3] - 1) if li else ("x_ready", V[5] - 1)
                if PROJECT in on_:
                    dst = take("lnT")
                    wait(pe, "ln_ready", V[2])
                    for c in range(QC):
                        tr = nc.tensor.transpose(dst[:, c * P:(c + 1) * P], ln[:, sl[2], c, :], ident)
                    tr.then_inc(s_("lnT_ps"), 1)
                    given("lnT", "lnT_sb", V[2])
                if OUTPUT in on_:
                    wait(pe, "o_sb", o0 + (b[5] + 1) * o_per)
                    for c in range(QC):
                        if c == 0 or li:
                            name = "oT2" if c else "oT"
                            dst = take(name)
                        for g in range(G):
                            at = (c * G + g) * P if not li else g * P
                            tr = nc.tensor.transpose(dst[:, at:at + P], oT[:, sl[5], g, c * P:(c + 1) * P], ident)
                        if li:
                            tr.then_inc(s_("oT_ps"), 1)
                            given(name, "on_done", B + b[5] * 2 + c + 1)
                    if not li:
                        tr.then_inc(s_("oT_ps"), 1)
                        given("oT", "on_done", b[5] + 1)
                for k in range(NB):
                    max_banks(b[3], sl[3], 0, on_, k)
                if ROUTE in on_:
                    dst = take("tT")
                    wait(pe, "t_ready", V[6])
                    for c in range(QC):
                        tr = nc.tensor.transpose(dst[:, c * P:(c + 1) * P], row[:, sl[6], c, 0, 0:P], ident)
                    tr.then_inc(s_("tT_ps"), 1)
                    given("tT", "tT_sb", V[6])
                for g in range(1, G):
                    for k in range(NB):
                        exp_banks(b[4], sl[4], g - 1, on_, k)
                        max_banks(b[3], sl[3], g, on_, k)
                    if g > 1:
                        weigh(b[4], sl[4], g - 2, on_)
                    if g == 1 and PROJECT in on_:
                        dst = take("qk")
                        wait(pe, "lnT_sb", V[2])
                        for a in range(2):
                            mm = nc.tensor.matmul(dst[:, a * T:(a + 1) * T], wqkv[li][:, a, :], lnT[:, sl[2], :],
                                                  start=True, stop=True)
                        mm.then_inc(s_("qk_ps"), 1)
                        given("qk", "rest1", V[2])
                        dst = take("v")
                        for c in range(QC):
                            mm = nc.tensor.matmul(dst[:, c * P:(c + 1) * P], lnT[:, sl[2], c * P:(c + 1) * P],
                                                  wqkv[li][:, 2, :], start=True, stop=True)
                        mm.then_inc(s_("v_ps"), 1)
                        given("v", "v_sb", V[2])
                    if g == 1 and ROUTE in on_:
                        dst = take("lg")
                        wait(pe, "tT_sb", V[6])
                        for c in range(QC):
                            mm = nc.tensor.matmul(dst[:, c * E:(c + 1) * E], tT[:, sl[6], c * P:(c + 1) * P],
                                                  wrs[:, :], start=True, stop=True)
                        mm.then_inc(s_("lg_ps"), 1)
                        given("lg", "lg_done", V[6])
                    if g == 1 and OUTPUT in on_ and L["causal"]:
                        dst = take("onT")
                        wait(pe, "on_done", b[5] + 1)
                        for c in range(QC):
                            tr = nc.tensor.transpose(dst[:, c * P:(c + 1) * P], on[:, sl[5], c, :], ident)
                        tr.then_inc(s_("onT_ps"), 1)
                        given("onT", "onT_sb", b[5] + 1)
                    if g == 2 and ROUTE in on_:
                        ranks(b, sl, V)
                if MAXIMA in on_:
                    dst = take("mxT")
                    wait(pe, "max_read", e0 + (b[3] + 1) * G * NB)
                    nc.tensor.transpose(dst[0:2 * H, 0:P], mx[:, sl[3], 0:2 * H], ident).then_inc(s_("mxT_ps"), 1)
                    given("mxT", "m_lo", V[3])
                for k in range(NB):
                    exp_banks(b[4], sl[4], G - 1, on_, k)
                weigh(b[4], sl[4], G - 2, on_)
                if ROUTE in on_ and G == 2:
                    ranks(b, sl, V)
                if OUTPUT in on_ and L["causal"]:
                    dst = take("pr")
                    wait(pe, "onT_sb", b[5] + 1)
                    for c in range(QC):
                        mm = nc.tensor.matmul(dst[:, c * P:(c + 1) * P], onT[:, sl[5], c * P:(c + 1) * P],
                                              wo[:, :], start=True, stop=True)
                    mm.then_inc(s_("pr_ps"), 1)
                    given("pr", "x_ready", b[5] + 1)
                weigh(b[4], sl[4], G - 1, on_)
                if isinstance(s, int):
                    for last in read.values():
                        if last:
                            wait(pe, *last)
                    read[0] = read[1] = None

            def ranks(b, sl, V):
                dst = take("rank")
                wait(pe, "ohb_done", V[6])
                o = ohb[:, sl[6], :, :]
                nc.tensor.matmul(dst[:, 0:QC * E], earlier[:, :], o.rearrange("p c e -> p (c e)"),
                                 start=True, stop=False, skip_group_check=True)
                nc.tensor.matmul(dst[:, E:2 * E], onesb[:, :], o[:, 0, :],
                                 start=False, stop=False, skip_group_check=True)
                for c in range(QC):
                    mm = nc.tensor.matmul(dst[:, QC * E:(QC + 1) * E], onesb[:, :], o[:, c, :],
                                          start=False, stop=(c == QC - 1), skip_group_check=True)
                mm.then_inc(s_("rank_ps"), 1)
                given("rank", "rank_read", V[6])
            steps(pe, PIPE, step)

        def dve_attention(dve, li):
            L = LAYERS[li]
            H, hd, G, NB = L["H"], L["hd"], L["groups"], L["banks"]
            e0, _, _, _ = counts_of(li)
            bank = BANK[li]

            def maxima(b, slot, g, on_):
                if MAXIMA not in on_:
                    return
                for k, (c, heads) in enumerate(score_banks(L, g)):
                    wait(dve, "max_ps", e0 + (b * G + g) * NB + k + 1)
                    qc = {"wide": 1, "narrow": 0}.get(c, c)
                    a, n = 2 * heads[0] + qc, len(heads)
                    nc.vector.tensor_reduce(mx[:, slot, a:a + 2 * n - 1:2],
                                            pM[(g * NB + k) % 2][:, :].rearrange("p (h w) -> p h w", h=n),
                                            axis=AX.X, op=ALU.max).then_inc(s_("max_read"), 1)

            def normed(b, slot, on_):
                if OUTPUT not in on_:
                    return
                for i in range(1 + li):
                    v = B * li + b * (1 + li) + i + 1
                    wait(dve, "oT_ps", v)
                    src = pX[bank["oT2" if i else "oT"]][:, :].rearrange("p (n w) -> p n w", w=32)
                    n = src.shape[1]
                    den = rden[:, :, :].rearrange("p c h -> p (c h)")[:, i * 16:i * 16 + n]
                    dst = on[:, slot, :, :].rearrange("p c d -> p (c d)")[:, i * P:i * P + n * hd]
                    nc.vector.reciprocal(den, src[:, :, hd]).then_inc(s_("rden_done"), 1)
                    wait(dve, "rden_done", v)
                    nc.vector.tensor_tensor(dst.rearrange("p (n d) -> p n d", d=hd), src[:, :, 0:hd],
                                            den.unsqueeze(2).to_broadcast([P, n, hd]), ALU.mult)\
                        .then_inc(s_("on_done"), 1)

            def choose(slot, v):
                wait(dve, "lg_ps", v)
                nc.vector.tensor_tensor(lg[:, slot, :, :],
                                        pX[bank["lg"]][:, 0:QC * E].rearrange("p (c e) -> p c e", c=QC),
                                        brs[:, :, :], ALU.add).then_inc(s_("lg_done"), 1)
                wait_apart(dve, "lg_done", v)
                for c in range(QC):
                    ins = nc.vector.max(mx8[:, slot, c, :], lg[:, slot, c, :])
                ins.then_inc(s_("mx8_done"), 1)
                wait_apart(dve, "mx8_done", v)
                for c in range(QC):
                    ins = nc.vector.max_index(ix8[:, slot, c, :], mx8[:, slot, c, :], lg[:, slot, c, :])
                ins.then_inc(s_("ix8_done"), 1)
                nc.vector.tensor_tensor(dv[:, slot, 0, :], mx8[:, slot, :, 1], mx8[:, slot, :, 0], ALU.subtract)\
                    .then_inc(s_("diff"), 1)
                wait(dve, "ix8_done", v)
                nc.vector.tensor_copy(ixf[:, :, :], ix8[:, slot, :, 0:2]).then_inc(s_("ixf_done"), 1)
                wait(dve, "ixf_done", v)
                nc.vector.tensor_tensor(oh[:, :, :, :], ixf[:, :, :].unsqueeze(3).to_broadcast([P, QC, 2, E]),
                                        iota8.unsqueeze(1).unsqueeze(1).to_broadcast([P, QC, 2, E]), ALU.is_equal)\
                    .then_inc(s_("oh_done"), 1)
                wait(dve, "oh_done", v)
                nc.vector.tensor_tensor(ohb[:, slot, :, :], oh[:, :, 0, :], oh[:, :, 1, :], ALU.add)\
                    .then_inc(s_("ohb_done"), 1)

            def send_to(b, slot, v):
                src = pX[bank["rank"]]
                wait(dve, "rank_ps", v)
                nc.vector.tensor_tensor(place[:, :, :], src[:, 0:QC * E].rearrange("p (c e) -> p c e", c=QC),
                                        run[:, :].unsqueeze(1).to_broadcast([P, QC, E]), ALU.add)\
                    .then_inc(s_("place_done"), 1)
                wait(dve, "e_done", v)
                nc.vector.tensor_scalar(dv[:, slot, 2, :], dv[:, slot, 1, :], 1.0, None, ALU.add)\
                    .then_inc(s_("den_done"), 1)
                wait(dve, "place_done", v)
                nc.vector.tensor_tensor(run[:, :], src[:, QC * E:(QC + 1) * E], run[:, :], ALU.add)\
                    .then_inc(s_("rank_read"), 1)
                nc.vector.tensor_tensor(pick[:, :, :, :], oh[:, :, :, :],
                                        place[:, :, :].unsqueeze(2).to_broadcast([P, QC, 2, E]), ALU.mult)\
                    .then_inc(s_("pick_done"), 1)
                wait(dve, "den_done", v)
                nc.vector.reciprocal(row[:, slot, :, 0, P + 1], dv[:, slot, 2, :]).then_inc(s_("w0_done"), 1)
                wait(dve, "pick_done", v)
                nc.vector.tensor_reduce(placed[:, :, :], pick[:, :, :, :], axis=AX.X, op=ALU.add)\
                    .then_inc(s_("placed_done"), 1)
                wait(dve, "w0_done", v)
                nc.vector.tensor_tensor(row[:, slot, :, 1, P + 1], row[:, slot, :, 0, P + 1], dv[:, slot, 1, :],
                                        ALU.mult).then_inc(s_("w1_done"), 1)
                wait(dve, "placed_done", v)
                nc.vector.tensor_copy(index[:, slot, :, :], placed[:, :, :]).then_inc(s_("index_done"), 1)

            def step(s, m, on_):
                b, sl = names(s, m)
                V = [n + (B * li + 1) for n in b]
                normed(b[5], sl[5], on_)
                maxima(b[3], sl[3], 0, on_)
                if COMBINE in on_ and li:
                    dve_sum(dve, b[0], sl[0], 0)
                if NORM in on_:
                    if not li:
                        wait_apart(dve, "x_in", 16)
                    dve_stats(dve, lambda c: tile_of(x, b[1], c), LN, "ln", V[1], sl[1])
                maxima(b[3], sl[3], 1, on_)
                if PROJECT in on_:
                    wait(dve, "part1", V[2])
                    wait(dve, "part3", V[2] - RING)
                    nc.vector.tensor_tensor(rest[:, sl[2], :, :],
                                            pX[bank["qk"]][:, :].rearrange("p (a t) -> p a t", a=2),
                                            parts[:, sl[2], 0, :, :], ALU.subtract).then_inc(s_("rest1"), 1)
                if ROUTE in on_:
                    choose(sl[6], V[6])
                if MAXIMA in on_ and G == 2:
                    shifts(b[3], sl[3], V[3])
                if G > 2:
                    maxima(b[3], sl[3], 2, on_)
                if COMBINE in on_ and li:
                    dve_norm(dve, b[0], sl[0], 0)
                if NORM in on_:
                    wait(dve, "lnT_ps", V[1] - RING)
                    dve_normalise(dve, lambda c: tile_of(x, b[1], c), lambda c: ln[:, sl[1], c, :], LN, "ln",
                                  V[1], sl[1]).then_inc(s_("ln_ready"), 1)
                if ROUTE in on_:
                    send_to(b[6], sl[6], V[6])
                if OUTPUT in on_:
                    if not li:
                        wait(dve, "pr_ps", V[5])
                        nc.vector.tensor_tensor(x[:, tok(b[5]), :], x[:, tok(b[5]), :],
                                                pX[bank["pr"]][:, 0:T].rearrange("p (c d) -> p c d", c=QC),
                                                ALU.add).then_inc(s_("x_ready"), 1)
                    wait_apart(dve, "x_ready", V[5])
                    dve_stats(dve, lambda c: tile_of(x, b[5], c), TN, "t", V[5], sl[5])
                if G > 2:
                    maxima(b[3], sl[3], 3, on_)
                    if MAXIMA in on_:
                        shifts(b[3], sl[3], V[3])
                if COMBINE in on_ and li:
                    dve_residual(dve, b[0], sl[0], 0)
                if OUTPUT in on_:
                    wait(dve, "id_done", V[5] - RING + 1)
                    dve_normalise(dve, lambda c: tile_of(x, b[5], c), lambda c: row[:, sl[5], c, 0, 0:P], TN, "t",
                                  V[5], sl[5]).then_inc(s_("t_ready"), 1)

            def shifts(b, slot, v):
                src = pX[bank["mxT"]][0:2 * H, 0:P]
                wait(dve, "mxT_ps", v)
                wait(dve, f"m_in{slot}", nth(b, slot, li) * 32 - 32)
                nc.vector.tensor_scalar(mparts[0:2 * H, slot, 0, :], src, -1.0, None, ALU.mult)\
                    .then_inc(s_("m_hi"), 1)
                wait(dve, "m_hi", v)
                nc.vector.scalar_tensor_tensor(out=mparts[0:2 * H, slot, 1, :], in0=src, scalar=-1.0,
                                               in1=mparts[0:2 * H, slot, 0, :], op0=ALU.mult, op1=ALU.subtract)\
                    .then_inc(s_("m_lo"), 1)
            steps(dve, PIPE, step)

        def pool_attention(pool, li):
            def step(s, m, on_):
                b, sl = names(s, m)
                V = [n + (B * li + 1) for n in b]
                if OUTPUT in on_ and li:
                    wait(pool, "on_done", B + (b[5] + 1) * 2)
                    nc.gpsimd.tensor_tensor(x[:, tok(b[5]), :], x[:, tok(b[5]), :], on[:, sl[5], :, :], ALU.add)\
                        .then_inc(s_("x_ready"), 1)
                if COMBINE in on_ and li:
                    pool_sum(pool, b[0], sl[0], 0)
                    pool_rstd(pool, CN, "c", b[0] + 1, sl[0])
                if NORM in on_:
                    pool_rstd(pool, LN, "ln", V[1], sl[1])
                if PROJECT in on_:
                    wait(pool, "part2", V[2])
                    nc.gpsimd.tensor_tensor(parts[:, sl[2], 2, :, :], rest[:, sl[2], :, :],
                                            parts[:, sl[2], 1, :, :], ALU.subtract).then_inc(s_("part3"), 1)
                if COMBINE in on_ and li:
                    pool_scale(pool, b[0], sl[0], 0)
                if OUTPUT in on_:
                    pool_rstd(pool, TN, "t", V[5], sl[5])
                if ROUTE in on_:
                    wait(pool, "index_done", V[6])
                    if not isinstance(s, int) or b[6]:
                        wait(pool, f"scat{(sl[6] - 1) % RING}", sent(b[6] - 1, (sl[6] - 1) % RING, li))
                    wait(pool, f"t_cp{sl[6]}", nth(b[6], sl[6], li) * 32)
                    nc.gpsimd.tensor_copy(row[:, sl[6], :, :, P].bitcast(I32), ids[:, tok(b[6]), :])\
                        .then_inc(s_("id_done"), 1)
                    wait_apart(pool, "id_done", V[6])
                    for c in range(QC):
                        for k in range(2):
                            pool.indirect_dma_start(
                                out=xs, out_offset=bass.IndirectOffsetOnAxis(ap=index[:, sl[6], c, k:k + 1], axis=0),
                                in_=row[:, sl[6], c, k, :], in_offset=None).then_inc(s_(f"scat{sl[6]}"), 16)
            steps(pool, PIPE, step)

        chained = [0]

        def link(dve, ins):
            chained[0] += 1
            ins.then_inc(s_("chain"), 1)
            dve.wait_ge(s_("chain"), chained[0])

        def dve_tiles(dve, li):
            dve.wait_ge(s_("rank_read"), B * (li + 1))
            if li:
                for k in range(SLOTS):
                    dve.wait_ge(s_(f"w_in{k}"), 16 * (NJ // SLOTS))
            nc.vector.tensor_copy(pad_row[:, :], run[:, :])
            link(dve, nc.vector.tensor_tensor(ct[:, :], run[:, :], first_row, ALU.subtract))
            link(dve, nc.vector.tensor_scalar(ct_i[:, :], ct[:, :], float(TILE - 1), None, ALU.add))
            link(dve, nc.vector.tensor_scalar(ct_s[:, :], ct_i[:, :], TILE.bit_length() - 1, None,
                                              ALU.logical_shift_right))
            link(dve, nc.vector.tensor_copy(tiles[:, :], ct_s[:, :]))
            nc.vector.tensor_scalar(skip[:, :], tiles[:, :], -float(TILE), float(REGION), ALU.mult, ALU.add)
            u, d, k = tiles, 1, 0
            while d < E:
                dst = upto[k % 2]
                nc.vector.tensor_copy(dst[:, 0:d], u[:, 0:d])
                link(dve, nc.vector.tensor_tensor(dst[:, d:E], u[:, d:E], u[:, 0:E - d], ALU.add))
                u, d, k = dst, 2 * d, k + 1
            link(dve, nc.vector.tensor_tensor(past[:, :, :], iotaj.unsqueeze(2).to_broadcast([P, NJ, E]),
                                              u[:, :].unsqueeze(1).to_broadcast([P, NJ, E]), ALU.is_ge))
            nc.vector.tensor_reduce(t_exp[:, :], past[:, :, :], axis=AX.X, op=ALU.add)
            link(dve, nc.vector.tensor_tensor(skipped[:, :, :], past[:, :, :],
                                              skip[:, :].unsqueeze(1).to_broadcast([P, NJ, E]), ALU.mult))
            link(dve, nc.vector.tensor_reduce(t_row[:, :], skipped[:, :, :], axis=AX.X, op=ALU.add))
            nc.vector.tensor_scalar(t_exp_i[:, :], t_exp[:, :], float(E - 1), None, ALU.min)
            nc.vector.scalar_tensor_tensor(out=t_row_i[:, :], in0=iotaj, scalar=float(TILE), in1=t_row[:, :],
                                           op0=ALU.mult, op1=ALU.add).then_inc(s_("tiles_known"), 1)
            link(dve, nc.vector.tensor_copy(run[:, :], first_row))

        def tile_loop(eng, body):
            for j in range(SLOTS):
                body(j, j)
            with eng.Fori(0, NJ // SLOTS - 2) as i:
                for k in range(SLOTS):
                    body(At(i, SLOTS, SLOTS + k), k)
            for j in range(NJ - SLOTS, NJ):
                body(j, j % SLOTS)

        def turn(li, j, k):
            return (j - k) // SLOTS + 1 + NJ // SLOTS * li

        def before(j, n):
            return isinstance(j, int) and j < n

        def sp_experts(sp, li):
            sp.wait_ge(s_("tiles_known"), li + 1)
            for e in range(E):
                at = sp.value_load(pad_row[0:1, e:e + 1], min_val=0, max_val=E * REGION - TILE)
                sp.dma_start(xs[bass.ds(at, TILE), :], pads[e * TILE:(e + 1) * TILE, :]).then_inc(s_("pads_in"), 16)
            sp.wait_ge(s_("pads_in"), 16 * E * (li + 1))
            sp.wait_ge(s_("spare_in"), 16)
            for k in range(RING):
                sp.wait_ge(s_(f"scat{k}"), sent(B - 1 - (B - 1 - k) % RING, k, li))

            def body(j, k):
                n = sp.snap(val(j)) if isinstance(j, At) else j
                wait_apart(sp, "yT_sb", NJ * li + j + 1 - SLOTS)
                e = sp.value_load(t_exp_i[0:1, bass.ds(n, 1)], min_val=0, max_val=E - 1)
                at = sp.value_load(t_row_i[0:1, bass.ds(n, 1)], min_val=0,
                                   max_val=E * REGION + (SPARE - 1) * TILE)
                sp.dma_start(wsl[:, k, :], wall[bass.ds(e, 1), :, :].rearrange("a p c -> p (a c)"))\
                    .then_inc(s_(f"w_in{k}"), 16)
                wait_apart(sp, "idw_done", NJ * li + j + 1 - SLOTS)
                wait_apart(sp, "xT_ps", NJ * li + j + 1 - SLOTS)
                sp.dma_start(xt[:, k, :, :], xs[bass.ds(at, TILE), :].rearrange("(c p) d -> p c d", p=P))\
                    .then_inc(s_(f"xt_in{k}"), 16)
            tile_loop(sp, body)

        def pe_experts(pe, li):
            n0 = NJ * li

            def rows_in(j, k):
                wait(pe, f"xt_in{k}", turn(li, j, k) * 16)
                wait(pe, "xT_sb", n0 + j)
                for c in range(QC):
                    tr = nc.tensor.transpose(pXT[:, c * P:(c + 1) * P], xt[:, k, c, 0:P], ident)
                tr.then_inc(s_("xT_ps"), 1)

            def rows_out(j, k):
                wait(pe, "yT_sb", n0 + j + 1)
                wait(pe, "yt_sb", n0 + j)
                for c in range(QC):
                    tr = nc.tensor.transpose(pYT[:, c * P:(c + 1) * P], yT[:, k, c * P:(c + 1) * P], ident)
                tr.then_inc(s_("yt_ps"), 1)

            def body(j, k):
                wait(pe, "xT_sb", n0 + j + 1)
                wait(pe, f"w_in{k}", turn(li, j, k) * 16)
                wait(pe, "h_act", (n0 + j) * 2)
                wait(pe, "h_dve", (n0 + j) * 2)
                for f in range(FC):
                    nc.tensor.matmul(pH[f][:, 0:TILE], wsl[:, k, f * P:(f + 1) * P], xT[:, k, :],
                                     start=True, stop=True).then_inc(s_("h_ps"), 1)
                if not isinstance(j, int) or j + 1 < NJ:
                    rows_in(j + 1, (k + 1) % SLOTS)
                if not before(j, 1):
                    rows_out(j - 1, (k - 1) % SLOTS)
                wait(pe, "yT_sb", n0 + j)
                for f in range(FC):
                    wait(pe, "h_dve" if f % 2 else "h_act", (n0 + j) * 2 + f // 2 + 1)
                    mm = nc.tensor.matmul(pY[:, 0:TILE], wsl[:, k, F + f * P:F + (f + 1) * P], hT[:, f, :],
                                          start=(f == 0), stop=(f == FC - 1))
                mm.then_inc(s_("y_ps"), 1)
            rows_in(0, 0)
            tile_loop(pe, body)
            rows_out(NJ - 1, (NJ - 1) % SLOTS)

        def bias1(k, f):
            return wsl[:, k, F + FC * P + f:F + FC * P + f + 1]

        def act_experts(act, li):
            n0 = NJ * li

            def body(j, k):
                for f in (0, 2):
                    wait(act, "h_ps", (n0 + j) * FC + f + 1)
                    wait(act, "y_ps", n0 + j)
                    nc.scalar.activation(hT[:, f, :], pH[f][:, 0:TILE], ACT.Relu, bias=bias1(k, f))\
                        .then_inc(s_("h_act"), 1)
                wait(act, "y_ps", n0 + j + 1)
                nc.scalar.activation(yT[:, k, :], pY[:, 0:TILE], ACT.Identity,
                                     bias=wsl[:, k, WCOLS - 1:WCOLS]).then_inc(s_("yT_sb"), 1)
            tile_loop(act, body)

        def dve_experts(dve, li):
            n0 = NJ * li

            def columns(j, k):
                wait(dve, "xT_ps", n0 + j + 1)
                nc.vector.tensor_copy(xT[:, k, :], pXT[:, 0:TILE]).then_inc(s_("xT_sb"), 1)
                wait(dve, f"y_out{k}", turn(li, j, k) * 32 - 32)
                nc.vector.tensor_copy(idw[:, k, :, :].bitcast(I32), xt[:, k, :, P:P + 2].bitcast(I32))\
                    .then_inc(s_("idw_done"), 1)

            def weighed(j, k):
                wait(dve, "yt_ps", n0 + j + 1)
                for c in range(QC):
                    ins = nc.vector.tensor_scalar(yt[:, k, c, :], pYT[:, c * P:(c + 1) * P], idw[:, k, c, 1:2],
                                                  None, ALU.mult)
                ins.then_inc(s_("yt_sb"), 1)

            def body(j, k):
                for f in (1, 3):
                    wait(dve, "h_ps", (n0 + j) * FC + f + 1)
                    wait(dve, "y_ps", n0 + j)
                    nc.vector.tensor_scalar(hT[:, f, :], pH[f][:, 0:TILE], bias1(k, f), 0.0, ALU.add, ALU.max)\
                        .then_inc(s_("h_dve"), 1)
                if not isinstance(j, int) or j + 1 < NJ:
                    columns(j + 1, (k + 1) % SLOTS)
                if not before(j, 1):
                    weighed(j - 1, (k - 1) % SLOTS)
            columns(0, 0)
            tile_loop(dve, body)
            weighed(NJ - 1, (NJ - 1) % SLOTS)

        def pool_experts(pool, li):
            if not li:
                pool.wait_ge(s_("av_done"), B * LAYERS[0]["groups"])
                pool_fill(pool, LAYERS[1])

            def body(j, k):
                wait_apart(pool, "yt_sb", NJ * li + j + 1)
                for c in range(QC):
                    pool.indirect_dma_start(
                        out=ys, out_offset=bass.IndirectOffsetOnAxis(ap=idw[:, k, c, 0:1].bitcast(U32), axis=0),
                        in_=yt[:, k, c, :], in_offset=None).then_inc(s_(f"y_out{k}"), 16)
            tile_loop(pool, body)

        def pool_fill(pool, L):
            pair_of_ones = float(np.array([0x3F803F80], np.uint32).view(np.float32)[0])
            n = 2 * LAYERS.index(L)
            nc.gpsimd.memset(kst[L["ones"]:L["ones"] + 32, :, :, :].bitcast(F32), pair_of_ones)\
                .then_inc(s_("filled"), 1)
            pool.wait_ge(s_("filled"), n + 1)
            nc.gpsimd.memset(vaug[:, :, :, :, :], 0.0).then_inc(s_("filled"), 1)
            pool.wait_ge(s_("filled"), n + 2)
            nc.gpsimd.memset(vaug[:, :, :, :, L["hd"]:L["hd"] + 1], 1.0).then_inc(s_("ones_set"), 1)

        def last_steps(eng, step):
            steps(eng, 1, lambda s, m, on_: step(s, m, [k for k in (0, 1) if not isinstance(s, int) or s >= k]))
            step(B, B, [1])

        @block.sync
        def _(sp):
            sp.dma_start(cst[:, :, :], consts.rearrange("s p c -> p s c")).then_inc(s_("consts_in"), 16)
            sp.dma_start(cnt[:, 0:2 * E + NJ], counts).then_inc(s_("consts_in"), 16)
            sp.dma_start(hs[:, :], hs_in).then_inc(s_("consts_in"), 16)
            sp.dma_start(wqt[:, :], wq_t).then_inc(s_("consts_in"), 16)
            sp.dma_start(x[:, :, :], x_in.rearrange("b (c p) d -> p (b c) d", p=P)).then_inc(s_("x_in"), 16)
            sp.dma_start(wqkv[0][:, 1:3, :], w_a.rearrange("p (a c) -> p a c", a=2)).then_inc(s_("weights_in"), 16)
            sp.dma_start(wqkv[1][:, :, :], w_b.rearrange("p (a c) -> p a c", a=3)).then_inc(s_("weights_in"), 16)
            sp.dma_start(wo[:, :], w_o).then_inc(s_("weights_in"), 16)
            sp.dma_start(wrs[:, :], wr).then_inc(s_("weights_in"), 16)
            sp.dma_start(brs[:, :, :], br.unsqueeze(1).to_broadcast([P, QC, E])).then_inc(s_("weights_in"), 16)
            sp.dma_start(gam[:, :, :], gamma.unsqueeze(1).to_broadcast([P, QC, P])).then_inc(s_("weights_in"), 16)
            sp.dma_start(bet[:, :, :], beta.unsqueeze(1).to_broadcast([P, QC, P])).then_inc(s_("weights_in"), 16)
            sp.dma_start(ids[:, :, :], id_in.rearrange("p (n k) -> p n k", k=2)).then_inc(s_("weights_in"), 16)
            sp.dma_start(xs[E * REGION:E * REGION + SPARE * TILE, :], pads[E * TILE:(E + SPARE) * TILE, :])\
                .then_inc(s_("spare_in"), 16)
            for li in range(2):
                sp_attention(sp, li)
                sp_experts(sp, li)
                for k in range(SLOTS):
                    sp.wait_ge(s_(f"y_out{k}"), 32 * (NJ // SLOTS) * (li + 1))

            def step(s, m, on_):
                if 0 in on_:
                    sp_results(sp, s, m % RING, 1)
                if 1 in on_:
                    b = s - 1
                    wait_apart(sp, "c_x", b + B + 1)
                    sp.dma_start(out[ds(b, 1), :, :].rearrange("a (c p) d -> p (a c) d", p=P), x[:, tok(b), :])\
                        .then_inc(s_("out_w"), 16)
            last_steps(sp, step)
            sp.wait_ge(s_("out_w"), 16 * B)

        @block.vector
        def _(dve):
            nc.vector.memset(onesb[:, :], 1.0)
            nc.vector.memset(halfm[:, :], -0.5)
            for mk in (maskm_w, maske_w):
                nc.vector.memset(mk[:, :, :, :], 0.0).then_inc(s_("bf_made"), 1)
            dve.wait_ge(s_("bf_made"), 2)
            dve.wait_ge(s_("consts_in"), 64)
            link(dve, nc.vector.tensor_scalar(geo[:, :], cst[:, 4, :], hs[:, 0:1], None, ALU.mult))
            link(dve, nc.vector.scalar_tensor_tensor(out=geo[:, :], in0=cst[:, 0, :],
                                                     scalar=float(LAYERS[0]["hd"]) ** -0.5, in1=geo[:, :],
                                                     op0=ALU.mult, op1=ALU.add))
            nc.vector.tensor_copy(identb[:, :], cst[:, 0, :])
            nc.vector.tensor_copy(earlier[:, :], cst[:, 3, :])
            nc.vector.tensor_copy(run[:, :], first_row)
            for a in range(2):
                nc.vector.tensor_copy(maskm_w[:, a, 1, :], cst[:, 1, :])
                nc.vector.tensor_copy(maske_w[:, a, 0, :], cst[:, 2, :])
            for a in range(4):
                nc.vector.tensor_copy(maskm_n[:, a, :], cst[:, 1, :])
                ins = nc.vector.tensor_copy(maske_n[:, a, :], cst[:, 2, :])
            ins.then_inc(s_("consts_made"), 1)
            dve.wait_ge(s_("weights_in"), 16 * 8)
            dve.wait_ge(s_("wq_ps"), 1)
            nc.vector.tensor_copy(wqkv[0][:, 0, :], pX[0][:, 0:P])
            nc.vector.tensor_scalar(wqkv[1][:, 0, :], wqkv[1][:, 0, :], float(LAYERS[1]["hd"]) ** -0.5, None,
                                    ALU.mult).then_inc(s_("wq_made"), 1)
            for li in range(2):
                dve_attention(dve, li)
                dve_tiles(dve, li)
                dve_experts(dve, li)

            def step(s, m, on_):
                if 0 in on_:
                    dve_sum(dve, s, m % RING, 1)
                if 1 in on_:
                    dve_norm(dve, s - 1, (m - 1) % RING, 1)
                    dve_residual(dve, s - 1, (m - 1) % RING, 1)
            last_steps(dve, step)

        @block.tensor
        def _(pe):
            pe.wait_ge(s_("consts_made"), 1)
            nc.tensor.matmul(pX[0][:, 0:P], wqt[:, :], geo[:, :], start=True, stop=True).then_inc(s_("wq_ps"), 1)
            pe.wait_ge(s_("wq_made"), 1)
            for li in range(2):
                if li:
                    pe.wait_ge(s_("yt_sb"), NJ)
                    pe.wait_ge(s_("ones_set"), 2)
                else:
                    pe.wait_ge(s_("ones_set"), 1)
                pe_attention(pe, li)
                pe_experts(pe, li)

        @block.scalar
        def _(act):
            act.wait_ge(s_("ones_set"), 1)
            for li in range(2):
                if li:
                    act.wait_ge(s_("ones_set"), 2)
                act_attention(act, li)
                act_experts(act, li)

        @block.gpsimd
        def _(pool):
            pool_fill(pool, LAYERS[0])
            pool.wait_ge(s_("weights_in"), 16 * 8)
            pool.wait_ge(s_("consts_made"), 1)
            for li in range(2):
                pool_attention(pool, li)
                pool_experts(pool, li)

            def step(s, m, on_):
                if 0 in on_:
                    pool_sum(pool, s, m % RING, 1)
                    pool_rstd(pool, CN, "c", s + B + 1, m % RING)
                if 1 in on_:
                    pool_scale(pool, s - 1, (m - 1) % RING, 1)
            last_steps(pool, step)


def kernel(**inputs):
    import numpy as _np
    import concourse.bacc as _bacc
    from concourse import mybir as _mybir
    from concourse.bass_utils import run_bass_kernel_spmd as _run

    a = {k: _np.ascontiguousarray(v) for k, v in inputs.items()}
    D = P

    def by_row(w, H):
        return w.reshape(D, H, D // H).transpose(0, 2, 1).reshape(D, D)

    HA, HB = LAYERS[0]["H"], LAYERS[1]["H"]
    wqkv = a["L0_attn_a_w_qkv"]
    dirs = _np.array([[(i >> 2 & 1) * 2 - 1, (i >> 1 & 1) * 2 - 1, (i & 1) * 2 - 1] for i in range(HA)],
                     dtype=_np.float32) / _np.sqrt(3.0, dtype=_np.float32)
    consts = _np.zeros((5, P, P), _np.float32)
    i = _np.arange(P)
    consts[0] = _np.eye(P, dtype=_np.float32)
    consts[1] = _np.where(i[None, :] > i[:, None], MASKED, 0.0)
    consts[2] = _np.where(i[None, :] < i[:, None], MASKED, 0.0)
    consts[3] = _np.where(i[:, None] < i[None, :], 1.0, 0.0)
    for h in range(HA):
        for r1 in range(3):
            for r2 in range(3):
                consts[4][r1 * HA + h, r2 * HA + h] = dirs[h, r1] * dirs[h, r2]
    counts = _np.zeros((P, 2 * E + NJ), _np.float32)
    counts[:, 0:E] = _np.arange(E)
    counts[:, E:2 * E] = _np.arange(E) * REGION
    counts[:, 2 * E:] = _np.arange(NJ)
    token = _np.arange(NT)[None, :, None] * P + i[:, None, None]
    ids = (token + _np.arange(2)[None, None, :] * B * T).astype(_np.int32).reshape(P, NT * 2)
    pads = _np.zeros(((E + SPARE) * TILE, ROW), _np.float32)
    pads.view(_np.int32)[:, P] = PAIRS + _np.arange((E + SPARE) * TILE)
    w1 = a["L0_ffn_W1"].transpose(0, 2, 1)
    w2 = a["L0_ffn_W2"].transpose(0, 2, 1).reshape(E, FC, P, D).transpose(0, 2, 1, 3).reshape(E, P, FC * D)
    b1 = a["L0_ffn_b1"].reshape(E, FC, P).transpose(0, 2, 1)
    b2 = a["L0_ffn_b2"].reshape(E, D, 1)
    arrays = {
        "x_in": a["L0_attn_a_x"],
        "w_a": _np.concatenate([by_row(wqkv[:, D:2 * D], HA), wqkv[:, 2 * D:]], axis=1),
        "w_o": a["L0_attn_a_w_out"],
        "wq_t": by_row(wqkv[:, 0:D], HA).T,
        "w_b": _np.concatenate([by_row(a["L0_attn_b_Wq"].T, HB), by_row(a["L0_attn_b_Wk"].T, HB),
                                a["L0_attn_b_Wv"].T], axis=1),
        "hs_in": _np.tile(a["L0_attn_a_head_scales"], D // HA).reshape(D, 1),
        "wr": a["L0_ffn_Wr"].T,
        "br": _np.broadcast_to(a["L0_ffn_br"], (P, E)),
        "wall": _np.concatenate([w1, w2, b1, b2], axis=2),
        "gamma": _np.broadcast_to(a["L0_ffn_gamma"], (P, D)),
        "beta": _np.broadcast_to(a["L0_ffn_beta"], (P, D)),
        "consts": consts, "counts": counts, "id_in": ids, "pads": pads,
    }
    nc = _bacc.Bacc("TRN2", target_bir_lowering=False, num_devices=1)
    aps, given = {}, {}
    for name, array in arrays.items():
        array = _np.ascontiguousarray(array)
        given["in_" + name] = array
        aps[name] = nc.dram_tensor("in_" + name, array.shape, _mybir.dt.from_np(array.dtype),
                                   kind="ExternalInput").ap()
    out = nc.dram_tensor("out_x", (B, T, D), F32, kind="ExternalOutput").ap()
    build(nc, out=out, **aps)
    res = _run(nc, [given], core_ids=[0])
    return res.results[0]["out_x"]
```

```python
from contextlib import ExitStack

import numpy as np

import concourse.bass as bass
from concourse import mybir

F32 = mybir.dt.float32
BF16 = mybir.dt.bfloat16
I32 = mybir.dt.int32
U32 = mybir.dt.uint32
ACT = mybir.ActivationFunctionType
ALU = mybir.AluOpType
AX = mybir.AxisListType

P = 128
B = 16
T = 256
QC = T // P
NT = B * QC
F = 512
FC = F // P
E = 8
TILE = 256
NJ = (2 * B * T + E * (TILE - 1)) // TILE
SLOTS = 3
WCOLS = F + FC * P + FC + 1
EPS = 1e-5
MASKED = -1.0e30
PIPE = 8
RING = 3
REGION = B * T + TILE
SPARE = NJ - 2 * B * T // TILE
ROW = P + 2
PAIRS = 2 * B * T
COMBINE, NORM, PROJECT, STACK, MAXIMA, EXPS, OUTPUT, ROUTE = range(PIPE)
assert NJ % SLOTS == 0
BANK = [dict(lnT=0, oT=1, tT=0, qk=1, v=0, lg=1, onT=0, mxT=1, rank=0, pr=1),
        dict(lnT=1, oT=0, oT2=1, tT=0, qk=1, v=0, lg=1, rank=0, mxT=1)]

LAYERS = [
    dict(H=8, hd=16, causal=True, products=6, ones=96, groups=2,
         stack=[(0, 0, 2, 1, 2), (1, 0, 1, 1, 2), (1, 1, 1, 1, 2), (0, 0, 2, 2, 1), (1, 2, 1, 1, 1),
                (1, 0, 1, 1, 1)]),
    dict(H=16, hd=8, causal=False, products=9, ones=64, groups=4,
         stack=[(0, 0, 3, 1, 3), (1, 0, 1, 1, 3), (1, 1, 1, 1, 3), (1, 2, 1, 1, 3)]),
]
for _l in LAYERS:
    _l["rows"] = _l["products"] * _l["hd"]
    _l["banks"] = 3 if _l["causal"] else 4


class At:

    def __init__(self, i, a, c):
        self.i, self.a, self.c = i, a, c

    def __add__(self, n):
        return At(self.i, self.a, self.c + n)

    def __sub__(self, n):
        return At(self.i, self.a, self.c - n)

    def __mul__(self, n):
        return At(self.i, self.a * n, self.c * n)

    def __floordiv__(self, n):
        assert self.a % n == 0
        return At(self.i, self.a // n, self.c // n)

    __radd__, __rmul__ = __add__, __mul__


def val(n):
    if not isinstance(n, At):
        return n
    return n.i * n.a + n.c if n.c else n.i * n.a


def ds(n, size):
    return bass.ds(val(n), size)


def score_banks(layer, g):
    heads = [4 * g + j for j in range(4)]
    if layer["causal"]:
        return [("wide", heads[0:2]), ("wide", heads[2:4]), ("narrow", heads)]
    return [(c, heads[2 * i:2 * i + 2]) for c in range(QC) for i in range(2)]


def build(nc, x_in, w_a, w_o, wq_t, w_b, hs_in, wr, br, wall, gamma, beta, consts, counts, id_in, pads, out):
    with ExitStack() as ctx:
        def sb(name, shape, dt=F32):
            return ctx.enter_context(nc.sbuf_tensor(name, shape, dt))

        def pb(name):
            return ctx.enter_context(nc.psum_tensor(name, [P, 512], F32))

        scr = [nc.dram_tensor(f"scr{i}", (2, 3, P, T), BF16).ap() for i in range(RING)]
        xs = nc.dram_tensor("xs", (E * REGION + SPARE * TILE, ROW), F32).ap()
        ys = nc.dram_tensor("ys", (PAIRS + (E + SPARE) * TILE, P), F32).ap()

        x = sb("x", [P, NT, P])
        t = sb("t", [P, NT, P])
        cst = sb("cst", [P, 5, P])
        cnt = sb("cnt", [P, 2 * E + NJ])
        identb = sb("identb", [P, P], BF16)
        maskm_w = sb("maskm_w", [P, 2, 2, P], BF16)
        maskm_n = sb("maskm_n", [P, 4, P], BF16)
        maske_w = sb("maske_w", [P, 2, 2, P], BF16)
        maske_n = sb("maske_n", [P, 4, P], BF16)
        earlier = sb("earlier", [P, P], BF16)
        onesb = sb("onesb", [P, P], BF16)
        halfm = sb("halfm", [P, QC])
        ids = sb("ids", [P, NT, 2], I32)
        wqkv = [sb(f"wqkv{i}", [P, 3, P]) for i in range(2)]
        wo = sb("wo", [P, P])
        wqt = sb("wqt", [P, P])
        hs = sb("hs_sb", [P, 1])
        geo = sb("geo", [P, P])
        wrs = sb("wrs", [P, E])
        brs = sb("brs", [P, QC, E])
        gam = sb("gam", [P, QC, P])
        bet = sb("bet", [P, QC, P])
        ident, iota8, iotaj = cst[:, 0, :], cnt[:, 0:E], cnt[:, 2 * E:2 * E + NJ]
        first_row = cnt[:, E:2 * E]

        ln = sb("ln", [P, RING, QC, P])
        stats = sb("stats", [P, 3, QC, 6])
        mv = sb("mv", [P, 3, RING, QC, 2])
        rstd = sb("rstd", [P, 3, RING, QC, 2])
        lnT = sb("lnT", [P, RING, T])
        parts = sb("parts", [P, RING, 2, 3, T], BF16)
        rest = sb("rest", [P, RING, 2, T])
        vaug = sb("vaug", [P, RING, QC, 16, 32])
        qst = sb("qst", [P, RING, 16, T], BF16)
        kst = sb("kst", [P, RING, 16, T], BF16)
        mx = sb("mx", [P, RING, 32])
        mparts = sb("mparts", [32, RING, 2, P], BF16)
        prob = sb("prob", [P, 2, 4, 512])
        oT = sb("oT", [P, RING, 4, T])
        rden = sb("rden", [P, QC, 16])
        on = sb("on", [P, RING, QC, P])
        onT = sb("onT", [P, RING, T])
        row = sb("row", [P, RING, QC, 2, ROW])
        tT = sb("tT", [P, RING, T])
        lg = sb("lg", [P, RING, QC, E])
        mx8 = sb("mx8", [P, RING, QC, 8])
        ix8 = sb("ix8", [P, RING, QC, 8], U32)
        ixf = sb("ixf", [P, QC, 2])
        oh = sb("oh", [P, QC, 2, E])
        ohb = sb("ohb", [P, RING, QC, E], BF16)
        place = sb("place", [P, QC, E])
        pick = sb("pick", [P, QC, 2, E])
        placed = sb("placed", [P, QC, 2])
        index = sb("index", [P, RING, QC, 2], U32)
        run = sb("run", [P, E])
        dv = sb("dv", [P, RING, 3, QC])
        ct = sb("ct", [P, E])
        ct_i = sb("ct_i", [P, E], I32)
        ct_s = sb("ct_s", [P, E], I32)
        tiles = sb("tiles", [P, E])
        upto = [sb(f"upto{i}", [P, E]) for i in range(2)]
        skip = sb("skip", [P, E])
        past = sb("past", [P, NJ, E])
        skipped = sb("skipped", [P, NJ, E])
        t_exp = sb("t_exp", [P, NJ])
        t_row = sb("t_row", [P, NJ])
        t_exp_i = sb("t_exp_i", [P, NJ], I32)
        t_row_i = sb("t_row_i", [P, NJ], I32)
        pad_row = sb("pad_row", [P, E], I32)
        wsl = sb("wsl", [P, SLOTS, WCOLS])
        xt = sb("xt", [P, SLOTS, QC, ROW])
        idw = sb("idw", [P, SLOTS, QC, 2])
        xT = prob[:, 1, :, :].rearrange("p k (a t) -> p (k a) t", a=2)[:, 0:SLOTS, :]
        hT = prob[:, 0, 0:FC // 2, :].rearrange("p k (a t) -> p (k a) t", a=2)
        yT = sb("yT", [P, SLOTS, TILE])
        yt = sb("yt", [P, SLOTS, QC, P])
        yg = sb("yg", [P, RING, 2, QC, P])
        r = sb("r", [P, RING, QC, P])

        pS = [pb("score0"), pb("score1")]
        pM = [pb("max0"), pb("max1")]
        pO = [pb("attn0"), pb("attn1")]
        pX = [pb("misc0"), pb("misc1")]
        pH = [pS[0], pS[1], pM[0], pM[1]]
        pXT, pY, pYT = pO[0], pO[1], pX[0]

        sems = {}

        def s_(name):
            if name not in sems:
                sems[name] = ctx.enter_context(nc.semaphore(name))
            return sems[name]

        for name in """consts_in x_in weights_in bf_made consts_made filled wq_ps wq_made ones_set spare_in
            c_sum c_add c_stats1 c_stats c_eps c_rstd c_norm c_gam c_bet c_x
            ln_stats1 ln_stats ln_eps ln_rstd ln_ready lnT_ps lnT_sb qk_ps part1 rest1 part2 part3 v_ps v_sb
            max_ps max_read mxT_ps m_hi m_lo exp_ps exp_done av_done o_sb oT_ps rden_done on_done onT_ps onT_sb
            pr_ps x_ready t_stats1 t_stats t_eps t_rstd t_ready tT_ps tT_sb lg_ps lg_done mx8_done ix8_done
            ixf_done diff e_done oh_done ohb_done den_done w0_done w1_done rank_ps place_done rank_read pick_done
            placed_done index_done id_done chain tiles_known pads_in xT_ps xT_sb idw_done h_ps h_act h_dve y_ps
            yT_sb yt_ps yt_sb out_w""".split():
            s_(name)
        for name in "y_in scr_w st_in m_in t_cp scat w_in xt_in y_out".split():
            for i in range(RING):
                s_(f"{name}{i}")
        block = ctx.enter_context(nc.Block())

        def wait(eng, name, n):
            if isinstance(n, At):
                assert n.c >= 1, (name, n.a, n.c)
                eng.wait_ge(s_(name), val(n))
            elif n > 0:
                eng.wait_ge(s_(name), n)

        def wait_apart(eng, name, n):
            if isinstance(n, At):
                assert n.c >= 1, (name, n.a, n.c)
                n = eng.to_reg(val(n))
                eng.wait_ge(s_("consts_made"), 1)
                eng.wait_ge(s_(name), n)
            else:
                wait(eng, name, n)

        def steps(eng, stages, step):
            for s in range(stages):
                step(s, s, [k for k in range(stages) if 0 <= s - k < B])
            with eng.Fori(0, (B - stages) // RING) as i:
                for u in range(RING):
                    step(At(i, RING, stages + u), stages + u, list(range(stages)))
            for s in range(after_loop(stages), B + stages - 1):
                step(s, s, [k for k in range(stages) if 0 <= s - k < B])

        def after_loop(stages):
            return B - (B - stages) % RING

        def attention_steps(eng, li, step):
            early = 1 - li
            steps(eng, PIPE - early, lambda s, m, on_: step(s + early, m + early, [k + early for k in on_]))

        def nth(b, slot, li):
            return (b - slot) // RING + 1 + li * len(range(slot, B, RING))

        def sent(b, slot, li):
            return nth(b, slot, li) * 64

        def tok(b):
            return ds(b * QC, QC)

        def tile_of(a, b, c):
            return a[:, ds(b * QC + c, 1), :].rearrange("p a d -> p (a d)")

        LN, TN, CN = 0, 1, 2

        def dve_stats(dve, src, which, pre, v, slot):
            for c in range(QC):
                ins = nc.vector.bn_stats(stats[:, which, c, :], src(c))
            ins.then_inc(s_(pre + "_stats1"), 1)
            wait_apart(dve, pre + "_stats1", v)
            for c in range(QC):
                ins = nc.vector.bn_aggr(mv[:, which, slot, c, :], stats[:, which, c, :])
            ins.then_inc(s_(pre + "_stats"), 1)

        def pool_rstd(pool, which, pre, v, slot):
            wait_apart(pool, pre + "_stats", v)
            nc.gpsimd.tensor_scalar(rstd[:, which, slot, :, 0], mv[:, which, slot, :, 1], EPS, None, ALU.add)\
                .then_inc(s_(pre + "_eps"), 1)
            wait(pool, pre + "_eps", v)
            nc.gpsimd.tensor_tensor(rstd[:, which, slot, :, 1], rstd[:, which, slot, :, 0], halfm[:, :], ALU.pow)\
                .then_inc(s_(pre + "_rstd"), 1)

        def dve_normalise(dve, src, dst, which, pre, v, slot):
            wait(dve, pre + "_rstd", v)
            for c in range(QC):
                ins = nc.vector.tensor_scalar(dst(c), src(c), mv[:, which, slot, c, 0:1],
                                              rstd[:, which, slot, c, 1:2], ALU.subtract, ALU.mult)
            return ins

        def sp_results(sp, b, slot, li):
            wait_apart(sp, "c_sum", B * li + b + 1 - RING)
            for k in range(2):
                src = ys[ds(b * T + k * B * T, T), :].rearrange("(c p) d -> p c d", p=P)
                sp.dma_start(yg[:, slot, k, :, :], src).then_inc(s_(f"y_in{slot}"), 16)

        def pool_sum(pool, b, slot, li):
            v = B * li + b + 1
            wait(pool, f"y_in{slot}", nth(b, slot, li) * 32)
            wait(pool, "c_x", v - RING)
            nc.gpsimd.tensor_tensor(r[:, slot, :, :], yg[:, slot, 0, :, :], yg[:, slot, 1, :, :], ALU.add)\
                .then_inc(s_("c_sum"), 1)

        def dve_sum(dve, b, slot, li):
            v = B * li + b + 1
            wait(dve, "c_sum", v)
            nc.vector.tensor_tensor(r[:, slot, :, :], r[:, slot, :, :], t[:, tok(b), :], ALU.add)\
                .then_inc(s_("c_add"), 1)
            wait_apart(dve, "c_add", v)
            dve_stats(dve, lambda c: r[:, slot, c, :], CN, "c", v, slot)

        def dve_norm(dve, b, slot, li):
            dve_normalise(dve, lambda c: r[:, slot, c, :], lambda c: r[:, slot, c, :], CN, "c",
                          B * li + b + 1, slot).then_inc(s_("c_norm"), 1)

        def pool_scale(pool, b, slot, li):
            v = B * li + b + 1
            wait(pool, "c_norm", v)
            nc.gpsimd.tensor_tensor(r[:, slot, :, :], r[:, slot, :, :], gam[:, :, :], ALU.mult)\
                .then_inc(s_("c_gam"), 1)
            wait(pool, "c_gam", v)
            nc.gpsimd.tensor_tensor(r[:, slot, :, :], r[:, slot, :, :], bet[:, :, :], ALU.add)\
                .then_inc(s_("c_bet"), 1)

        def dve_residual(dve, b, slot, li):
            wait(dve, "c_bet", B * li + b + 1)
            nc.vector.tensor_tensor(x[:, tok(b), :], x[:, tok(b), :], r[:, slot, :, :], ALU.add)\
                .then_inc(s_("c_x"), 1)

        def counts_of(li):
            L0 = LAYERS[0]
            return (B * L0["groups"] * L0["banks"] * li, B * L0["groups"] * li, B * li, 1 + li)

        def names(s, m):
            b = [s - k for k in range(PIPE)]
            return b, [(m - k) % RING for k in range(PIPE)]

        def act_attention(act, li):
            L = LAYERS[li]
            H, hd, G, NB = L["H"], L["hd"], L["groups"], L["banks"]
            e0, g0, _, _ = counts_of(li)

            def exps(b, g, on_):
                if EXPS not in on_:
                    return
                wait(act, "av_done", g0 + b * G + g - 1)
                for k in range(NB):
                    wait(act, "exp_ps", e0 + (b * G + g) * NB + k + 1)
                    nc.scalar.activation(prob[:, g % 2, k, :], pS[(g * NB + k) % 2][:, :], ACT.Exp)\
                        .then_inc(s_("exp_done"), 1)

            def step(s, m, on_):
                b, sl = names(s, m)
                V = [n + (B * li + 1) for n in b]
                bank = BANK[li]
                if PROJECT in on_:
                    wait(act, "lnT_ps", V[2])
                    wait(act, "v_ps", V[2] - RING)
                    nc.scalar.copy(lnT[:, sl[2], :], pX[bank["lnT"]][:, 0:T]).then_inc(s_("lnT_sb"), 1)
                if ROUTE in on_:
                    wait(act, "tT_ps", V[7])
                    nc.scalar.copy(tT[:, sl[7], :], pX[bank["tT"]][:, 0:T]).then_inc(s_("tT_sb"), 1)
                exps(b[5], 0, on_)
                if STACK in on_:
                    wait(act, "v_ps", V[3])
                    nc.scalar.copy(vaug[:, sl[3], :, 0:H, 0:hd],
                                   pX[bank["v"]][:, 0:T].rearrange("p (c h d) -> p c h d", c=QC, d=hd))\
                        .then_inc(s_("v_sb"), 1)
                if PROJECT in on_:
                    wait(act, "qk_ps", V[2])
                    wait(act, f"scr_w{sl[2]}", 16 * nth(b[2], sl[2], li) - 16)
                    nc.scalar.copy(parts[:, sl[2], :, 0, :],
                                   pX[bank["qk"]][:, :].rearrange("p (a t) -> p a t", a=2)).then_inc(s_("part1"), 1)
                    wait(act, "rest1", V[2])
                    nc.scalar.copy(parts[:, sl[2], :, 1, :], rest[:, sl[2], :, :]).then_inc(s_("part2"), 1)
                if OUTPUT in on_ and L["causal"]:
                    wait(act, "onT_ps", b[6] + 1)
                    nc.scalar.copy(onT[:, sl[6], :], pX[bank["onT"]][:, 0:T]).then_inc(s_("onT_sb"), 1)
                exps(b[5], 1, on_)
                if ROUTE in on_:
                    wait(act, "diff", V[7])
                    nc.scalar.activation(dv[:, sl[7], 1, :], dv[:, sl[7], 0, :], ACT.Exp).then_inc(s_("e_done"), 1)
                for g in range(2, G):
                    exps(b[5], g, on_)
                if EXPS in on_:
                    wait(act, "av_done", g0 + (b[5] + 1) * G)
                    for h in range(G // 2):
                        nc.scalar.copy(oT[:, sl[5], 2 * h:2 * h + 2, :],
                                       pO[h][:, :].rearrange("p (a t) -> p a t", a=2)).then_inc(s_("o_sb"), 1)
            attention_steps(act, li, step)

        def stacked(b, slot, li):
            n = [16 * len(L["stack"]) for L in LAYERS]
            return nth(b, slot, 0) * n[li] + len(range(slot, B, RING)) * li * n[0]

        def stack_source(slot, li, a, first, n, by, copies):
            L = LAYERS[li]
            src = scr[slot][a][first:first + (n - 1) * by + 1:by].rearrange("s (r h) t -> s r (h t)", h=L["H"])
            if copies == 1:
                return src
            return src.rearrange("s r n -> (s r) n").unsqueeze(0).to_broadcast([copies, n * L["hd"], L["H"] * T])

        def sp_attention(sp, li):
            L = LAYERS[li]
            H, hd = L["H"], L["hd"]
            _, g0, _, _ = counts_of(li)

            def step(s, m, on_):
                b, sl = names(s, m)
                V = [n + (B * li + 1) for n in b]
                if COMBINE in on_ and li:
                    sp_results(sp, b[0], sl[0], 0)
                if STACK in on_:
                    i3 = sl[3]
                    wait_apart(sp, f"scr_w{i3}", 16 * nth(b[3], i3, li))
                    wait_apart(sp, "av_done", g0 + (b[3] - RING + 1) * L["groups"])
                    if isinstance(s, int) and s < STACK + RING:
                        sp.wait_ge(s_("ones_set"), 1 + li)
                    at = [0, 0]
                    for a, first, n, by, copies in L["stack"]:
                        rows = n * copies * hd
                        dst = (qst, kst)[a][at[a]:at[a] + rows, i3, 0:H, :].rearrange("p h t -> p (h t)")
                        sp.dma_start(dst, stack_source(i3, li, a, first, n, by, copies))\
                            .then_inc(s_(f"st_in{i3}"), 16)
                        at[a] += rows
                if PROJECT in on_:
                    i2 = sl[2]
                    wait_apart(sp, "part3", V[2])
                    wait_apart(sp, "part2", V[2])
                    if not isinstance(s, int) or b[2] >= RING:
                        wait_apart(sp, f"st_in{i2}", stacked(b[2] - RING, i2, li))
                    sp.dma_start(scr[i2].rearrange("a s p t -> p (a s) t"),
                                 parts[:, i2, :, :, :].rearrange("p a s t -> p (a s) t"))\
                        .then_inc(s_(f"scr_w{i2}"), 16)
                if MAXIMA in on_:
                    wait_apart(sp, "m_lo", V[4])
                    for i in range(2):
                        sp.dma_start(qst[L["rows"] + i:L["rows"] + i + 1, sl[4], 0:H, :],
                                     mparts[0:2 * H, sl[4], i, :]).then_inc(s_(f"m_in{sl[4]}"), 16)
                if OUTPUT in on_:
                    wait_apart(sp, "t_ready", V[6])
                    sp.dma_start(t[:, tok(b[6]), :], row[:, sl[6], :, 0, 0:P]).then_inc(s_(f"t_cp{sl[6]}"), 16)
                    sp.dma_start(row[:, sl[6], :, 1, 0:P], row[:, sl[6], :, 0, 0:P])\
                        .then_inc(s_(f"t_cp{sl[6]}"), 16)
            attention_steps(sp, li, step)

        def pe_attention(pe, li):
            L = LAYERS[li]
            H, hd, G, NB, R = L["H"], L["hd"], L["groups"], L["banks"], L["rows"]
            e0, g0, o0, o_per = counts_of(li)
            bank = BANK[li]
            read = {0: None, 1: None}

            def take(name):
                last = read[bank[name]]
                if last:
                    wait(pe, *last)
                read[bank[name]] = None
                return pX[bank[name]]

            def given(name, sem, n):
                read[bank[name]] = (sem, n)

            def mask(dst, m):
                nc.tensor.matmul(dst, identb[:, :], m, start=True, stop=False, skip_group_check=True)

            def exp_banks(b, slot, g, on_, k):
                if EXPS not in on_:
                    return
                c, heads = score_banks(L, g)[k]
                wait(pe, "exp_done", e0 + (b * G + g) * NB + k - 1)
                if k == 0 and g == 0:
                    wait(pe, f"m_in{slot}", nth(b, slot, li) * 32)
                dst = pS[(g * NB + k) % 2]
                if c == "wide":
                    mask(dst[:, :], maske_w[:, :, :, :].rearrange("p a b q -> p (a b q)"))
                    kc, q0, w = 0, 0, T
                elif c == "narrow":
                    mask(dst[:, :], maske_n[:, :, :].rearrange("p a q -> p (a q)"))
                    kc, q0, w = 1, P, P
                else:
                    kc, q0, w = c, 0, T
                for i, h in enumerate(heads):
                    mm = nc.tensor.matmul(dst[:, i * w:(i + 1) * w], kst[0:R + 2, slot, h, kc * P:(kc + 1) * P],
                                          qst[0:R + 2, slot, h, q0:q0 + w],
                                          start=not L["causal"], stop=True, skip_group_check=True)
                mm.then_inc(s_("exp_ps"), 1)

            def max_banks(b, slot, g, on_, k):
                if MAXIMA not in on_:
                    return
                c, heads = score_banks(L, g)[k]
                wait(pe, "max_read", e0 + (b * G + g) * NB + k - 1)
                if k == 0 and g == 0:
                    wait(pe, f"st_in{slot}", stacked(b, slot, li))
                dst = pM[(g * NB + k) % 2]
                if c == "wide":
                    mask(dst[:, :], maskm_w[:, :, :, :].rearrange("p a b q -> p (a b q)"))
                    qc, w = 1, T
                elif c == "narrow":
                    mask(dst[:, :], maskm_n[:, :, :].rearrange("p a q -> p (a q)"))
                    qc, w = 0, P
                else:
                    qc, w = c, T
                for i, h in enumerate(heads):
                    mm = nc.tensor.matmul(dst[:, i * w:(i + 1) * w], qst[0:R, slot, h, qc * P:(qc + 1) * P],
                                          kst[0:R, slot, h, 0:w],
                                          start=not L["causal"], stop=True, skip_group_check=True)
                mm.then_inc(s_("max_ps"), 1)

            def weigh(b, slot, g, on_):
                if EXPS not in on_:
                    return
                wait(pe, "exp_done", e0 + (b * G + g + 1) * NB)
                if g == 0:
                    wait(pe, "v_sb", b + (B * li + 1))
                if g % 2 == 0:
                    wait(pe, "o_sb", o0 + (b - 1) * o_per + g // 2 + 1)
                for kc in range(QC):
                    for j in range(4):
                        lo, src = (g % 2) * T, prob[:, g % 2]
                        if not L["causal"]:
                            rhs = prob[:, g % 2, 2 * kc + j // 2, (j % 2) * T:(j % 2 + 1) * T]
                        elif kc == 0:
                            rhs = prob[:, g % 2, j // 2, (j % 2) * T:(j % 2 + 1) * T]
                        else:
                            rhs, lo = prob[:, g % 2, 2, j * P:(j + 1) * P], lo + P
                        mm = nc.tensor.matmul(pO[g // 2][32 * j:32 * j + 32, lo:(g % 2 + 1) * T],
                                              vaug[:, slot, kc, 4 * g + j, :], rhs,
                                              start=(kc == 0), stop=(kc == QC - 1), skip_group_check=True)
                mm.then_inc(s_("av_done"), 1)

            def step(s, m, on_):
                b, sl = names(s, m)
                V = [n + (B * li + 1) for n in b]
                if not isinstance(s, int) or s == after_loop(PIPE - 1 + li) + 1 - li:
                    read[0] = ("rank_read", V[7] - 1)
                    read[1] = ("m_lo", V[4] - 1) if li else ("x_ready", V[6] - 1)
                if PROJECT in on_:
                    dst = take("lnT")
                    wait(pe, "ln_ready", V[2])
                    for c in range(QC):
                        tr = nc.tensor.transpose(dst[:, c * P:(c + 1) * P], ln[:, sl[2], c, :], ident)
                    tr.then_inc(s_("lnT_ps"), 1)
                    given("lnT", "lnT_sb", V[2])
                if OUTPUT in on_:
                    wait(pe, "o_sb", o0 + (b[6] + 1) * o_per)
                    for c in range(QC):
                        if c == 0 or li:
                            name = "oT2" if c else "oT"
                            dst = take(name)
                        for g in range(G):
                            at = (c * G + g) * P if not li else g * P
                            tr = nc.tensor.transpose(dst[:, at:at + P], oT[:, sl[6], g, c * P:(c + 1) * P], ident)
                        if li:
                            tr.then_inc(s_("oT_ps"), 1)
                            given(name, "on_done", B + b[6] * 2 + c + 1)
                    if not li:
                        tr.then_inc(s_("oT_ps"), 1)
                        given("oT", "on_done", b[6] + 1)
                for k in range(NB):
                    max_banks(b[4], sl[4], 0, on_, k)
                if ROUTE in on_:
                    dst = take("tT")
                    wait(pe, "t_ready", V[7])
                    for c in range(QC):
                        tr = nc.tensor.transpose(dst[:, c * P:(c + 1) * P], row[:, sl[7], c, 0, 0:P], ident)
                    tr.then_inc(s_("tT_ps"), 1)
                    given("tT", "tT_sb", V[7])
                for g in range(1, G):
                    for k in range(NB):
                        exp_banks(b[5], sl[5], g - 1, on_, k)
                        max_banks(b[4], sl[4], g, on_, k)
                    if g > 1:
                        weigh(b[5], sl[5], g - 2, on_)
                    if g == 1 and STACK in on_:
                        dst = take("v")
                        for c in range(QC):
                            mm = nc.tensor.matmul(dst[:, c * P:(c + 1) * P], lnT[:, sl[3], c * P:(c + 1) * P],
                                                  wqkv[li][:, 2, :], start=True, stop=True)
                        mm.then_inc(s_("v_ps"), 1)
                        given("v", "v_sb", V[3])
                    if g == 1 and PROJECT in on_:
                        dst = take("qk")
                        wait(pe, "lnT_sb", V[2])
                        for a in range(2):
                            mm = nc.tensor.matmul(dst[:, a * T:(a + 1) * T], wqkv[li][:, a, :], lnT[:, sl[2], :],
                                                  start=True, stop=True)
                        mm.then_inc(s_("qk_ps"), 1)
                        given("qk", "rest1", V[2])
                    if g == 1 and ROUTE in on_:
                        dst = take("lg")
                        wait(pe, "tT_sb", V[7])
                        for c in range(QC):
                            mm = nc.tensor.matmul(dst[:, c * E:(c + 1) * E], tT[:, sl[7], c * P:(c + 1) * P],
                                                  wrs[:, :], start=True, stop=True)
                        mm.then_inc(s_("lg_ps"), 1)
                        given("lg", "lg_done", V[7])
                    if g == 1 and OUTPUT in on_ and L["causal"]:
                        dst = take("onT")
                        wait(pe, "on_done", b[6] + 1)
                        for c in range(QC):
                            tr = nc.tensor.transpose(dst[:, c * P:(c + 1) * P], on[:, sl[6], c, :], ident)
                        tr.then_inc(s_("onT_ps"), 1)
                        given("onT", "onT_sb", b[6] + 1)
                    if g == 2 and ROUTE in on_:
                        ranks(b, sl, V)
                if MAXIMA in on_:
                    dst = take("mxT")
                    wait(pe, "max_read", e0 + (b[4] + 1) * G * NB)
                    nc.tensor.transpose(dst[0:2 * H, 0:P], mx[:, sl[4], 0:2 * H], ident).then_inc(s_("mxT_ps"), 1)
                    given("mxT", "m_lo", V[4])
                for k in range(NB):
                    exp_banks(b[5], sl[5], G - 1, on_, k)
                weigh(b[5], sl[5], G - 2, on_)
                if ROUTE in on_ and G == 2:
                    ranks(b, sl, V)
                if OUTPUT in on_ and L["causal"]:
                    dst = take("pr")
                    wait(pe, "onT_sb", b[6] + 1)
                    for c in range(QC):
                        mm = nc.tensor.matmul(dst[:, c * P:(c + 1) * P], onT[:, sl[6], c * P:(c + 1) * P],
                                              wo[:, :], start=True, stop=True)
                    mm.then_inc(s_("pr_ps"), 1)
                    given("pr", "x_ready", b[6] + 1)
                weigh(b[5], sl[5], G - 1, on_)
                if isinstance(s, int):
                    for last in read.values():
                        if last:
                            wait(pe, *last)
                    read[0] = read[1] = None

            def ranks(b, sl, V):
                dst = take("rank")
                wait(pe, "ohb_done", V[7])
                o = ohb[:, sl[7], :, :]
                nc.tensor.matmul(dst[:, 0:QC * E], earlier[:, :], o.rearrange("p c e -> p (c e)"),
                                 start=True, stop=False, skip_group_check=True)
                nc.tensor.matmul(dst[:, E:2 * E], onesb[:, :], o[:, 0, :],
                                 start=False, stop=False, skip_group_check=True)
                for c in range(QC):
                    mm = nc.tensor.matmul(dst[:, QC * E:(QC + 1) * E], onesb[:, :], o[:, c, :],
                                          start=False, stop=(c == QC - 1), skip_group_check=True)
                mm.then_inc(s_("rank_ps"), 1)
                given("rank", "rank_read", V[7])
            attention_steps(pe, li, step)

        def dve_attention(dve, li):
            L = LAYERS[li]
            H, hd, G, NB = L["H"], L["hd"], L["groups"], L["banks"]
            e0, _, _, _ = counts_of(li)
            bank = BANK[li]

            def maxima(b, slot, g, on_):
                if MAXIMA not in on_:
                    return
                for k, (c, heads) in enumerate(score_banks(L, g)):
                    wait(dve, "max_ps", e0 + (b * G + g) * NB + k + 1)
                    qc = {"wide": 1, "narrow": 0}.get(c, c)
                    a, n = 2 * heads[0] + qc, len(heads)
                    nc.vector.tensor_reduce(mx[:, slot, a:a + 2 * n - 1:2],
                                            pM[(g * NB + k) % 2][:, :].rearrange("p (h w) -> p h w", h=n),
                                            axis=AX.X, op=ALU.max).then_inc(s_("max_read"), 1)

            def normed(b, slot, on_):
                if OUTPUT not in on_:
                    return
                for i in range(1 + li):
                    v = B * li + b * (1 + li) + i + 1
                    wait(dve, "oT_ps", v)
                    src = pX[bank["oT2" if i else "oT"]][:, :].rearrange("p (n w) -> p n w", w=32)
                    n = src.shape[1]
                    den = rden[:, :, :].rearrange("p c h -> p (c h)")[:, i * 16:i * 16 + n]
                    dst = on[:, slot, :, :].rearrange("p c d -> p (c d)")[:, i * P:i * P + n * hd]
                    nc.vector.reciprocal(den, src[:, :, hd]).then_inc(s_("rden_done"), 1)
                    wait(dve, "rden_done", v)
                    nc.vector.tensor_tensor(dst.rearrange("p (n d) -> p n d", d=hd), src[:, :, 0:hd],
                                            den.unsqueeze(2).to_broadcast([P, n, hd]), ALU.mult)\
                        .then_inc(s_("on_done"), 1)

            def choose(slot, v):
                wait(dve, "lg_ps", v)
                nc.vector.tensor_tensor(lg[:, slot, :, :],
                                        pX[bank["lg"]][:, 0:QC * E].rearrange("p (c e) -> p c e", c=QC),
                                        brs[:, :, :], ALU.add).then_inc(s_("lg_done"), 1)
                wait_apart(dve, "lg_done", v)
                for c in range(QC):
                    ins = nc.vector.max(mx8[:, slot, c, :], lg[:, slot, c, :])
                ins.then_inc(s_("mx8_done"), 1)
                wait_apart(dve, "mx8_done", v)
                for c in range(QC):
                    ins = nc.vector.max_index(ix8[:, slot, c, :], mx8[:, slot, c, :], lg[:, slot, c, :])
                ins.then_inc(s_("ix8_done"), 1)
                nc.vector.tensor_tensor(dv[:, slot, 0, :], mx8[:, slot, :, 1], mx8[:, slot, :, 0], ALU.subtract)\
                    .then_inc(s_("diff"), 1)
                wait(dve, "ix8_done", v)
                nc.vector.tensor_copy(ixf[:, :, :], ix8[:, slot, :, 0:2]).then_inc(s_("ixf_done"), 1)
                wait(dve, "ixf_done", v)
                nc.vector.tensor_tensor(oh[:, :, :, :], ixf[:, :, :].unsqueeze(3).to_broadcast([P, QC, 2, E]),
                                        iota8.unsqueeze(1).unsqueeze(1).to_broadcast([P, QC, 2, E]), ALU.is_equal)\
                    .then_inc(s_("oh_done"), 1)
                wait(dve, "oh_done", v)
                nc.vector.tensor_tensor(ohb[:, slot, :, :], oh[:, :, 0, :], oh[:, :, 1, :], ALU.add)\
                    .then_inc(s_("ohb_done"), 1)

            def send_to(b, slot, v):
                src = pX[bank["rank"]]
                wait(dve, "rank_ps", v)
                nc.vector.tensor_tensor(place[:, :, :], src[:, 0:QC * E].rearrange("p (c e) -> p c e", c=QC),
                                        run[:, :].unsqueeze(1).to_broadcast([P, QC, E]), ALU.add)\
                    .then_inc(s_("place_done"), 1)
                wait(dve, "e_done", v)
                nc.vector.tensor_scalar(dv[:, slot, 2, :], dv[:, slot, 1, :], 1.0, None, ALU.add)\
                    .then_inc(s_("den_done"), 1)
                wait(dve, "place_done", v)
                nc.vector.tensor_tensor(run[:, :], src[:, QC * E:(QC + 1) * E], run[:, :], ALU.add)\
                    .then_inc(s_("rank_read"), 1)
                nc.vector.tensor_tensor(pick[:, :, :, :], oh[:, :, :, :],
                                        place[:, :, :].unsqueeze(2).to_broadcast([P, QC, 2, E]), ALU.mult)\
                    .then_inc(s_("pick_done"), 1)
                wait(dve, "den_done", v)
                nc.vector.reciprocal(row[:, slot, :, 0, P + 1], dv[:, slot, 2, :]).then_inc(s_("w0_done"), 1)
                wait(dve, "pick_done", v)
                nc.vector.tensor_reduce(placed[:, :, :], pick[:, :, :, :], axis=AX.X, op=ALU.add)\
                    .then_inc(s_("placed_done"), 1)
                wait(dve, "w0_done", v)
                nc.vector.tensor_tensor(row[:, slot, :, 1, P + 1], row[:, slot, :, 0, P + 1], dv[:, slot, 1, :],
                                        ALU.mult).then_inc(s_("w1_done"), 1)
                wait(dve, "placed_done", v)
                nc.vector.tensor_copy(index[:, slot, :, :], placed[:, :, :]).then_inc(s_("index_done"), 1)

            def step(s, m, on_):
                b, sl = names(s, m)
                V = [n + (B * li + 1) for n in b]
                normed(b[6], sl[6], on_)
                maxima(b[4], sl[4], 0, on_)
                if COMBINE in on_ and li:
                    dve_sum(dve, b[0], sl[0], 0)
                if NORM in on_:
                    if not li:
                        wait_apart(dve, "x_in", 16)
                    dve_stats(dve, lambda c: tile_of(x, b[1], c), LN, "ln", V[1], sl[1])
                maxima(b[4], sl[4], 1, on_)
                if PROJECT in on_:
                    wait(dve, "part1", V[2])
                    wait(dve, "part3", V[2] - RING)
                    nc.vector.tensor_tensor(rest[:, sl[2], :, :],
                                            pX[bank["qk"]][:, :].rearrange("p (a t) -> p a t", a=2),
                                            parts[:, sl[2], :, 0, :], ALU.subtract).then_inc(s_("rest1"), 1)
                if ROUTE in on_:
                    choose(sl[7], V[7])
                if MAXIMA in on_ and G == 2:
                    shifts(b[4], sl[4], V[4])
                if G > 2:
                    maxima(b[4], sl[4], 2, on_)
                if COMBINE in on_ and li:
                    dve_norm(dve, b[0], sl[0], 0)
                if NORM in on_:
                    wait(dve, "lnT_ps", V[1] - RING)
                    dve_normalise(dve, lambda c: tile_of(x, b[1], c), lambda c: ln[:, sl[1], c, :], LN, "ln",
                                  V[1], sl[1]).then_inc(s_("ln_ready"), 1)
                if ROUTE in on_:
                    send_to(b[7], sl[7], V[7])
                if OUTPUT in on_:
                    if not li:
                        wait(dve, "pr_ps", V[6])
                        nc.vector.tensor_tensor(x[:, tok(b[6]), :], x[:, tok(b[6]), :],
                                                pX[bank["pr"]][:, 0:T].rearrange("p (c d) -> p c d", c=QC),
                                                ALU.add).then_inc(s_("x_ready"), 1)
                    wait_apart(dve, "x_ready", V[6])
                    dve_stats(dve, lambda c: tile_of(x, b[6], c), TN, "t", V[6], sl[6])
                if G > 2:
                    maxima(b[4], sl[4], 3, on_)
                    if MAXIMA in on_:
                        shifts(b[4], sl[4], V[4])
                if COMBINE in on_ and li:
                    dve_residual(dve, b[0], sl[0], 0)
                if OUTPUT in on_:
                    wait(dve, "id_done", V[6] - RING + 1)
                    dve_normalise(dve, lambda c: tile_of(x, b[6], c), lambda c: row[:, sl[6], c, 0, 0:P], TN, "t",
                                  V[6], sl[6]).then_inc(s_("t_ready"), 1)

            def shifts(b, slot, v):
                src = pX[bank["mxT"]][0:2 * H, 0:P]
                wait(dve, "mxT_ps", v)
                wait(dve, f"m_in{slot}", nth(b, slot, li) * 32 - 32)
                nc.vector.tensor_scalar(mparts[0:2 * H, slot, 0, :], src, -1.0, None, ALU.mult)\
                    .then_inc(s_("m_hi"), 1)
                wait(dve, "m_hi", v)
                nc.vector.scalar_tensor_tensor(out=mparts[0:2 * H, slot, 1, :], in0=src, scalar=-1.0,
                                               in1=mparts[0:2 * H, slot, 0, :], op0=ALU.mult, op1=ALU.subtract)\
                    .then_inc(s_("m_lo"), 1)
            attention_steps(dve, li, step)

        def pool_attention(pool, li):
            def step(s, m, on_):
                b, sl = names(s, m)
                V = [n + (B * li + 1) for n in b]
                if OUTPUT in on_ and li:
                    wait(pool, "on_done", B + (b[6] + 1) * 2)
                    nc.gpsimd.tensor_tensor(x[:, tok(b[6]), :], x[:, tok(b[6]), :], on[:, sl[6], :, :], ALU.add)\
                        .then_inc(s_("x_ready"), 1)
                if COMBINE in on_ and li:
                    pool_sum(pool, b[0], sl[0], 0)
                    pool_rstd(pool, CN, "c", b[0] + 1, sl[0])
                if NORM in on_:
                    pool_rstd(pool, LN, "ln", V[1], sl[1])
                if PROJECT in on_:
                    wait(pool, "part2", V[2])
                    nc.gpsimd.tensor_tensor(parts[:, sl[2], :, 2, :], rest[:, sl[2], :, :],
                                            parts[:, sl[2], :, 1, :], ALU.subtract).then_inc(s_("part3"), 1)
                if COMBINE in on_ and li:
                    pool_scale(pool, b[0], sl[0], 0)
                if OUTPUT in on_:
                    pool_rstd(pool, TN, "t", V[6], sl[6])
                if ROUTE in on_:
                    wait(pool, "index_done", V[7])
                    if not isinstance(s, int) or b[7]:
                        wait(pool, f"scat{(sl[7] - 1) % RING}", sent(b[7] - 1, (sl[7] - 1) % RING, li))
                    wait(pool, f"t_cp{sl[7]}", nth(b[7], sl[7], li) * 32)
                    nc.gpsimd.tensor_copy(row[:, sl[7], :, :, P].bitcast(I32), ids[:, tok(b[7]), :])\
                        .then_inc(s_("id_done"), 1)
                    wait_apart(pool, "id_done", V[7])
                    for c in range(QC):
                        for k in range(2):
                            pool.indirect_dma_start(
                                out=xs, out_offset=bass.IndirectOffsetOnAxis(ap=index[:, sl[7], c, k:k + 1], axis=0),
                                in_=row[:, sl[7], c, k, :], in_offset=None).then_inc(s_(f"scat{sl[7]}"), 16)
            attention_steps(pool, li, step)

        chained = [0]

        def link(dve, ins):
            chained[0] += 1
            ins.then_inc(s_("chain"), 1)
            dve.wait_ge(s_("chain"), chained[0])

        def dve_tiles(dve, li):
            dve.wait_ge(s_("rank_read"), B * (li + 1))
            if li:
                for k in range(SLOTS):
                    dve.wait_ge(s_(f"w_in{k}"), 16 * (NJ // SLOTS))
            nc.vector.tensor_copy(pad_row[:, :], run[:, :])
            link(dve, nc.vector.tensor_tensor(ct[:, :], run[:, :], first_row, ALU.subtract))
            link(dve, nc.vector.tensor_scalar(ct_i[:, :], ct[:, :], float(TILE - 1), None, ALU.add))
            link(dve, nc.vector.tensor_scalar(ct_s[:, :], ct_i[:, :], TILE.bit_length() - 1, None,
                                              ALU.logical_shift_right))
            link(dve, nc.vector.tensor_copy(tiles[:, :], ct_s[:, :]))
            nc.vector.tensor_scalar(skip[:, :], tiles[:, :], -float(TILE), float(REGION), ALU.mult, ALU.add)
            u, d, k = tiles, 1, 0
            while d < E:
                dst = upto[k % 2]
                nc.vector.tensor_copy(dst[:, 0:d], u[:, 0:d])
                link(dve, nc.vector.tensor_tensor(dst[:, d:E], u[:, d:E], u[:, 0:E - d], ALU.add))
                u, d, k = dst, 2 * d, k + 1
            link(dve, nc.vector.tensor_tensor(past[:, :, :], iotaj.unsqueeze(2).to_broadcast([P, NJ, E]),
                                              u[:, :].unsqueeze(1).to_broadcast([P, NJ, E]), ALU.is_ge))
            nc.vector.tensor_reduce(t_exp[:, :], past[:, :, :], axis=AX.X, op=ALU.add)
            link(dve, nc.vector.tensor_tensor(skipped[:, :, :], past[:, :, :],
                                              skip[:, :].unsqueeze(1).to_broadcast([P, NJ, E]), ALU.mult))
            link(dve, nc.vector.tensor_reduce(t_row[:, :], skipped[:, :, :], axis=AX.X, op=ALU.add))
            nc.vector.tensor_scalar(t_exp_i[:, :], t_exp[:, :], float(E - 1), None, ALU.min)
            nc.vector.scalar_tensor_tensor(out=t_row_i[:, :], in0=iotaj, scalar=float(TILE), in1=t_row[:, :],
                                           op0=ALU.mult, op1=ALU.add).then_inc(s_("tiles_known"), 1)
            link(dve, nc.vector.tensor_copy(run[:, :], first_row))

        def tile_loop(eng, body):
            first = SLOTS + 1
            turns = (NJ - first - 1) // SLOTS
            for j in range(first):
                body(j, j % SLOTS)
            with eng.Fori(0, turns) as i:
                for k in range(first, first + SLOTS):
                    body(At(i, SLOTS, k), k % SLOTS)
            for j in range(first + turns * SLOTS, NJ):
                body(j, j % SLOTS)

        def turn(li, j, k):
            return (j - k) // SLOTS + 1 + NJ // SLOTS * li

        def before(j, n):
            return isinstance(j, int) and j < n

        def sp_experts(sp, li):
            sp.wait_ge(s_("tiles_known"), li + 1)
            for e in range(E):
                at = sp.value_load(pad_row[0:1, e:e + 1], min_val=0, max_val=E * REGION - TILE)
                sp.dma_start(xs[bass.ds(at, TILE), :], pads[e * TILE:(e + 1) * TILE, :]).then_inc(s_("pads_in"), 16)
            sp.wait_ge(s_("pads_in"), 16 * E * (li + 1))
            sp.wait_ge(s_("spare_in"), 16)
            for k in range(RING):
                sp.wait_ge(s_(f"scat{k}"), sent(B - 1 - (B - 1 - k) % RING, k, li))

            def body(j, k):
                n = sp.snap(val(j)) if isinstance(j, At) else j
                wait_apart(sp, "yT_sb", NJ * li + j + 1 - SLOTS)
                e = sp.value_load(t_exp_i[0:1, bass.ds(n, 1)], min_val=0, max_val=E - 1)
                at = sp.value_load(t_row_i[0:1, bass.ds(n, 1)], min_val=0,
                                   max_val=E * REGION + (SPARE - 1) * TILE)
                sp.dma_start(wsl[:, k, :], wall[bass.ds(e, 1), :, :].rearrange("a p c -> p (a c)"))\
                    .then_inc(s_(f"w_in{k}"), 16)
                wait_apart(sp, "idw_done", NJ * li + j + 1 - SLOTS)
                wait_apart(sp, "xT_ps", NJ * li + j + 1 - SLOTS)
                sp.dma_start(xt[:, k, :, :], xs[bass.ds(at, TILE), :].rearrange("(c p) d -> p c d", p=P))\
                    .then_inc(s_(f"xt_in{k}"), 16)
            tile_loop(sp, body)

        def pe_experts(pe, li):
            n0 = NJ * li

            def rows_in(j, k):
                wait(pe, f"xt_in{k}", turn(li, j, k) * 16)
                wait(pe, "xT_sb", n0 + j)
                for c in range(QC):
                    tr = nc.tensor.transpose(pXT[:, c * P:(c + 1) * P], xt[:, k, c, 0:P], ident)
                tr.then_inc(s_("xT_ps"), 1)

            def rows_out(j, k):
                wait(pe, "yT_sb", n0 + j + 1)
                wait(pe, "yt_sb", n0 + j)
                for c in range(QC):
                    tr = nc.tensor.transpose(pYT[:, c * P:(c + 1) * P], yT[:, k, c * P:(c + 1) * P], ident)
                tr.then_inc(s_("yt_ps"), 1)

            def body(j, k):
                wait(pe, "xT_sb", n0 + j + 1)
                wait(pe, f"w_in{k}", turn(li, j, k) * 16)
                wait(pe, "h_act", (n0 + j) * 2)
                wait(pe, "h_dve", (n0 + j) * 2)
                for f in range(FC):
                    nc.tensor.matmul(pH[f][:, 0:TILE], wsl[:, k, f * P:(f + 1) * P], xT[:, k, :],
                                     start=True, stop=True).then_inc(s_("h_ps"), 1)
                if not isinstance(j, int) or j + 1 < NJ:
                    rows_in(j + 1, (k + 1) % SLOTS)
                if not before(j, 1):
                    rows_out(j - 1, (k - 1) % SLOTS)
                wait(pe, "yT_sb", n0 + j)
                for f in range(FC):
                    wait(pe, "h_dve" if f % 2 else "h_act", (n0 + j) * 2 + f // 2 + 1)
                    mm = nc.tensor.matmul(pY[:, 0:TILE], wsl[:, k, F + f * P:F + (f + 1) * P], hT[:, f, :],
                                          start=(f == 0), stop=(f == FC - 1))
                mm.then_inc(s_("y_ps"), 1)
            rows_in(0, 0)
            tile_loop(pe, body)
            rows_out(NJ - 1, (NJ - 1) % SLOTS)

        def bias1(k, f):
            return wsl[:, k, F + FC * P + f:F + FC * P + f + 1]

        def act_experts(act, li):
            n0 = NJ * li

            def body(j, k):
                for f in (0, 2):
                    wait(act, "h_ps", (n0 + j) * FC + f + 1)
                    wait(act, "y_ps", n0 + j)
                    nc.scalar.activation(hT[:, f, :], pH[f][:, 0:TILE], ACT.Relu, bias=bias1(k, f))\
                        .then_inc(s_("h_act"), 1)
                wait(act, "y_ps", n0 + j + 1)
                nc.scalar.activation(yT[:, k, :], pY[:, 0:TILE], ACT.Identity,
                                     bias=wsl[:, k, WCOLS - 1:WCOLS]).then_inc(s_("yT_sb"), 1)
            tile_loop(act, body)

        def dve_experts(dve, li):
            n0 = NJ * li

            def columns(j, k):
                wait(dve, "xT_ps", n0 + j + 1)
                nc.vector.tensor_copy(xT[:, k, :], pXT[:, 0:TILE]).then_inc(s_("xT_sb"), 1)

            def weighed(j, k):
                wait(dve, f"y_out{k}", turn(li, j, k) * 32 - 32)
                nc.vector.tensor_copy(idw[:, k, :, :].bitcast(I32), xt[:, k, :, P:P + 2].bitcast(I32))\
                    .then_inc(s_("idw_done"), 1)
                wait(dve, "idw_done", n0 + j + 1)
                wait(dve, "yt_ps", n0 + j + 1)
                for c in range(QC):
                    ins = nc.vector.tensor_scalar(yt[:, k, c, :], pYT[:, c * P:(c + 1) * P], idw[:, k, c, 1:2],
                                                  None, ALU.mult)
                ins.then_inc(s_("yt_sb"), 1)

            def body(j, k):
                for f in (1, 3):
                    wait(dve, "h_ps", (n0 + j) * FC + f + 1)
                    wait(dve, "y_ps", n0 + j)
                    nc.vector.tensor_scalar(hT[:, f, :], pH[f][:, 0:TILE], bias1(k, f), 0.0, ALU.add, ALU.max)\
                        .then_inc(s_("h_dve"), 1)
                if not isinstance(j, int) or j + 1 < NJ:
                    columns(j + 1, (k + 1) % SLOTS)
                if not before(j, 1):
                    weighed(j - 1, (k - 1) % SLOTS)
            columns(0, 0)
            tile_loop(dve, body)
            weighed(NJ - 1, (NJ - 1) % SLOTS)

        def pool_experts(pool, li):
            if not li:
                pool.wait_ge(s_("av_done"), B * LAYERS[0]["groups"])
                pool_fill(pool, LAYERS[1])

            def body(j, k):
                wait_apart(pool, "yt_sb", NJ * li + j + 1)
                for c in range(QC):
                    pool.indirect_dma_start(
                        out=ys, out_offset=bass.IndirectOffsetOnAxis(ap=idw[:, k, c, 0:1].bitcast(U32), axis=0),
                        in_=yt[:, k, c, :], in_offset=None).then_inc(s_(f"y_out{k}"), 16)
            tile_loop(pool, body)

        def pool_fill(pool, L):
            pair_of_ones = float(np.array([0x3F803F80], np.uint32).view(np.float32)[0])
            n = 2 * LAYERS.index(L)
            nc.gpsimd.memset(kst[L["ones"]:L["ones"] + 32, :, :, :].bitcast(F32), pair_of_ones)\
                .then_inc(s_("filled"), 1)
            pool.wait_ge(s_("filled"), n + 1)
            nc.gpsimd.memset(vaug[:, :, :, :, :], 0.0).then_inc(s_("filled"), 1)
            pool.wait_ge(s_("filled"), n + 2)
            nc.gpsimd.memset(vaug[:, :, :, :, L["hd"]:L["hd"] + 1], 1.0).then_inc(s_("ones_set"), 1)

        def last_steps(eng, step):
            steps(eng, 1, lambda s, m, on_: step(s, m, [k for k in (0, 1) if not isinstance(s, int) or s >= k]))
            step(B, B, [1])

        @block.sync
        def _(sp):
            sp.dma_start(cst[:, :, :], consts.rearrange("s p c -> p s c")).then_inc(s_("consts_in"), 16)
            sp.dma_start(cnt[:, 0:2 * E + NJ], counts).then_inc(s_("consts_in"), 16)
            sp.dma_start(hs[:, :], hs_in).then_inc(s_("consts_in"), 16)
            sp.dma_start(wqt[:, :], wq_t).then_inc(s_("consts_in"), 16)
            sp.dma_start(x[:, :, :], x_in.rearrange("b (c p) d -> p (b c) d", p=P)).then_inc(s_("x_in"), 16)
            sp.dma_start(wqkv[0][:, 1:3, :], w_a.rearrange("p (a c) -> p a c", a=2)).then_inc(s_("weights_in"), 16)
            sp.dma_start(wqkv[1][:, :, :], w_b.rearrange("p (a c) -> p a c", a=3)).then_inc(s_("weights_in"), 16)
            sp.dma_start(wo[:, :], w_o).then_inc(s_("weights_in"), 16)
            sp.dma_start(wrs[:, :], wr).then_inc(s_("weights_in"), 16)
            sp.dma_start(brs[:, :, :], br.unsqueeze(1).to_broadcast([P, QC, E])).then_inc(s_("weights_in"), 16)
            sp.dma_start(gam[:, :, :], gamma.unsqueeze(1).to_broadcast([P, QC, P])).then_inc(s_("weights_in"), 16)
            sp.dma_start(bet[:, :, :], beta.unsqueeze(1).to_broadcast([P, QC, P])).then_inc(s_("weights_in"), 16)
            sp.dma_start(ids[:, :, :], id_in.rearrange("p (n k) -> p n k", k=2)).then_inc(s_("weights_in"), 16)
            sp.dma_start(xs[E * REGION:E * REGION + SPARE * TILE, :], pads[E * TILE:(E + SPARE) * TILE, :])\
                .then_inc(s_("spare_in"), 16)
            for li in range(2):
                sp_attention(sp, li)
                sp_experts(sp, li)
                for k in range(SLOTS):
                    sp.wait_ge(s_(f"y_out{k}"), 32 * (NJ // SLOTS) * (li + 1))

            def step(s, m, on_):
                if 0 in on_:
                    sp_results(sp, s, m % RING, 1)
            last_steps(sp, step)
            sp.wait_ge(s_("out_w"), 16 * B)

        @block.vector
        def _(dve):
            nc.vector.memset(onesb[:, :], 1.0)
            nc.vector.memset(halfm[:, :], -0.5)
            for mk in (maskm_w, maske_w):
                nc.vector.memset(mk[:, :, :, :], 0.0).then_inc(s_("bf_made"), 1)
            dve.wait_ge(s_("bf_made"), 2)
            dve.wait_ge(s_("consts_in"), 64)
            link(dve, nc.vector.tensor_scalar(geo[:, :], cst[:, 4, :], hs[:, 0:1], None, ALU.mult))
            link(dve, nc.vector.scalar_tensor_tensor(out=geo[:, :], in0=cst[:, 0, :],
                                                     scalar=float(LAYERS[0]["hd"]) ** -0.5, in1=geo[:, :],
                                                     op0=ALU.mult, op1=ALU.add))
            nc.vector.tensor_copy(identb[:, :], cst[:, 0, :])
            nc.vector.tensor_copy(earlier[:, :], cst[:, 3, :])
            nc.vector.tensor_copy(run[:, :], first_row)
            for a in range(2):
                nc.vector.tensor_copy(maskm_w[:, a, 1, :], cst[:, 1, :])
                nc.vector.tensor_copy(maske_w[:, a, 0, :], cst[:, 2, :])
            for a in range(4):
                nc.vector.tensor_copy(maskm_n[:, a, :], cst[:, 1, :])
                ins = nc.vector.tensor_copy(maske_n[:, a, :], cst[:, 2, :])
            ins.then_inc(s_("consts_made"), 1)
            dve.wait_ge(s_("weights_in"), 16 * 8)
            dve.wait_ge(s_("wq_ps"), 1)
            nc.vector.tensor_copy(wqkv[0][:, 0, :], pX[0][:, 0:P])
            nc.vector.tensor_scalar(wqkv[1][:, 0, :], wqkv[1][:, 0, :], float(LAYERS[1]["hd"]) ** -0.5, None,
                                    ALU.mult).then_inc(s_("wq_made"), 1)
            for li in range(2):
                dve_attention(dve, li)
                dve_tiles(dve, li)
                dve_experts(dve, li)

            def step(s, m, on_):
                if 0 in on_:
                    dve_sum(dve, s, m % RING, 1)
                if 1 in on_:
                    dve_norm(dve, s - 1, (m - 1) % RING, 1)
                    dve_residual(dve, s - 1, (m - 1) % RING, 1)
            last_steps(dve, step)

        @block.tensor
        def _(pe):
            pe.wait_ge(s_("consts_made"), 1)
            nc.tensor.matmul(pX[0][:, 0:P], wqt[:, :], geo[:, :], start=True, stop=True).then_inc(s_("wq_ps"), 1)
            pe.wait_ge(s_("wq_made"), 1)
            for li in range(2):
                if li:
                    pe.wait_ge(s_("yt_sb"), NJ)
                    pe.wait_ge(s_("ones_set"), 2)
                else:
                    pe.wait_ge(s_("ones_set"), 1)
                pe_attention(pe, li)
                pe_experts(pe, li)

        @block.scalar
        def _(act):
            act.wait_ge(s_("ones_set"), 1)
            for li in range(2):
                if li:
                    act.wait_ge(s_("ones_set"), 2)
                act_attention(act, li)
                act_experts(act, li)

            def step(s, m, on_):
                if 1 in on_:
                    b = s - 1
                    wait_apart(act, "c_x", b + B + 1)
                    nc.scalar.dma_start(out[ds(b, 1), :, :].rearrange("a (c p) d -> p (a c) d", p=P),
                                        x[:, tok(b), :]).then_inc(s_("out_w"), 16)
            last_steps(act, step)

        @block.gpsimd
        def _(pool):
            pool_fill(pool, LAYERS[0])
            pool.wait_ge(s_("weights_in"), 16 * 8)
            pool.wait_ge(s_("consts_made"), 1)
            for li in range(2):
                pool_attention(pool, li)
                pool_experts(pool, li)

            def step(s, m, on_):
                if 0 in on_:
                    pool_sum(pool, s, m % RING, 1)
                    pool_rstd(pool, CN, "c", s + B + 1, m % RING)
                if 1 in on_:
                    pool_scale(pool, s - 1, (m - 1) % RING, 1)
            last_steps(pool, step)


def kernel(**inputs):
    import numpy as _np
    import concourse.bacc as _bacc
    from concourse import mybir as _mybir
    from concourse.bass_utils import run_bass_kernel_spmd as _run

    a = {k: _np.ascontiguousarray(v) for k, v in inputs.items()}
    D = P

    def by_row(w, H):
        return w.reshape(D, H, D // H).transpose(0, 2, 1).reshape(D, D)

    HA, HB = LAYERS[0]["H"], LAYERS[1]["H"]
    wqkv = a["L0_attn_a_w_qkv"]
    dirs = _np.array([[(i >> 2 & 1) * 2 - 1, (i >> 1 & 1) * 2 - 1, (i & 1) * 2 - 1] for i in range(HA)],
                     dtype=_np.float32) / _np.sqrt(3.0, dtype=_np.float32)
    consts = _np.zeros((5, P, P), _np.float32)
    i = _np.arange(P)
    consts[0] = _np.eye(P, dtype=_np.float32)
    consts[1] = _np.where(i[None, :] > i[:, None], MASKED, 0.0)
    consts[2] = _np.where(i[None, :] < i[:, None], MASKED, 0.0)
    consts[3] = _np.where(i[:, None] < i[None, :], 1.0, 0.0)
    for h in range(HA):
        for r1 in range(3):
            for r2 in range(3):
                consts[4][r1 * HA + h, r2 * HA + h] = dirs[h, r1] * dirs[h, r2]
    counts = _np.zeros((P, 2 * E + NJ), _np.float32)
    counts[:, 0:E] = _np.arange(E)
    counts[:, E:2 * E] = _np.arange(E) * REGION
    counts[:, 2 * E:] = _np.arange(NJ)
    token = _np.arange(NT)[None, :, None] * P + i[:, None, None]
    ids = (token + _np.arange(2)[None, None, :] * B * T).astype(_np.int32).reshape(P, NT * 2)
    pads = _np.zeros(((E + SPARE) * TILE, ROW), _np.float32)
    pads.view(_np.int32)[:, P] = PAIRS + _np.arange((E + SPARE) * TILE)
    w1 = a["L0_ffn_W1"].transpose(0, 2, 1)
    w2 = a["L0_ffn_W2"].transpose(0, 2, 1).reshape(E, FC, P, D).transpose(0, 2, 1, 3).reshape(E, P, FC * D)
    b1 = a["L0_ffn_b1"].reshape(E, FC, P).transpose(0, 2, 1)
    b2 = a["L0_ffn_b2"].reshape(E, D, 1)
    arrays = {
        "x_in": a["L0_attn_a_x"],
        "w_a": _np.concatenate([by_row(wqkv[:, D:2 * D], HA), wqkv[:, 2 * D:]], axis=1),
        "w_o": a["L0_attn_a_w_out"],
        "wq_t": by_row(wqkv[:, 0:D], HA).T,
        "w_b": _np.concatenate([by_row(a["L0_attn_b_Wq"].T, HB), by_row(a["L0_attn_b_Wk"].T, HB),
                                a["L0_attn_b_Wv"].T], axis=1),
        "hs_in": _np.tile(a["L0_attn_a_head_scales"], D // HA).reshape(D, 1),
        "wr": a["L0_ffn_Wr"].T,
        "br": _np.broadcast_to(a["L0_ffn_br"], (P, E)),
        "wall": _np.concatenate([w1, w2, b1, b2], axis=2),
        "gamma": _np.broadcast_to(a["L0_ffn_gamma"], (P, D)),
        "beta": _np.broadcast_to(a["L0_ffn_beta"], (P, D)),
        "consts": consts, "counts": counts, "id_in": ids, "pads": pads,
    }
    nc = _bacc.Bacc("TRN2", target_bir_lowering=False, num_devices=1)
    aps, given = {}, {}
    for name, array in arrays.items():
        array = _np.ascontiguousarray(array)
        given["in_" + name] = array
        aps[name] = nc.dram_tensor("in_" + name, array.shape, _mybir.dt.from_np(array.dtype),
                                   kind="ExternalInput").ap()
    out = nc.dram_tensor("out_x", (B, T, D), F32, kind="ExternalOutput").ap()
    build(nc, out=out, **aps)
    res = _run(nc, [given], core_ids=[0])
    return res.results[0]["out_x"]
```

```python
from contextlib import ExitStack

import numpy as np

import concourse.bass as bass
from concourse import mybir

F32 = mybir.dt.float32
BF16 = mybir.dt.bfloat16
I32 = mybir.dt.int32
U32 = mybir.dt.uint32
ACT = mybir.ActivationFunctionType
ALU = mybir.AluOpType
AX = mybir.AxisListType

P = 128
B = 16
T = 256
QC = T // P
NT = B * QC
F = 512
FC = F // P
E = 8
TILE = 256
NJ = (2 * B * T + E * (TILE - 1)) // TILE
SLOTS = 3
WCOLS = F + FC * P + FC + P
EPS = 1e-5
MASKED = -1.0e30
PIPE = 8
RING = 3
REGION = B * T + TILE
SPARE = NJ - 2 * B * T // TILE
ROW = P + 2
PAIRS = 2 * B * T
COMBINE, NORM, PROJECT, STACK, MAXIMA, EXPS, LAST = range(7)
OUTPUT, ROUTE, SEND = (7, 6), (8, 7), 8
STAGES = 9
FIRST = 3
STAGES_OF = (PIPE, PIPE + 1)
assert NJ % SLOTS == 0
BANK = [dict(mxT=0, oT=1, lnT=0, tT=0, qk=1, lg=0, v=0, onT=0, pr=0, rank=0),
        dict(mxT=0, lnT=0, v=0, qk=1, tT=0, lg=0, oT=0, oT2=1, rank=1)]

LAYERS = [
    dict(H=8, hd=16, causal=True, products=6, ones=96, groups=2,
         stack=[(0, 0, 2, 1, 2), (1, 0, 1, 1, 2), (1, 1, 1, 1, 2), (0, 0, 2, 2, 1), (1, 2, 1, 1, 1),
                (1, 0, 1, 1, 1)]),
    dict(H=16, hd=8, causal=False, products=9, ones=64, groups=4,
         stack=[(0, 0, 3, 1, 3), (1, 0, 1, 1, 3), (1, 1, 1, 1, 3), (1, 2, 1, 1, 3)]),
]
for _l in LAYERS:
    _l["rows"] = _l["products"] * _l["hd"]
    _l["banks"] = 3 if _l["causal"] else 4


class At:

    def __init__(self, i, a, c):
        self.i, self.a, self.c = i, a, c

    def __add__(self, n):
        return At(self.i, self.a, self.c + n)

    def __sub__(self, n):
        return At(self.i, self.a, self.c - n)

    def __mul__(self, n):
        return At(self.i, self.a * n, self.c * n)

    def __floordiv__(self, n):
        assert self.a % n == 0
        return At(self.i, self.a // n, self.c // n)

    __radd__, __rmul__ = __add__, __mul__


class Waiting:

    def __init__(self, engine, semaphore):
        self.engine, self.semaphore = engine, semaphore

    def wait_ge(self, name, n, apart=False):
        if isinstance(n, At):
            assert n.c >= 1, (name, n.a, n.c)
            n = val(n)
            if apart:
                n = self.engine.to_reg(n)
                self.engine.wait_ge(self.semaphore("consts_made"), 1)
            self.engine.wait_ge(self.semaphore(name), n)
        elif n > 0:
            self.engine.wait_ge(self.semaphore(name), n)


def val(n):
    if not isinstance(n, At):
        return n
    return n.i * n.a + n.c if n.c else n.i * n.a


def ds(n, size):
    return bass.ds(val(n), size)


def score_banks(layer, g):
    heads = [4 * g + j for j in range(4)]
    if layer["causal"]:
        return [("wide", heads[0:2]), ("wide", heads[2:4]), ("narrow", heads)]
    return [(c, heads[2 * i:2 * i + 2]) for c in range(QC) for i in range(2)]


def build(nc, x_in, w_a, w_o, wq_t, w_b, hs_in, wr, br, wall, gamma, beta, consts, counts, id_in, pads, out):
    with ExitStack() as ctx:
        def sb(name, shape, dt=F32):
            return ctx.enter_context(nc.sbuf_tensor(name, shape, dt))

        def pb(name):
            return ctx.enter_context(nc.psum_tensor(name, [P, 512], F32))

        scr = [nc.dram_tensor(f"scr{i}", (2, 3, P, T), BF16).ap() for i in range(RING)]
        xs = nc.dram_tensor("xs", (E * REGION + SPARE * TILE, ROW), F32).ap()
        ys = nc.dram_tensor("ys", (PAIRS + (E + SPARE) * TILE, P), F32).ap()

        x = sb("x", [P, NT, P])
        t = sb("t", [P, NT, P])
        cst = sb("cst", [P, 5, P])
        cnt = sb("cnt", [P, 2 * E + NJ])
        identb = sb("identb", [P, P], BF16)
        halfm = sb("halfm", [P, 2, QC])
        minusb = sb("minusb", [P, P], BF16)
        maskm_w = sb("maskm_w", [P, 2, 2, P], BF16)
        maskm_n = sb("maskm_n", [P, 4, P], BF16)
        maske_w = sb("maske_w", [P, 2, 2, P], BF16)
        maske_n = sb("maske_n", [P, 4, P], BF16)
        earlier = sb("earlier", [P, P], BF16)
        onesb = sb("onesb", [P, P], BF16)
        ids = sb("ids", [P, NT, 2], I32)
        wqkv = [sb(f"wqkv{i}", [P, 3, P]) for i in range(2)]
        wo = sb("wo", [P, P])
        wqt = sb("wqt", [P, P])
        hs = sb("hs_sb", [P, 1])
        geo = sb("geo", [P, P])
        wrs = sb("wrs", [P, E])
        brs = sb("brs", [P, QC, E])
        gam = sb("gam", [P, QC, P])
        bet = sb("bet", [P, QC, P])
        ident, iota8, iotaj = cst[:, 0, :], cnt[:, 0:E], cnt[:, 2 * E:2 * E + NJ]
        first_row = cnt[:, E:2 * E]

        ln = sb("ln", [P, RING, QC, P])
        stats = sb("stats", [P, 3, QC, 6])
        mv = sb("mv", [P, 3, RING, QC, 2])
        rstd = sb("rstd", [P, 3, RING, QC, 2])
        lnT = sb("lnT", [P, RING, T])
        parts = sb("parts", [P, RING, 2, 3, T], BF16)
        vaug = sb("vaug", [P, RING, QC, 16, 32])
        qst = sb("qst", [P, RING, 16, T], BF16)
        kst = sb("kst", [P, RING, 16, T], BF16)
        mx = sb("mx", [P, RING, 32])
        mparts = sb("mparts", [32, RING, 2, P], BF16)
        prob = sb("prob", [P, 2, 4, 512])
        oT = sb("oT", [P, RING, 4, T])
        rden = sb("rden", [P, QC, 16])
        on = sb("on", [P, RING, QC, P])
        onT = sb("onT", [P, RING, T])
        row = sb("row", [P, RING, QC, 2, ROW])
        tT = sb("tT", [P, RING, T])
        lg = sb("lg", [P, RING, QC, E])
        mx8 = sb("mx8", [P, RING, QC, 8])
        ix8 = sb("ix8", [P, RING, QC, 8], U32)
        ixf = sb("ixf", [P, QC, 2])
        oh = sb("oh", [P, QC, 2, E])
        ohb = sb("ohb", [P, RING, QC, E], BF16)
        place = sb("place", [P, QC, E])
        pick = sb("pick", [P, QC, 2, E])
        placed = sb("placed", [P, QC, 2])
        index = sb("index", [P, RING, QC, 2], U32)
        run = sb("run", [P, E])
        dv = sb("dv", [P, RING, 3, QC])
        ct = sb("ct", [P, E])
        ct_i = sb("ct_i", [P, E], I32)
        ct_s = sb("ct_s", [P, E], I32)
        tiles = sb("tiles", [P, E])
        upto = [sb(f"upto{i}", [P, E]) for i in range(2)]
        skip = sb("skip", [P, E])
        past = sb("past", [P, NJ, E])
        skipped = sb("skipped", [P, NJ, E])
        t_exp = sb("t_exp", [P, NJ])
        t_row = sb("t_row", [P, NJ])
        t_exp_i = sb("t_exp_i", [P, NJ], I32)
        t_row_i = sb("t_row_i", [P, NJ], I32)
        pad_row = sb("pad_row", [P, E], I32)
        wsl = sb("wsl", [P, SLOTS, WCOLS])
        xt = sb("xt", [P, SLOTS, QC, ROW])
        idw = sb("idw", [P, SLOTS, QC, 2])
        xT = prob[:, 1, :, :].rearrange("p k (a t) -> p (k a) t", a=2)[:, 0:SLOTS, :]
        hT = prob[:, 0, 0:FC // 2, :].rearrange("p k (a t) -> p (k a) t", a=2)
        ysum = sb("ysum", [P, SLOTS, QC, P])
        yt = sb("yt", [P, SLOTS, QC, P])
        yg = sb("yg", [P, RING, 2, QC, P])
        r = sb("r", [P, RING, QC, P])

        pS = [pb("score0"), pb("score1")]
        pM = [pb("max0"), pb("max1")]
        pO = [pb("attn0"), pb("attn1")]
        pX = [pb("misc0"), pb("misc1")]
        pH = [pS[0], pS[1], pM[0], pM[1]]
        pXT, pY = pO[0], pO[1]

        sems = {}

        def s_(name):
            if name not in sems:
                sems[name] = ctx.enter_context(nc.semaphore(name))
            return sems[name]

        for name in """consts_in x_in proj_in weights_in bf_made consts_made filled wq_ps wq_made ones_set spare_in
            c_sum c_add c_stats1 c_stats c_eps c_rstd c_bias c_norm c_gam c_bet c_x
            n_stats1 n_stats n_eps n_rstd n_bias ln_ready lnT_ps lnT_sb qk_ps part1 less1 part2 less2 part3 v_ps v_sb
            max_ps max_read mxT_ps m_hi m_lo exp_ps exp_done av_done o_sb oT_ps rden_done on_done onT_ps onT_sb
            pr_ps x_ready t_stats1 t_stats t_eps t_rstd t_bias t_ready tT_ps tT_sb lg_ps lg_done mx8_done ix8_done
            ixf_done diff e_done oh_done ohb_done den_done w0_done w1_done rank_ps place_done rank_read pick_done
            placed_done index_done id_done chain tiles_known pads_in xT_ps xT_sb idw_done h_ps h_act h_dve y_ps
            ysum_sb yt_sb out_w""".split():
            s_(name)
        for name in "y_in scr_w st_in m_in t_cp scat w_in xt_in y_out".split():
            for i in range(RING):
                s_(f"{name}{i}")
        block = ctx.enter_context(nc.Block())

        def steps(eng, stages, step):
            for s in range(stages):
                step(s, s, [k for k in range(stages) if 0 <= s - k < B])
            with eng.engine.Fori(0, (B - stages) // RING) as i:
                for u in range(RING):
                    step(At(i, RING, stages + u), stages + u, list(range(stages)))
            for s in range(after_loop(stages), B + stages - 1):
                step(s, s, [k for k in range(stages) if 0 <= s - k < B])

        def after_loop(stages):
            return B - (B - stages) % RING

        def attention_steps(eng, li, step):
            early = 1 - li
            steps(eng, STAGES_OF[li], lambda s, m, on_: step(s + early, m + early, [k + early for k in on_]))

        def nth(b, slot, li):
            return (b - slot) // RING + 1 + li * len(range(slot, B, RING))

        def sent(b, slot, li):
            return nth(b, slot, li) * 64

        def tok(b):
            return ds(b * QC, QC)

        def tile_of(a, b, c):
            return a[:, ds(b * QC + c, 1), :].rearrange("p a d -> p (a d)")

        CN, LN, TN = 0, 1, 2

        def dve_stats(src, which, slot):
            for c in range(QC):
                ins = nc.vector.bn_stats(stats[:, which, c, :], src(c))
            return ins

        def dve_mean_var(which, slot):
            for c in range(QC):
                ins = nc.vector.bn_aggr(mv[:, which, slot, c, :], stats[:, which, c, :])
            return ins

        def dve_eps(dve, which, pre, v, slot):
            dve.wait_ge(pre + "_stats", v)
            nc.vector.tensor_scalar(rstd[:, which, slot, :, 0], mv[:, which, slot, :, 1], EPS, None, ALU.add)\
                .then_inc(s_(pre + "_eps"), 1)

        def pool_rstd(pool, which, pre, v, slot):
            pool.wait_ge(pre + "_eps", v)
            half = halfm[:, which, :] if isinstance(which, slice) else halfm[:, 0, :]
            nc.gpsimd.tensor_tensor(rstd[:, which, slot, :, 1], rstd[:, which, slot, :, 0], half, ALU.pow)\
                .then_inc(s_(pre + "_rstd"), 1)

        def dve_bias(dve, which, pre, v, slot):
            dve.wait_ge(pre + "_rstd", v)
            nc.vector.scalar_tensor_tensor(out=rstd[:, which, slot, :, 0], in0=mv[:, which, slot, :, 0], scalar=-1.0,
                                           in1=rstd[:, which, slot, :, 1], op0=ALU.mult, op1=ALU.mult)\
                .then_inc(s_(pre + "_bias"), 1)

        def act_normalise(act, src, dst, which, pre, v, slot):
            act.wait_ge(pre + "_bias", v)
            for c in range(QC):
                ins = nc.scalar.activation(dst(c), src(c), ACT.Identity, bias=rstd[:, which, slot, c, 0:1],
                                           scale=rstd[:, which, slot, c, 1:2])
            return ins

        def sp_results(sp, b, slot, li):
            sp.wait_ge("c_add", B * li + b + 1 - RING, apart=True)
            for k in range(2):
                src = ys[ds(b * T + k * B * T, T), :].rearrange("(c p) d -> p c d", p=P)
                nc.sync.dma_start(yg[:, slot, k, :, :], src).then_inc(s_(f"y_in{slot}"), 16)

        def pool_sum(pool, b, slot, li):
            pool.wait_ge(f"y_in{slot}", nth(b, slot, li) * 32)
            nc.gpsimd.tensor_tensor(yg[:, slot, 0, :, :], yg[:, slot, 0, :, :], yg[:, slot, 1, :, :], ALU.add)\
                .then_inc(s_("c_sum"), 1)

        def add_input(eng, ops, b, slot, li):
            v = B * li + b + 1
            eng.wait_ge("c_sum", v)
            eng.wait_ge("c_x", v - RING)
            ops.tensor_tensor(r[:, slot, :, :], yg[:, slot, 0, :, :], t[:, tok(b), :], ALU.add)\
                .then_inc(s_("c_add"), 1)

        def normalise(eng, ops, b, slot):
            eng.wait_ge("n_rstd", B + b + 1, apart=True)
            for c in range(QC):
                ins = ops.tensor_scalar(r[:, slot, c, :], r[:, slot, c, :], mv[:, CN, slot, c, 0:1],
                                        rstd[:, CN, slot, c, 1:2], ALU.subtract, ALU.mult)
            ins.then_inc(s_("c_norm"), 1)

        def early(li, s, on_):
            return li and COMBINE in on_ and MAXIMA not in on_

        def scale(eng, ops, b, slot, li):
            eng.wait_ge("c_norm", B * li + b + 1)
            ops.tensor_tensor(r[:, slot, :, :], r[:, slot, :, :], gam[:, :, :], ALU.mult)\
                .then_inc(s_("c_gam"), 1)

        def shift_and_add(eng, ops, b, slot, li):
            v = B * li + b + 1
            eng.wait_ge("c_gam", v)
            ops.tensor_tensor(r[:, slot, :, :], r[:, slot, :, :], bet[:, :, :], ALU.add).then_inc(s_("c_bet"), 1)
            eng.wait_ge("c_bet", v)
            ops.tensor_tensor(x[:, tok(b), :], x[:, tok(b), :], r[:, slot, :, :], ALU.add).then_inc(s_("c_x"), 1)

        def counts_of(li):
            L0 = LAYERS[0]
            return B * L0["groups"] * L0["banks"] * li, B * L0["groups"] * li, 2 * B * li

        def names(li, s, m):
            b = [s - k for k in range(STAGES)]
            return b, [(m - k) % RING for k in range(STAGES)], [n + (B * li + 1) for n in b]

        def both_norms(li, b, V, on_):
            which = ([CN] if COMBINE in on_ and li else []) + ([LN] if NORM in on_ else [])
            return which and slice(which[0], which[-1] + 1), V[0] if li else V[1]

        def misc(li, name, n, rows=P, at=0):
            return pX[BANK[li][name]][0:rows, at:at + n]

        def act_attention(act, li):
            L = LAYERS[li]
            H, hd, G, NB = L["H"], L["hd"], L["groups"], L["banks"]
            e0, g0, o0 = counts_of(li)
            OUT, RTE = OUTPUT[li], ROUTE[li]

            def step(s, m, on_):
                b, sl, V = names(li, s, m)

                def exp(st, g, k):
                    if st not in on_:
                        return
                    if k == 0:
                        act.wait_ge("av_done", g0 + b[st] * G + g - 1)
                    act.wait_ge("exp_ps", e0 + (b[st] * G + g) * NB + k + 1)
                    nc.scalar.activation(prob[:, g % 2, k, :], pS[(g * NB + k) % 2][:, :], ACT.Exp)\
                        .then_inc(s_("exp_done"), 1)

                def results(st, half):
                    if st not in on_:
                        return
                    n = G // 2
                    act.wait_ge("av_done", g0 + b[st] * G + (half + 1) * n)
                    nc.scalar.copy(oT[:, sl[st], half * n:half * n + n, :],
                                   pO[half][:, 0:n * T].rearrange("p (a t) -> p a t", a=n)).then_inc(s_("o_sb"), 1)

                def part(i):
                    if PROJECT not in on_:
                        return
                    act.wait_ge(("qk_ps", "less1", "less2")[i], V[2])
                    if i == 0:
                        act.wait_ge(f"scr_w{sl[2]}", 16 * nth(b[2], sl[2], li) - 16)
                    nc.scalar.copy(parts[:, sl[2], :, i, :],
                                   misc(li, "qk", 2 * T).rearrange("p (a t) -> p a t", a=2))\
                        .then_inc(s_(f"part{i + 1}"), 1)

                def values():
                    if MAXIMA in on_:
                        act.wait_ge("v_ps", V[4])
                        nc.scalar.copy(vaug[:, sl[4], :, 0:H, 0:hd],
                                       misc(li, "v", T).rearrange("p (c h d) -> p c h d", c=QC, d=hd))\
                            .then_inc(s_("v_sb"), 1)

                def ln_columns():
                    if PROJECT in on_:
                        act.wait_ge("lnT_ps", V[2])
                        act.wait_ge("v_ps", V[2] - RING)
                        nc.scalar.copy(lnT[:, sl[2], :], misc(li, "lnT", T)).then_inc(s_("lnT_sb"), 1)

                def experts_input():
                    if RTE in on_:
                        act.wait_ge("id_done", V[RTE] - 1)
                        act_normalise(act, lambda c: tile_of(x, b[RTE], c), lambda c: row[:, sl[RTE], c, 0, 0:P],
                                      TN, "t", V[RTE], sl[RTE]).then_inc(s_("t_ready"), 1)

                def input_columns():
                    if RTE in on_:
                        act.wait_ge("tT_ps", V[RTE])
                        nc.scalar.copy(tT[:, sl[RTE], :], misc(li, "tT", T)).then_inc(s_("tT_sb"), 1)

                def norm():
                    if NORM in on_:
                        act.wait_ge("lnT_ps", V[1] - RING)
                        act_normalise(act, lambda c: tile_of(x, b[1], c), lambda c: ln[:, sl[1], c, :], LN, "n",
                                      V[1], sl[0]).then_inc(s_("ln_ready"), 1)

                def choice():
                    if RTE in on_:
                        act.wait_ge("diff", V[RTE])
                        nc.scalar.activation(dv[:, sl[RTE], 1, :], dv[:, sl[RTE], 0, :], ACT.Exp)\
                            .then_inc(s_("e_done"), 1)

                if li == 0:
                    exp(LAST, 1, 0)
                    experts_input()
                    exp(LAST, 1, 1)
                    exp(LAST, 1, 2)
                    ln_columns()
                    results(LAST, 0)
                    exp(EXPS, 0, 0)
                    input_columns()
                    part(0)
                    exp(EXPS, 0, 1)
                    values()
                    if OUT in on_:
                        act.wait_ge("onT_ps", V[OUT])
                        nc.scalar.copy(onT[:, sl[OUT], :], misc(li, "onT", T)).then_inc(s_("onT_sb"), 1)
                    part(1)
                    exp(EXPS, 0, 2)
                    results(LAST, 1)
                    part(2)
                    norm()
                    choice()
                else:
                    results(LAST, 0)
                    exp(LAST, 3, 0)
                    exp(LAST, 3, 1)
                    ln_columns()
                    exp(LAST, 3, 2)
                    exp(LAST, 3, 3)
                    exp(EXPS, 0, 0)
                    part(0)
                    exp(EXPS, 0, 1)
                    experts_input()
                    values()
                    exp(EXPS, 0, 2)
                    part(1)
                    exp(EXPS, 0, 3)
                    input_columns()
                    results(LAST, 1)
                    exp(EXPS, 1, 0)
                    exp(EXPS, 1, 1)
                    part(2)
                    exp(EXPS, 1, 2)
                    exp(EXPS, 1, 3)
                    exp(EXPS, 2, 0)
                    choice()
                    exp(EXPS, 2, 1)
                    exp(EXPS, 2, 2)
                    exp(EXPS, 2, 3)
                    norm()
            attention_steps(act, li, step)

        def stacked(b, slot, li):
            n = [16 * len(L["stack"]) for L in LAYERS]
            return nth(b, slot, 0) * n[li] + len(range(slot, B, RING)) * li * n[0]

        def stack_source(slot, li, a, first, n, by, copies):
            L = LAYERS[li]
            src = scr[slot][a][first:first + (n - 1) * by + 1:by].rearrange("s (r h) t -> s r (h t)", h=L["H"])
            if copies == 1:
                return src
            return src.rearrange("s r n -> (s r) n").unsqueeze(0).to_broadcast([copies, n * L["hd"], L["H"] * T])

        def sp_attention(sp, li):
            L = LAYERS[li]
            H, hd, G, NB = L["H"], L["hd"], L["groups"], L["banks"]
            e0, g0, _ = counts_of(li)
            OUT, RTE = OUTPUT[li], ROUTE[li]

            def step(s, m, on_):
                b, sl, V = names(li, s, m)
                if COMBINE in on_:
                    sp_results(sp, b[0], sl[0], 0)
                if EXPS in on_:
                    for i, made in enumerate(("m_hi", "m_lo")):
                        sp.wait_ge(made, V[EXPS], apart=True)
                        nc.sync.dma_start(qst[L["rows"] + i:L["rows"] + i + 1, sl[EXPS], 0:H, :],
                                     mparts[0:2 * H, sl[EXPS], i, :]).then_inc(s_(f"m_in{sl[EXPS]}"), 16)
                if STACK in on_:
                    i3 = sl[3]
                    sp.wait_ge(f"scr_w{i3}", 16 * nth(b[3], i3, li), apart=True)
                    sp.wait_ge("exp_ps", e0 + (b[3] - RING + 1) * G * NB, apart=True)
                    if isinstance(s, int) and s < STACK + RING:
                        sp.wait_ge("ones_set", 1 + li)
                    at = [0, 0]
                    for a, first, n, by, copies in L["stack"]:
                        rows = n * copies * hd
                        dst = (qst, kst)[a][at[a]:at[a] + rows, i3, 0:H, :].rearrange("p h t -> p (h t)")
                        nc.sync.dma_start(dst, stack_source(i3, li, a, first, n, by, copies))\
                            .then_inc(s_(f"st_in{i3}"), 16)
                        at[a] += rows
                if RTE in on_:
                    sp.wait_ge("t_ready", V[RTE], apart=True)
                    nc.sync.dma_start(t[:, tok(b[RTE]), :], row[:, sl[RTE], :, 0, 0:P])\
                        .then_inc(s_(f"t_cp{sl[RTE]}"), 16)
                    nc.sync.dma_start(row[:, sl[RTE], :, 1, 0:P], row[:, sl[RTE], :, 0, 0:P])\
                        .then_inc(s_(f"t_cp{sl[RTE]}"), 16)
                if PROJECT in on_:
                    i2 = sl[2]
                    sp.wait_ge("part3", V[2], apart=True)
                    if not isinstance(s, int) or b[2] >= RING:
                        sp.wait_ge(f"st_in{i2}", stacked(b[2] - RING, i2, li), apart=True)
                    nc.sync.dma_start(scr[i2].rearrange("a s p t -> p (a s) t"),
                                 parts[:, i2, :, :, :].rearrange("p a s t -> p (a s) t"))\
                        .then_inc(s_(f"scr_w{i2}"), 16)
            attention_steps(sp, li, step)

        def pe_attention(pe, li):
            L = LAYERS[li]
            H, hd, G, NB, R = L["H"], L["hd"], L["groups"], L["banks"], L["rows"]
            e0, g0, o0 = counts_of(li)
            OUT, RTE = OUTPUT[li], ROUTE[li]
            def mask(dst, m):
                nc.tensor.matmul(dst, identb[:, :], m, start=True, stop=False, skip_group_check=True)

            def step(s, m, on_):
                b, sl, V = names(li, s, m)

                def count(k, back=0):
                    n = b[k] - back + (B * li + 1)
                    return min(n, B * (li + 1)) if isinstance(n, int) else n

                def exp_bank(st, g, k):
                    if st not in on_:
                        return
                    c, heads = score_banks(L, g)[k]
                    pe.wait_ge("exp_done", e0 + (b[st] * G + g) * NB + k - 1)
                    if k == 0 and g == 0:
                        pe.wait_ge(f"m_in{sl[st]}", nth(b[st], sl[st], li) * 32)
                    dst = pS[(g * NB + k) % 2]
                    if c == "wide":
                        mask(dst[:, :], maske_w[:, :, :, :].rearrange("p a b q -> p (a b q)"))
                        kc, q0, w = 0, 0, T
                    elif c == "narrow":
                        mask(dst[:, :], maske_n[:, :, :].rearrange("p a q -> p (a q)"))
                        kc, q0, w = 1, P, P
                    else:
                        kc, q0, w = c, 0, T
                    for i, h in enumerate(heads):
                        mm = nc.tensor.matmul(dst[:, i * w:(i + 1) * w],
                                              kst[0:R + 2, sl[st], h, kc * P:(kc + 1) * P],
                                              qst[0:R + 2, sl[st], h, q0:q0 + w],
                                              start=not L["causal"], stop=True, skip_group_check=True)
                    mm.then_inc(s_("exp_ps"), 1)

                def max_bank(g, k):
                    if MAXIMA not in on_:
                        return
                    c, heads = score_banks(L, g)[k]
                    pe.wait_ge("max_read", e0 + (b[4] * G + g) * NB + k - 1)
                    if k == 0 and g == 0:
                        pe.wait_ge(f"st_in{sl[4]}", stacked(b[4], sl[4], li))
                    dst = pM[(g * NB + k) % 2]
                    if c == "wide":
                        mask(dst[:, :], maskm_w[:, :, :, :].rearrange("p a b q -> p (a b q)"))
                        qc, w = 1, T
                    elif c == "narrow":
                        mask(dst[:, :], maskm_n[:, :, :].rearrange("p a q -> p (a q)"))
                        qc, w = 0, P
                    else:
                        qc, w = c, T
                    for i, h in enumerate(heads):
                        mm = nc.tensor.matmul(dst[:, i * w:(i + 1) * w], qst[0:R, sl[4], h, qc * P:(qc + 1) * P],
                                              kst[0:R, sl[4], h, 0:w],
                                              start=not L["causal"], stop=True, skip_group_check=True)
                    mm.then_inc(s_("max_ps"), 1)

                def banks(g, k):
                    max_bank(g, k)
                    if g == 0:
                        exp_bank(LAST, G - 1, k)
                    else:
                        exp_bank(EXPS, g - 1, k)

                def weigh(st, g, kc):
                    if st not in on_:
                        return
                    bank, lo = (g, 0) if G == 2 else (g // 2, g % 2 * T)
                    if kc == 0:
                        pe.wait_ge("exp_done", e0 + (b[st] * G + g + 1) * NB)
                        if g == 0:
                            pe.wait_ge("v_sb", V[st])
                        if lo == 0:
                            pe.wait_ge("o_sb", o0 + (b[st] - 1) * 2 + bank + 1)
                    for j in range(4):
                        at, src = lo, prob[:, g % 2]
                        if not L["causal"]:
                            rhs = src[:, 2 * kc + j // 2, (j % 2) * T:(j % 2 + 1) * T]
                        elif kc == 0:
                            rhs = src[:, j // 2, (j % 2) * T:(j % 2 + 1) * T]
                        else:
                            rhs, at = src[:, 2, j * P:(j + 1) * P], lo + P
                        mm = nc.tensor.matmul(pO[bank][32 * j:32 * j + 32, at:lo + T],
                                              vaug[:, sl[st], kc, 4 * g + j, :], rhs,
                                              start=(kc == 0), stop=(kc == QC - 1), skip_group_check=True)
                    if kc == QC - 1:
                        mm.then_inc(s_("av_done"), 1)

                def transposes(name, src):
                    for c in range(QC):
                        tr = nc.tensor.transpose(misc(li, name, P, at=c * P), src(c), ident)
                    return tr

                def ln_columns():
                    pe.wait_ge("m_lo", count(EXPS))
                    if PROJECT in on_:
                        pe.wait_ge("ln_ready", V[2])
                        transposes("lnT", lambda c: ln[:, sl[2], c, :]).then_inc(s_("lnT_ps"), 1)

                def input_columns():
                    if li:
                        pe.wait_ge("v_sb", count(4))
                    else:
                        pe.wait_ge("lnT_sb", count(2))
                    if RTE in on_:
                        pe.wait_ge("t_ready", V[RTE])
                        transposes("tT", lambda c: row[:, sl[RTE], c, 0, 0:P]).then_inc(s_("tT_ps"), 1)

                def queries_keys():
                    if li:
                        pe.wait_ge("rank_read", count(RTE, 1))
                    else:
                        pe.wait_ge("on_done", count(OUT))
                    if PROJECT in on_:
                        pe.wait_ge("lnT_sb", V[2])
                        for a in range(2):
                            mm = nc.tensor.matmul(misc(li, "qk", 2 * T)[:, a * T:(a + 1) * T], wqkv[li][:, a, :],
                                                  lnT[:, sl[2], :], start=(a == 0), stop=False,
                                                  skip_group_check=True)
                        mm.then_inc(s_("qk_ps"), 1)

                def less(i):
                    if PROJECT in on_:
                        pe.wait_ge(f"part{i}", V[2])
                        nc.tensor.matmul(misc(li, "qk", 2 * T), minusb[:, :], parts[:, sl[2], :, i - 1, :],
                                         start=False, stop=True, skip_group_check=True).then_inc(s_(f"less{i}"), 1)

                def values():
                    if li:
                        pe.wait_ge("lnT_sb", count(2))
                    else:
                        pe.wait_ge("lg_done", count(RTE))
                    if MAXIMA in on_:
                        pe.wait_ge("lnT_sb", V[4])
                        for c in range(QC):
                            mm = nc.tensor.matmul(misc(li, "v", P, at=c * P), lnT[:, sl[4], c * P:(c + 1) * P],
                                                  wqkv[li][:, 2, :], start=True, stop=True)
                        mm.then_inc(s_("v_ps"), 1)

                def logits():
                    pe.wait_ge("tT_sb", count(RTE))
                    if RTE in on_:
                        pe.wait_ge("tT_sb", V[RTE])
                        for c in range(QC):
                            mm = nc.tensor.matmul(misc(li, "lg", E, at=c * E), tT[:, sl[RTE], c * P:(c + 1) * P],
                                                  wrs[:, :], start=True, stop=True)
                        mm.then_inc(s_("lg_ps"), 1)

                def tokens_back(c):
                    if not li:
                        pe.wait_ge("part3", count(2, 1))
                    elif c:
                        pe.wait_ge("part3", count(2))
                    else:
                        pe.wait_ge("lg_done", count(RTE))
                    if OUT in on_:
                        name = "oT2" if c else "oT"
                        pe.wait_ge("o_sb", o0 + (b[OUT] + 1) * 2)
                        at = 0
                        for cc in range(QC) if c is None else [c]:
                            for g in range(G):
                                tr = nc.tensor.transpose(misc(li, name, P, at=at), oT[:, sl[OUT], g, cc * P:(cc + 1) * P],
                                                         ident)
                                at += P
                        tr.then_inc(s_("oT_ps"), 1)

                def maxima_rows():
                    if li:
                        pe.wait_ge("on_done", 2 * count(OUT, 1) - (B + 1))
                    else:
                        pe.wait_ge("rank_read", count(RTE, 1))
                    if EXPS in on_:
                        pe.wait_ge("max_read", e0 + (b[EXPS] + 1) * G * NB)
                        nc.tensor.transpose(misc(li, "mxT", P, rows=2 * H), mx[:, sl[EXPS], 0:2 * H], ident)\
                            .then_inc(s_("mxT_ps"), 1)

                def ranks():
                    if li:
                        pe.wait_ge("on_done", 2 * count(OUT) - B)
                    else:
                        pe.wait_ge("x_ready", count(OUT))
                    if RTE not in on_:
                        return
                    pe.wait_ge("ohb_done", V[RTE])
                    o = ohb[:, sl[RTE], :, :]
                    nc.tensor.matmul(misc(li, "rank", QC * E), earlier[:, :], o.rearrange("p c e -> p (c e)"),
                                     start=True, stop=False, skip_group_check=True)
                    nc.tensor.matmul(misc(li, "rank", E, at=E), onesb[:, :], o[:, 0, :],
                                     start=False, stop=False, skip_group_check=True)
                    for c in range(QC):
                        mm = nc.tensor.matmul(misc(li, "rank", E, at=QC * E), onesb[:, :], o[:, c, :],
                                              start=False, stop=(c == QC - 1), skip_group_check=True)
                    mm.then_inc(s_("rank_ps"), 1)

                if li == 0:
                    banks(0, 0)
                    tokens_back(None)
                    maxima_rows()
                    banks(0, 1)
                    weigh(LAST, 0, 0)
                    ln_columns()
                    banks(0, 2)
                    weigh(LAST, 0, 1)
                    max_bank(1, 0)
                    input_columns()
                    exp_bank(EXPS, 0, 0)
                    queries_keys()
                    weigh(LAST, 1, 0)
                    logits()
                    banks(1, 1)
                    values()
                    less(1)
                    weigh(LAST, 1, 1)
                    pe.wait_ge("v_sb", count(4))
                    if OUT in on_:
                        pe.wait_ge("on_done", V[OUT])
                        transposes("onT", lambda c: on[:, sl[OUT], c, :]).then_inc(s_("onT_ps"), 1)
                    banks(1, 2)
                    if OUT in on_:
                        if isinstance(s, int):
                            pe.wait_ge("weights_in", 16 * 6)
                        pe.wait_ge("onT_sb", V[OUT])
                        for c in range(QC):
                            mm = nc.tensor.matmul(misc(li, "pr", P, at=c * P), onT[:, sl[OUT], c * P:(c + 1) * P],
                                                  wo[:, :], start=True, stop=True)
                        mm.then_inc(s_("pr_ps"), 1)
                    less(2)
                    ranks()
                else:
                    banks(0, 0)
                    maxima_rows()
                    banks(0, 1)
                    weigh(LAST, 2, 0)
                    banks(0, 2)
                    ln_columns()
                    banks(0, 3)
                    weigh(LAST, 2, 1)
                    max_bank(1, 0)
                    queries_keys()
                    exp_bank(EXPS, 0, 0)
                    banks(1, 1)
                    values()
                    weigh(LAST, 3, 0)
                    banks(1, 2)
                    less(1)
                    banks(1, 3)
                    input_columns()
                    weigh(LAST, 3, 1)
                    banks(2, 0)
                    weigh(EXPS, 0, 0)
                    logits()
                    banks(2, 1)
                    less(2)
                    tokens_back(0)
                    banks(2, 2)
                    weigh(EXPS, 0, 1)
                    banks(2, 3)
                    banks(3, 0)
                    tokens_back(1)
                    banks(3, 1)
                    weigh(EXPS, 1, 0)
                    banks(3, 2)
                    banks(3, 3)
                    weigh(EXPS, 1, 1)
                    ranks()
            attention_steps(pe, li, step)

        def dve_attention(dve, li):
            L = LAYERS[li]
            H, hd, G, NB = L["H"], L["hd"], L["groups"], L["banks"]
            e0, _, _ = counts_of(li)
            OUT, RTE = OUTPUT[li], ROUTE[li]
            TNS = (OUT, RTE)[li]

            def step(s, m, on_):
                b, sl, V = names(li, s, m)

                def maxima(g, k):
                    if MAXIMA not in on_:
                        return
                    c, heads = score_banks(L, g)[k]
                    dve.wait_ge("max_ps", e0 + (b[4] * G + g) * NB + k + 1)
                    qc = {"wide": 1, "narrow": 0}.get(c, c)
                    a, n = 2 * heads[0] + qc, len(heads)
                    nc.vector.tensor_reduce(mx[:, sl[4], a:a + 2 * n - 1:2],
                                            pM[(g * NB + k) % 2][:, :].rearrange("p (h w) -> p h w", h=n),
                                            axis=AX.X, op=ALU.max).then_inc(s_("max_read"), 1)

                def norms(i):
                    which, v = both_norms(li, b, V, on_)
                    if not which:
                        return
                    slot = sl[0]
                    if i == -1 and NORM in on_:
                        if li:
                            dve.wait_ge("c_x", V[1] - B, apart=True)
                        else:
                            first = isinstance(s, int) and b[1] < FIRST
                            dve.wait_ge("x_in", 16 if first else 32, apart=True)
                        ins = dve_stats(lambda c: tile_of(x, b[1], c), LN, slot)
                        if not (COMBINE in on_ and li):
                            ins.then_inc(s_("n_stats1"), 1)
                    elif i == -1:
                        return
                    elif i == 0:
                        if COMBINE in on_ and li:
                            dve.wait_ge("c_add", b[0] + 1, apart=True)
                            dve_stats(lambda c: r[:, sl[0], c, :], CN, slot).then_inc(s_("n_stats1"), 1)
                    elif i == 1:
                        dve.wait_ge("n_stats1", v, apart=True)
                        for w in range(which.start, which.stop):
                            ins = dve_mean_var(w, slot)
                        ins.then_inc(s_("n_stats"), 1)
                    elif i == 2:
                        dve_eps(dve, which, "n", v, slot)
                    elif NORM in on_:
                        dve_bias(dve, LN, "n", v, slot)

                def normed(i):
                    if OUT not in on_:
                        return
                    v = B * li + b[OUT] * (1 + li) + i + 1
                    dve.wait_ge("oT_ps", v)
                    src = misc(li, "oT2" if i else "oT", 2 * T).rearrange("p (n w) -> p n w", w=32)
                    n = src.shape[1]
                    den = rden[:, :, :].rearrange("p c h -> p (c h)")[:, i * 16:i * 16 + n]
                    dst = on[:, sl[OUT], :, :].rearrange("p c d -> p (c d)")[:, i * P:i * P + n * hd]
                    nc.vector.reciprocal(den, src[:, :, hd]).then_inc(s_("rden_done"), 1)
                    dve.wait_ge("rden_done", v)
                    nc.vector.tensor_tensor(dst.rearrange("p (n d) -> p n d", d=hd), src[:, :, 0:hd],
                                            den.unsqueeze(2).to_broadcast([P, n, hd]), ALU.mult)\
                        .then_inc(s_("on_done"), 1)

                def choose(i):
                    if RTE not in on_:
                        return
                    slot, v = sl[RTE], V[RTE]
                    if i == 0:
                        if li == 0 and isinstance(s, int):
                            dve.wait_ge("weights_in", 16 * 6)
                        dve.wait_ge("lg_ps", v)
                        nc.vector.tensor_tensor(lg[:, slot, :, :],
                                                misc(li, "lg", QC * E).rearrange("p (c e) -> p c e", c=QC),
                                                brs[:, :, :], ALU.add).then_inc(s_("lg_done"), 1)
                    elif i == 1:
                        dve.wait_ge("lg_done", v, apart=True)
                        for c in range(QC):
                            ins = nc.vector.max(mx8[:, slot, c, :], lg[:, slot, c, :])
                        ins.then_inc(s_("mx8_done"), 1)
                    elif i == 2:
                        dve.wait_ge("mx8_done", v, apart=True)
                        for c in range(QC):
                            ins = nc.vector.max_index(ix8[:, slot, c, :], mx8[:, slot, c, :], lg[:, slot, c, :])
                        ins.then_inc(s_("ix8_done"), 1)
                        nc.vector.tensor_tensor(dv[:, slot, 0, :], mx8[:, slot, :, 1], mx8[:, slot, :, 0],
                                                ALU.subtract).then_inc(s_("diff"), 1)
                    elif i == 3:
                        dve.wait_ge("ix8_done", v)
                        nc.vector.tensor_copy(ixf[:, :, :], ix8[:, slot, :, 0:2]).then_inc(s_("ixf_done"), 1)
                    elif i == 4:
                        dve.wait_ge("ixf_done", v)
                        nc.vector.tensor_tensor(oh[:, :, :, :], ixf[:, :, :].unsqueeze(3).to_broadcast([P, QC, 2, E]),
                                                iota8.unsqueeze(1).unsqueeze(1).to_broadcast([P, QC, 2, E]),
                                                ALU.is_equal).then_inc(s_("oh_done"), 1)
                    else:
                        dve.wait_ge("oh_done", v)
                        nc.vector.tensor_tensor(ohb[:, slot, :, :], oh[:, :, 0, :], oh[:, :, 1, :], ALU.add)\
                            .then_inc(s_("ohb_done"), 1)

                def send_to(i):
                    if RTE not in on_:
                        return
                    slot, v = sl[RTE], V[RTE]
                    if i == 0:
                        dve.wait_ge("e_done", v)
                        nc.vector.tensor_scalar(dv[:, slot, 2, :], dv[:, slot, 1, :], 1.0, None, ALU.add)\
                            .then_inc(s_("den_done"), 1)
                        dve.wait_ge("rank_ps", v)
                        nc.vector.tensor_tensor(place[:, :, :],
                                                misc(li, "rank", QC * E).rearrange("p (c e) -> p c e", c=QC),
                                                run[:, :].unsqueeze(1).to_broadcast([P, QC, E]), ALU.add)\
                            .then_inc(s_("place_done"), 1)
                        dve.wait_ge("den_done", v)
                        nc.vector.reciprocal(row[:, slot, :, 0, P + 1], dv[:, slot, 2, :]).then_inc(s_("w0_done"), 1)
                        dve.wait_ge("place_done", v)
                        nc.vector.tensor_tensor(run[:, :], misc(li, "rank", E, at=QC * E), run[:, :], ALU.add)\
                            .then_inc(s_("rank_read"), 1)
                        nc.vector.tensor_tensor(pick[:, :, :, :], oh[:, :, :, :],
                                                place[:, :, :].unsqueeze(2).to_broadcast([P, QC, 2, E]), ALU.mult)\
                            .then_inc(s_("pick_done"), 1)
                        dve.wait_ge("w0_done", v)
                        nc.vector.tensor_tensor(row[:, slot, :, 1, P + 1], row[:, slot, :, 0, P + 1],
                                                dv[:, slot, 1, :], ALU.mult).then_inc(s_("w1_done"), 1)
                        dve.wait_ge("pick_done", v)
                        nc.vector.tensor_reduce(placed[:, :, :], pick[:, :, :, :], axis=AX.X, op=ALU.add)\
                            .then_inc(s_("placed_done"), 1)
                    else:
                        dve.wait_ge("placed_done", v)
                        nc.vector.tensor_copy(index[:, slot, :, :], placed[:, :, :]).then_inc(s_("index_done"), 1)

                def shift(i):
                    if EXPS not in on_:
                        return
                    src = misc(li, "mxT", P, rows=2 * H)
                    if i == 0:
                        dve.wait_ge("mxT_ps", V[EXPS])
                        dve.wait_ge(f"m_in{sl[EXPS]}", nth(b[EXPS], sl[EXPS], li) * 32 - 32)
                        nc.vector.tensor_scalar(mparts[0:2 * H, sl[EXPS], 0, :], src, -1.0, None, ALU.mult)\
                            .then_inc(s_("m_hi"), 1)
                    else:
                        dve.wait_ge("m_hi", V[EXPS])
                        nc.vector.scalar_tensor_tensor(out=mparts[0:2 * H, sl[EXPS], 1, :], in0=src, scalar=-1.0,
                                                       in1=mparts[0:2 * H, sl[EXPS], 0, :], op0=ALU.mult,
                                                       op1=ALU.subtract).then_inc(s_("m_lo"), 1)

                def x_ready():
                    if TNS not in on_:
                        return
                    if li:
                        dve.wait_ge("on_done", B + (b[TNS] + 1) * 2)
                        more = on[:, sl[TNS], :, :]
                    else:
                        dve.wait_ge("pr_ps", V[OUT])
                        more = misc(li, "pr", T).rearrange("p (c d) -> p c d", c=QC)
                    nc.vector.tensor_tensor(x[:, tok(b[TNS]), :], x[:, tok(b[TNS]), :], more, ALU.add)\
                        .then_inc(s_("x_ready"), 1)

                def t_stats(i):
                    if TNS in on_ and i < 3:
                        v, slot = V[TNS], sl[TNS]
                        if i == 0:
                            dve.wait_ge("x_ready", v, apart=True)
                            dve_stats(lambda c: tile_of(x, b[TNS], c), TN, slot).then_inc(s_("t_stats1"), 1)
                        elif i == 1:
                            dve.wait_ge("t_stats1", v, apart=True)
                            dve_mean_var(TN, slot).then_inc(s_("t_stats"), 1)
                        else:
                            dve_eps(dve, TN, "t", v, slot)
                    if RTE in on_ and i == 3:
                        dve_bias(dve, TN, "t", V[RTE], sl[RTE])

                if li == 0:
                    maxima(0, 0)
                    shift(0)
                    t_stats(3)
                    shift(1)
                    norms(-1)
                    maxima(0, 1)
                    norms(1)
                    normed(0)
                    norms(2)
                    maxima(0, 2)
                    maxima(1, 0)
                    choose(0)
                    norms(3)
                    maxima(1, 1)
                    choose(1)
                    choose(2)
                    choose(3)
                    maxima(1, 2)
                    choose(4)
                    choose(5)
                    x_ready()
                    t_stats(0)
                    t_stats(1)
                    t_stats(2)
                    send_to(0)
                    send_to(1)
                else:
                    maxima(0, 0)
                    shift(0)
                    x_ready()
                    shift(1)
                    maxima(0, 1)
                    t_stats(0)
                    maxima(0, 2)
                    t_stats(1)
                    maxima(0, 3)
                    t_stats(2)
                    maxima(1, 0)
                    norms(-1)
                    maxima(1, 1)
                    t_stats(3)
                    maxima(1, 2)
                    maxima(1, 3)
                    if early(li, s, on_):
                        add_input(dve, nc.vector, b[0], sl[0], 0)
                    maxima(2, 0)
                    norms(0)
                    choose(0)
                    maxima(2, 1)
                    choose(1)
                    norms(1)
                    maxima(2, 2)
                    choose(2)
                    normed(0)
                    maxima(2, 3)
                    choose(3)
                    norms(2)
                    maxima(3, 0)
                    choose(4)
                    maxima(3, 1)
                    choose(5)
                    norms(3)
                    if early(li, s, on_):
                        normalise(dve, nc.vector, b[0], sl[0])
                        scale(dve, nc.vector, b[0], sl[0], 0)
                        shift_and_add(dve, nc.vector, b[0], sl[0], 0)
                    maxima(3, 2)
                    normed(1)
                    maxima(3, 3)
                    send_to(0)
                    send_to(1)
            attention_steps(dve, li, step)

        def pool_attention(pool, li):
            OUT, RTE = OUTPUT[li], ROUTE[li]

            def step(s, m, on_):
                b, sl, V = names(li, s, m)
                def send():
                    if SEND not in on_:
                        return
                    slot = sl[SEND]
                    if li == 0 and isinstance(s, int):
                        pool.wait_ge("weights_in", 16 * 6)
                    pool.wait_ge("index_done", V[SEND])
                    if not isinstance(s, int) or b[SEND]:
                        pool.wait_ge(f"scat{(slot - 1) % RING}", sent(b[SEND] - 1, (slot - 1) % RING, li))
                    pool.wait_ge(f"t_cp{slot}", nth(b[SEND], slot, li) * 32)
                    nc.gpsimd.tensor_copy(row[:, slot, :, :, P].bitcast(I32), ids[:, tok(b[SEND]), :])\
                        .then_inc(s_("id_done"), 1)
                    pool.wait_ge("id_done", V[SEND], apart=True)
                    for c in range(QC):
                        for k in range(2):
                            nc.gpsimd.indirect_dma_start(
                                out=xs, out_offset=bass.IndirectOffsetOnAxis(ap=index[:, slot, c, k:k + 1], axis=0),
                                in_=row[:, slot, c, k, :], in_offset=None).then_inc(s_(f"scat{slot}"), 16)

                which, v = both_norms(li, b, V, on_)
                slot = sl[0]
                if COMBINE in on_ and li:
                    pool_sum(pool, b[0], slot, 0)
                    if not early(li, s, on_):
                        add_input(pool, nc.gpsimd, b[0], slot, 0)
                if li:
                    if RTE in on_:
                        pool_rstd(pool, TN, "t", V[RTE], sl[RTE])
                    send()
                if which:
                    pool_rstd(pool, which, "n", v, slot)
                if COMBINE in on_ and li and not early(li, s, on_):
                    normalise(pool, nc.gpsimd, b[0], slot)
                    scale(pool, nc.gpsimd, b[0], slot, 0)
                    shift_and_add(pool, nc.gpsimd, b[0], slot, 0)
                if not li:
                    if OUT in on_:
                        pool_rstd(pool, TN, "t", V[OUT], sl[OUT])
                    send()
            attention_steps(pool, li, step)

        chained = [0]

        def link(dve, ins):
            chained[0] += 1
            ins.then_inc(s_("chain"), 1)
            dve.wait_ge("chain", chained[0])

        def dve_tiles(dve, li):
            dve.wait_ge("rank_read", B * (li + 1))
            if li:
                for k in range(SLOTS):
                    dve.wait_ge(f"w_in{k}", 16 * (NJ // SLOTS))
            nc.vector.tensor_copy(pad_row[:, :], run[:, :])
            link(dve, nc.vector.tensor_tensor(ct[:, :], run[:, :], first_row, ALU.subtract))
            link(dve, nc.vector.tensor_scalar(ct_i[:, :], ct[:, :], float(TILE - 1), None, ALU.add))
            link(dve, nc.vector.tensor_scalar(ct_s[:, :], ct_i[:, :], TILE.bit_length() - 1, None,
                                              ALU.logical_shift_right))
            link(dve, nc.vector.tensor_copy(tiles[:, :], ct_s[:, :]))
            nc.vector.tensor_scalar(skip[:, :], tiles[:, :], -float(TILE), float(REGION), ALU.mult, ALU.add)
            u, d, k = tiles, 1, 0
            while d < E:
                dst = upto[k % 2]
                nc.vector.tensor_copy(dst[:, 0:d], u[:, 0:d])
                link(dve, nc.vector.tensor_tensor(dst[:, d:E], u[:, d:E], u[:, 0:E - d], ALU.add))
                u, d, k = dst, 2 * d, k + 1
            link(dve, nc.vector.tensor_tensor(past[:, :, :], iotaj.unsqueeze(2).to_broadcast([P, NJ, E]),
                                              u[:, :].unsqueeze(1).to_broadcast([P, NJ, E]), ALU.is_ge))
            nc.vector.tensor_reduce(t_exp[:, :], past[:, :, :], axis=AX.X, op=ALU.add)
            link(dve, nc.vector.tensor_tensor(skipped[:, :, :], past[:, :, :],
                                              skip[:, :].unsqueeze(1).to_broadcast([P, NJ, E]), ALU.mult))
            link(dve, nc.vector.tensor_reduce(t_row[:, :], skipped[:, :, :], axis=AX.X, op=ALU.add))
            nc.vector.tensor_scalar(t_exp_i[:, :], t_exp[:, :], float(E - 1), None, ALU.min)
            nc.vector.scalar_tensor_tensor(out=t_row_i[:, :], in0=iotaj, scalar=float(TILE), in1=t_row[:, :],
                                           op0=ALU.mult, op1=ALU.add).then_inc(s_("tiles_known"), 1)
            link(dve, nc.vector.tensor_copy(run[:, :], first_row))

        def tile_loop(eng, body):
            first = SLOTS + 1
            turns = (NJ - first - 1) // SLOTS
            for j in range(first):
                body(j, j % SLOTS)
            with eng.engine.Fori(0, turns) as i:
                for k in range(first, first + SLOTS):
                    body(At(i, SLOTS, k), k % SLOTS)
            for j in range(first + turns * SLOTS, NJ):
                body(j, j % SLOTS)

        def turn(li, j, k):
            return (j - k) // SLOTS + 1 + NJ // SLOTS * li

        def before(j, n):
            return isinstance(j, int) and j < n

        def pad(ops, experts):
            for e in experts:
                at = ops.value_load(pad_row[0:1, e:e + 1], min_val=0, max_val=E * REGION - TILE)
                ops.dma_start(xs[bass.ds(at, TILE), :], pads[e * TILE:(e + 1) * TILE, :])\
                    .then_inc(s_("pads_in"), 16)

        def sp_experts(sp, li):
            sp.wait_ge("tiles_known", li + 1)
            pad(nc.sync, range(E // 2, E))
            sp.wait_ge("pads_in", 16 * E * (li + 1))
            sp.wait_ge("spare_in", 16)
            for k in range(RING):
                sp.wait_ge(f"scat{k}", sent(B - 1 - (B - 1 - k) % RING, k, li))

            def body(j, k):
                n = nc.sync.snap(val(j)) if isinstance(j, At) else j
                sp.wait_ge("idw_done", NJ * li + j + 1 - SLOTS, apart=True)
                sp.wait_ge("xT_ps", NJ * li + j + 1 - SLOTS, apart=True)
                at = nc.sync.value_load(t_row_i[0:1, bass.ds(n, 1)], min_val=0,
                                        max_val=E * REGION + (SPARE - 1) * TILE)
                nc.sync.dma_start(xt[:, k, :, :], xs[bass.ds(at, TILE), :].rearrange("(c p) d -> p c d", p=P))\
                    .then_inc(s_(f"xt_in{k}"), 16)
                e = nc.sync.value_load(t_exp_i[0:1, bass.ds(n, 1)], min_val=0, max_val=E - 1)
                sp.wait_ge("ysum_sb", NJ * li + j + 1 - SLOTS, apart=True)
                nc.sync.dma_start(wsl[:, k, :], wall[bass.ds(e, 1), :, :].rearrange("a p c -> p (a c)"))\
                    .then_inc(s_(f"w_in{k}"), 16)
            tile_loop(sp, body)

        def pe_experts(pe, li):
            n0 = NJ * li
            pe.wait_ge("rank_read", B * (li + 1))
            pe.wait_ge("o_sb", 2 * B * (li + 1))

            def rows_in(j, k):
                pe.wait_ge(f"xt_in{k}", turn(li, j, k) * 16)
                pe.wait_ge("xT_sb", n0 + j)
                for c in range(QC):
                    tr = nc.tensor.transpose(pXT[:, c * P:(c + 1) * P], xt[:, k, c, 0:P], ident)
                tr.then_inc(s_("xT_ps"), 1)

            def body(j, k):
                pe.wait_ge("xT_sb", n0 + j + 1)
                pe.wait_ge(f"w_in{k}", turn(li, j, k) * 16)
                pe.wait_ge("h_act", (n0 + j) * 2)
                pe.wait_ge("h_dve", (n0 + j) * 2)
                for f in range(FC):
                    nc.tensor.matmul(pH[f][:, 0:TILE], wsl[:, k, f * P:(f + 1) * P], xT[:, k, :],
                                     start=True, stop=True).then_inc(s_("h_ps"), 1)
                if not isinstance(j, int) or j + 1 < NJ:
                    rows_in(j + 1, (k + 1) % SLOTS)
                pe.wait_ge("ysum_sb", n0 + j)
                for f in range(FC):
                    pe.wait_ge("h_dve" if f % 2 else "h_act", (n0 + j) * 2 + f // 2 + 1)
                    for c in range(QC):
                        mm = nc.tensor.matmul(pY[:, c * P:(c + 1) * P], hT[:, f, c * P:(c + 1) * P],
                                              wsl[:, k, F + f * P:F + (f + 1) * P],
                                              start=(f == 0 and c == 0), stop=(f == FC - 1), skip_group_check=True)
                mm.then_inc(s_("y_ps"), 1)
            rows_in(0, 0)
            tile_loop(pe, body)

        def bias1(k, f):
            return wsl[:, k, F + FC * P + f:F + FC * P + f + 1]

        def act_experts(act, li):
            n0 = NJ * li
            act.wait_ge("tiles_known", li + 1)
            pad(nc.scalar, range(E // 2))

            def body(j, k):
                for f in (0, 2):
                    act.wait_ge("h_ps", (n0 + j) * FC + f + 1)
                    act.wait_ge("y_ps", n0 + j)
                    nc.scalar.activation(hT[:, f, :], pH[f][:, 0:TILE], ACT.Relu, bias=bias1(k, f))\
                        .then_inc(s_("h_act"), 1)
                    if f == 0 and not before(j, 1):
                        weighed(j - 1, (k - 1) % SLOTS)

            def weighed(j, k):
                act.wait_ge("ysum_sb", n0 + j + 1)
                for c in range(QC):
                    ins = nc.scalar.activation(yt[:, k, c, :], ysum[:, k, c, :], ACT.Identity,
                                               scale=idw[:, k, c, 1:2])
                ins.then_inc(s_("yt_sb"), 1)
            tile_loop(act, body)
            weighed(NJ - 1, (NJ - 1) % SLOTS)

        def dve_experts(dve, li):
            n0 = NJ * li

            def columns(j, k):
                dve.wait_ge("xT_ps", n0 + j + 1)
                nc.vector.tensor_copy(xT[:, k, :], pXT[:, 0:TILE]).then_inc(s_("xT_sb"), 1)

            def results(j, k):
                dve.wait_ge(f"y_out{k}", turn(li, j, k) * 32 - 32)
                nc.vector.tensor_copy(idw[:, k, :, :].bitcast(I32), xt[:, k, :, P:P + 2].bitcast(I32))\
                    .then_inc(s_("idw_done"), 1)
                dve.wait_ge("y_ps", n0 + j + 1)
                nc.vector.tensor_tensor(ysum[:, k, :, :], pY[:, 0:TILE].rearrange("p (c d) -> p c d", c=QC),
                                        wsl[:, k, WCOLS - P:WCOLS].unsqueeze(1).to_broadcast([P, QC, P]), ALU.add)\
                    .then_inc(s_("ysum_sb"), 1)

            def body(j, k):
                if not before(j, 1):
                    results(j - 1, (k - 1) % SLOTS)
                for f in (1, 3):
                    dve.wait_ge("h_ps", (n0 + j) * FC + f + 1)
                    dve.wait_ge("y_ps", n0 + j)
                    nc.vector.tensor_scalar(hT[:, f, :], pH[f][:, 0:TILE], bias1(k, f), 0.0, ALU.add, ALU.max)\
                        .then_inc(s_("h_dve"), 1)
                if not isinstance(j, int) or j + 1 < NJ:
                    columns(j + 1, (k + 1) % SLOTS)
            columns(0, 0)
            tile_loop(dve, body)
            results(NJ - 1, (NJ - 1) % SLOTS)

        def pool_experts(pool, li):
            if not li:
                pool.wait_ge("av_done", B * LAYERS[0]["groups"])
                pool_fill(pool, LAYERS[1])

            def body(j, k):
                pool.wait_ge("yt_sb", NJ * li + j + 1, apart=True)
                for c in range(QC):
                    nc.gpsimd.indirect_dma_start(
                        out=ys, out_offset=bass.IndirectOffsetOnAxis(ap=idw[:, k, c, 0:1].bitcast(U32), axis=0),
                        in_=yt[:, k, c, :], in_offset=None).then_inc(s_(f"y_out{k}"), 16)
            tile_loop(pool, body)

        def pool_fill(pool, L):
            pair_of_ones = float(np.array([0x3F803F80], np.uint32).view(np.float32)[0])
            n = 2 * LAYERS.index(L)
            nc.gpsimd.memset(kst[L["ones"]:L["ones"] + 32, :, :, :].bitcast(F32), pair_of_ones)\
                .then_inc(s_("filled"), 1)
            pool.wait_ge("filled", n + 1)
            nc.gpsimd.memset(vaug[:, :, :, :, :], 0.0).then_inc(s_("filled"), 1)
            pool.wait_ge("filled", n + 2)
            nc.gpsimd.memset(vaug[:, :, :, :, L["hd"]:L["hd"] + 1], 1.0).then_inc(s_("ones_set"), 1)

        @block.sync
        def _(sp):
            sp = Waiting(sp, s_)
            nc.sync.dma_start(cst[:, :, :], consts.rearrange("s p c -> p s c")).then_inc(s_("consts_in"), 16)
            nc.sync.dma_start(cnt[:, 0:2 * E + NJ], counts).then_inc(s_("consts_in"), 16)
            nc.sync.dma_start(hs[:, :], hs_in).then_inc(s_("consts_in"), 16)
            nc.sync.dma_start(wqt[:, :], wq_t).then_inc(s_("consts_in"), 16)
            for lo, hi in ((0, FIRST), (FIRST, B)):
                nc.sync.dma_start(x[:, lo * QC:hi * QC, :],
                                  x_in[lo:hi].rearrange("b (c p) d -> p (b c) d", p=P)).then_inc(s_("x_in"), 16)
                if lo == 0:
                    nc.sync.dma_start(wqkv[0][:, 1:3, :], w_a.rearrange("p (a c) -> p a c", a=2))\
                        .then_inc(s_("proj_in"), 16)
                    nc.sync.dma_start(wqkv[1][:, :, :], w_b.rearrange("p (a c) -> p a c", a=3))\
                        .then_inc(s_("proj_in"), 16)
            nc.sync.dma_start(wo[:, :], w_o).then_inc(s_("weights_in"), 16)
            nc.sync.dma_start(wrs[:, :], wr).then_inc(s_("weights_in"), 16)
            nc.sync.dma_start(brs[:, :, :], br.unsqueeze(1).to_broadcast([P, QC, E])).then_inc(s_("weights_in"), 16)
            nc.sync.dma_start(gam[:, :, :], gamma.unsqueeze(1).to_broadcast([P, QC, P])).then_inc(s_("weights_in"), 16)
            nc.sync.dma_start(bet[:, :, :], beta.unsqueeze(1).to_broadcast([P, QC, P])).then_inc(s_("weights_in"), 16)
            nc.sync.dma_start(ids[:, :, :], id_in.rearrange("p (n k) -> p n k", k=2)).then_inc(s_("weights_in"), 16)
            nc.sync.dma_start(xs[E * REGION:E * REGION + SPARE * TILE, :], pads[E * TILE:(E + SPARE) * TILE, :])\
                .then_inc(s_("spare_in"), 16)
            for li in range(2):
                sp_attention(sp, li)
                sp_experts(sp, li)
                for k in range(SLOTS):
                    sp.wait_ge(f"y_out{k}", 32 * (NJ // SLOTS) * (li + 1))

            def step(s, m, on_):
                if 0 in on_:
                    sp_results(sp, s, m % RING, 1)
            steps(sp, 3, step)
            sp.wait_ge("out_w", 16 * B)

        @block.vector
        def _(dve):
            dve = Waiting(dve, s_)
            nc.vector.memset(onesb[:, :], 1.0)
            nc.vector.memset(halfm[:, :, :], -0.5)
            for mk in (maskm_w, maske_w):
                nc.vector.memset(mk[:, :, :, :], 0.0).then_inc(s_("bf_made"), 1)
            dve.wait_ge("bf_made", 2)
            dve.wait_ge("consts_in", 64)
            link(dve, nc.vector.tensor_scalar(geo[:, :], cst[:, 4, :], hs[:, 0:1], None, ALU.mult))
            link(dve, nc.vector.scalar_tensor_tensor(out=geo[:, :], in0=cst[:, 0, :],
                                                     scalar=float(LAYERS[0]["hd"]) ** -0.5, in1=geo[:, :],
                                                     op0=ALU.mult, op1=ALU.add))
            nc.vector.tensor_copy(identb[:, :], cst[:, 0, :])
            nc.vector.tensor_scalar(minusb[:, :], cst[:, 0, :], -1.0, None, ALU.mult)
            nc.vector.tensor_copy(earlier[:, :], cst[:, 3, :])
            nc.vector.tensor_copy(run[:, :], first_row)
            for a in range(2):
                nc.vector.tensor_copy(maskm_w[:, a, 1, :], cst[:, 1, :])
                nc.vector.tensor_copy(maske_w[:, a, 0, :], cst[:, 2, :])
            for a in range(4):
                nc.vector.tensor_copy(maskm_n[:, a, :], cst[:, 1, :])
                ins = nc.vector.tensor_copy(maske_n[:, a, :], cst[:, 2, :])
            ins.then_inc(s_("consts_made"), 1)
            dve.wait_ge("proj_in", 16 * 2)
            dve.wait_ge("wq_ps", 1)
            nc.vector.tensor_copy(wqkv[0][:, 0, :], pX[0][:, 0:P])
            nc.vector.tensor_scalar(wqkv[1][:, 0, :], wqkv[1][:, 0, :], float(LAYERS[1]["hd"]) ** -0.5, None,
                                    ALU.mult).then_inc(s_("wq_made"), 1)
            for li in range(2):
                dve_attention(dve, li)
                dve_tiles(dve, li)
                dve_experts(dve, li)

            def step(s, m, on_):
                if 0 in on_:
                    slot, v = m % RING, s + 1
                    add_input(dve, nc.vector, s, slot, 1)
                    dve.wait_ge("c_add", v + B, apart=True)
                    dve_stats(lambda c: r[:, slot, c, :], CN, slot).then_inc(s_("c_stats1"), 1)
                if 1 in on_:
                    dve_bias(dve, CN, "c", s, (m - 1) % RING)
                if 0 in on_:
                    dve.wait_ge("c_stats1", v, apart=True)
                    dve_mean_var(CN, slot).then_inc(s_("c_stats"), 1)
                    dve_eps(dve, CN, "c", v, slot)
                if 2 in on_:
                    shift_and_add(dve, nc.vector, s - 2, (m - 2) % RING, 1)
            steps(dve, 3, step)

        @block.tensor
        def _(pe):
            pe = Waiting(pe, s_)
            pe.wait_ge("consts_made", 1)
            nc.tensor.matmul(pX[0][:, 0:P], wqt[:, :], geo[:, :], start=True, stop=True).then_inc(s_("wq_ps"), 1)
            pe.wait_ge("wq_made", 1)
            for li in range(2):
                if li:
                    pe.wait_ge("ysum_sb", NJ)
                    pe.wait_ge("ones_set", 2)
                else:
                    pe.wait_ge("ones_set", 1)
                pe_attention(pe, li)
                pe_experts(pe, li)

        @block.scalar
        def _(act):
            act = Waiting(act, s_)
            act.wait_ge("ones_set", 1)
            for li in range(2):
                if li:
                    act.wait_ge("ones_set", 2)
                act_attention(act, li)
                act_experts(act, li)

            def step(s, m, on_):
                if 1 in on_:
                    slot = (m - 1) % RING
                    act_normalise(act, lambda c: r[:, slot, c, :], lambda c: r[:, slot, c, :], CN, "c",
                                  s, slot).then_inc(s_("c_norm"), 1)
                if 2 in on_:
                    b = s - 2
                    act.wait_ge("c_x", b + B + 1, apart=True)
                    nc.scalar.dma_start(out[ds(b, 1), :, :].rearrange("a (c p) d -> p (a c) d", p=P),
                                        x[:, tok(b), :]).then_inc(s_("out_w"), 16)
            steps(act, 3, step)

        @block.gpsimd
        def _(pool):
            pool = Waiting(pool, s_)
            pool_fill(pool, LAYERS[0])
            pool.wait_ge("consts_made", 1)
            for li in range(2):
                pool_attention(pool, li)
                pool_experts(pool, li)

            def step(s, m, on_):
                if 0 in on_:
                    pool_sum(pool, s, m % RING, 1)
                if 1 in on_:
                    pool_rstd(pool, CN, "c", s, (m - 1) % RING)
                if 2 in on_:
                    scale(pool, nc.gpsimd, s - 2, (m - 2) % RING, 1)
            steps(pool, 3, step)


def kernel(**inputs):
    import numpy as _np
    import concourse.bacc as _bacc
    from concourse import mybir as _mybir
    from concourse.bass_utils import run_bass_kernel_spmd as _run

    a = {k: _np.ascontiguousarray(v) for k, v in inputs.items()}
    D = P

    def by_row(w, H):
        return w.reshape(D, H, D // H).transpose(0, 2, 1).reshape(D, D)

    HA, HB = LAYERS[0]["H"], LAYERS[1]["H"]
    wqkv = a["L0_attn_a_w_qkv"]
    dirs = _np.array([[(i >> 2 & 1) * 2 - 1, (i >> 1 & 1) * 2 - 1, (i & 1) * 2 - 1] for i in range(HA)],
                     dtype=_np.float32) / _np.sqrt(3.0, dtype=_np.float32)
    consts = _np.zeros((5, P, P), _np.float32)
    i = _np.arange(P)
    consts[0] = _np.eye(P, dtype=_np.float32)
    consts[1] = _np.where(i[None, :] > i[:, None], MASKED, 0.0)
    consts[2] = _np.where(i[None, :] < i[:, None], MASKED, 0.0)
    consts[3] = _np.where(i[:, None] < i[None, :], 1.0, 0.0)
    for h in range(HA):
        for r1 in range(3):
            for r2 in range(3):
                consts[4][r1 * HA + h, r2 * HA + h] = dirs[h, r1] * dirs[h, r2]
    counts = _np.zeros((P, 2 * E + NJ), _np.float32)
    counts[:, 0:E] = _np.arange(E)
    counts[:, E:2 * E] = _np.arange(E) * REGION
    counts[:, 2 * E:] = _np.arange(NJ)
    token = _np.arange(NT)[None, :, None] * P + i[:, None, None]
    ids = (token + _np.arange(2)[None, None, :] * B * T).astype(_np.int32).reshape(P, NT * 2)
    pads = _np.zeros(((E + SPARE) * TILE, ROW), _np.float32)
    pads.view(_np.int32)[:, P] = PAIRS + _np.arange((E + SPARE) * TILE)
    w1 = a["L0_ffn_W1"].transpose(0, 2, 1)
    w2 = a["L0_ffn_W2"].transpose(0, 2, 1).reshape(E, FC, P, D).transpose(0, 2, 1, 3).reshape(E, P, FC * D)
    b1 = a["L0_ffn_b1"].reshape(E, FC, P).transpose(0, 2, 1)
    b2 = _np.broadcast_to(a["L0_ffn_b2"][:, None, :], (E, P, D))
    arrays = {
        "x_in": a["L0_attn_a_x"],
        "w_a": _np.concatenate([by_row(wqkv[:, D:2 * D], HA), wqkv[:, 2 * D:]], axis=1),
        "w_o": a["L0_attn_a_w_out"],
        "wq_t": by_row(wqkv[:, 0:D], HA).T,
        "w_b": _np.concatenate([by_row(a["L0_attn_b_Wq"].T, HB), by_row(a["L0_attn_b_Wk"].T, HB),
                                a["L0_attn_b_Wv"].T], axis=1),
        "hs_in": _np.tile(a["L0_attn_a_head_scales"], D // HA).reshape(D, 1),
        "wr": a["L0_ffn_Wr"].T,
        "br": _np.broadcast_to(a["L0_ffn_br"], (P, E)),
        "wall": _np.concatenate([w1, w2, b1, b2], axis=2),
        "gamma": _np.broadcast_to(a["L0_ffn_gamma"], (P, D)),
        "beta": _np.broadcast_to(a["L0_ffn_beta"], (P, D)),
        "consts": consts, "counts": counts, "id_in": ids, "pads": pads,
    }
    nc = _bacc.Bacc("TRN2", target_bir_lowering=False, num_devices=1)
    aps, given = {}, {}
    for name, array in arrays.items():
        array = _np.ascontiguousarray(array)
        given["in_" + name] = array
        aps[name] = nc.dram_tensor("in_" + name, array.shape, _mybir.dt.from_np(array.dtype),
                                   kind="ExternalInput").ap()
    out = nc.dram_tensor("out_x", (B, T, D), F32, kind="ExternalOutput").ap()
    build(nc, out=out, **aps)
    res = _run(nc, [given], core_ids=[0])
    return res.results[0]["out_x"]
```
